# Optimizing a Trainium2 kernel written in Bass

```python
import numpy as np
import jax
import jax.numpy as jnp

def _softmax(x, axis=-1):
    return jax.nn.softmax(x, axis=axis)

def _gelu(x):
    return jax.nn.gelu(x, approximate=True)

def _silu(x):
    return jax.nn.silu(x)

def _sigmoid(x):
    return jax.nn.sigmoid(x)

def _layernorm(x, axis=-1, eps=1e-05):
    m = jnp.mean(x, axis=axis, keepdims=True)
    v = jnp.var(x, axis=axis, keepdims=True)
    return (x - m) / jnp.sqrt(v + eps)

def _scatter_add(tgt, idx, src, axis=0):
    return tgt.at[idx].add(src)

def _segment_sum(src, seg, n):
    return jax.ops.segment_sum(src, seg, n)
kernel_name = 'mk_lm_tower_d1_tok_ids768_r4_950622'

def setup_inputs(seed: int=0):
    np.random.seed(seed)
    _w = jnp.asarray

    def _rec_inputs():
        import jax
        import jax.numpy as jnp
        _rk = jax.random.key(seed)
        x = jax.random.randint(jax.random.fold_in(_rk, 1), (8, 512), 0, 127999, jnp.int32)
        return x
    x = _rec_inputs()

    def _L0_tok_setup():
        import jax, jax.numpy as jnp
        import numpy as np
        import math
        VOCAB = 32000
        BASIN_DIM = 64
        D_MODEL = 192
        EPS = 1e-08
        key = jax.random.key(seed)
        k1, k2, k3, k4 = jax.random.split(key, 4)
        token_ids = jax.random.randint(k1, (8, 1024), 0, VOCAB, dtype=jnp.int32)
        coords = jax.random.normal(k2, (VOCAB, BASIN_DIM), dtype=jnp.float32)
        coords = coords / jnp.linalg.norm(coords, axis=-1, keepdims=True)
        coords = coords * (math.sqrt(BASIN_DIM) / 5.0)
        coords = coords + jax.random.normal(k3, coords.shape, dtype=jnp.float32) * 0.01
        w = jax.random.normal(k4, (D_MODEL, BASIN_DIM), dtype=jnp.float32)
        q, _ = jnp.linalg.qr(w)
        proj_w = q * 0.1
        norm_w = jnp.ones((D_MODEL,), dtype=jnp.float32)
        return {'token_ids': token_ids, 'basin_coords': coords, 'proj_w': proj_w, 'norm_w': norm_w}
    _L0_tok_all = _L0_tok_setup()
    _L0_tok_in = {k: v for k, v in _L0_tok_all.items() if k in ('basin_coords', 'proj_w', 'norm_w')}
    del _L0_tok_all

    def _L0_attn_setup():
        import math
        import jax, jax.numpy as jnp
        import numpy as np
        NUM_HEADS = 12
        EPS = 0.0001

        def softmax_kernel_features(data, proj, is_query):
            d = data.shape[-1]
            data_normalizer = 1.0 / math.sqrt(math.sqrt(d))
            ratio = 1.0 / math.sqrt(proj.shape[0])
            data_dash = jnp.einsum('bhnd,md->bhnm', data_normalizer * data, proj)
            diag_data = jnp.sum(jnp.square(data), axis=-1, keepdims=True) * 0.5 * data_normalizer * data_normalizer
            if is_query:
                stab = jnp.max(data_dash, axis=-1, keepdims=True)
            else:
                stab = jnp.max(data_dash)
            return ratio * (jnp.exp(data_dash - diag_data - stab) + EPS)
        key = jax.random.key(seed)
        k0, k1, k2, k3, k4 = jax.random.split(key, 5)
        B, N, C, H = (8, 1024, 192, NUM_HEADS)
        hd = C // H
        m = int(hd * math.log(hd))
        x = jax.random.normal(k0, (B, N, C), dtype=jnp.float32)
        W_qkv = jax.random.normal(k1, (C, 3 * C), dtype=jnp.float32) / math.sqrt(C)
        W_proj = jax.random.normal(k2, (C, C), dtype=jnp.float32) / math.sqrt(C)
        b_proj = jnp.zeros((C,), dtype=jnp.float32)
        proj_mat = jax.random.normal(k3, (m, hd), dtype=jnp.float32)
        return {'x': x, 'W_qkv': W_qkv, 'W_proj': W_proj, 'b_proj': b_proj, 'proj_mat': proj_mat}
    _L0_attn_all = _L0_attn_setup()
    _L0_attn_in = {k: v for k, v in _L0_attn_all.items() if k in ('W_qkv', 'W_proj', 'b_proj', 'proj_mat')}
    del _L0_attn_all

    def _L0_ffn_setup():
        import jax, jax.numpy as jnp
        import numpy as np
        D_MODEL = 192
        D_FF = 768
        NUM_EXPERTS = 8
        EXPERT_CAPACITY = 256
        key = jax.random.key(seed)
        k0, k1, k2, k3 = jax.random.split(key, 4)
        hidden_states = jax.random.normal(k0, (2, 256, D_MODEL), dtype=jnp.float32)
        router_w = jax.random.normal(k1, (D_MODEL, NUM_EXPERTS), dtype=jnp.float32) * D_MODEL ** (-0.5)
        wi = jax.random.normal(k2, (NUM_EXPERTS, D_MODEL, D_FF), dtype=jnp.float32) * D_MODEL ** (-0.5)
        wo = jax.random.normal(k3, (NUM_EXPERTS, D_FF, D_MODEL), dtype=jnp.float32) * D_FF ** (-0.5)
        return {'hidden_states': hidden_states, 'router_w': router_w, 'wi': wi, 'wo': wo}
    _L0_ffn_all = _L0_ffn_setup()
    _L0_ffn_in = {k: v for k, v in _L0_ffn_all.items() if k in ('router_w', 'wi', 'wo')}
    del _L0_ffn_all
    return {'x': x, 'L0_tok_basin_coords': _L0_tok_in['basin_coords'], 'L0_tok_proj_w': _L0_tok_in['proj_w'], 'L0_tok_norm_w': _L0_tok_in['norm_w'], 'L0_attn_W_qkv': _L0_attn_in['W_qkv'], 'L0_attn_W_proj': _L0_attn_in['W_proj'], 'L0_attn_b_proj': _L0_attn_in['b_proj'], 'L0_attn_proj_mat': _L0_attn_in['proj_mat'], 'L0_ffn_router_w': _L0_ffn_in['router_w'], 'L0_ffn_wi': _L0_ffn_in['wi'], 'L0_ffn_wo': _L0_ffn_in['wo']}

def reference(x, L0_tok_basin_coords, L0_tok_proj_w, L0_tok_norm_w, L0_attn_W_qkv, L0_attn_W_proj, L0_attn_b_proj, L0_attn_proj_mat, L0_ffn_router_w, L0_ffn_wi, L0_ffn_wo):
    import jax
    import jax.numpy as jnp

    def _L0_tok_ref(token_ids, basin_coords, proj_w, norm_w):
        import jax, jax.numpy as jnp
        import numpy as np
        import math
        VOCAB = 32000
        BASIN_DIM = 64
        D_MODEL = 192
        EPS = 1e-08
        basin = basin_coords[token_ids]
        emb = jnp.einsum('bsk,dk->bsd', basin, proj_w)
        x_f = emb.astype(jnp.float32)
        rms = jnp.sqrt(jnp.mean(x_f * x_f, axis=-1, keepdims=True) + EPS)
        y = (x_f / rms).astype(emb.dtype)
        return y * norm_w

    def _L0_attn_ref(x, W_qkv, W_proj, b_proj, proj_mat):
        import math
        import jax, jax.numpy as jnp
        import numpy as np
        NUM_HEADS = 12
        EPS = 0.0001

        def softmax_kernel_features(data, proj, is_query):
            d = data.shape[-1]
            data_normalizer = 1.0 / math.sqrt(math.sqrt(d))
            ratio = 1.0 / math.sqrt(proj.shape[0])
            data_dash = jnp.einsum('bhnd,md->bhnm', data_normalizer * data, proj)
            diag_data = jnp.sum(jnp.square(data), axis=-1, keepdims=True) * 0.5 * data_normalizer * data_normalizer
            if is_query:
                stab = jnp.max(data_dash, axis=-1, keepdims=True)
            else:
                stab = jnp.max(data_dash)
            return ratio * (jnp.exp(data_dash - diag_data - stab) + EPS)
        B, N, C = x.shape
        H = NUM_HEADS
        hd = C // H
        qkv = (x @ W_qkv).reshape(B, N, 3, H, hd)
        qkv = jnp.transpose(qkv, (2, 0, 3, 1, 4))
        q, k, v = (qkv[0], qkv[1], qkv[2])
        q1 = softmax_kernel_features(q, proj_mat, is_query=True)
        k1 = softmax_kernel_features(k, proj_mat, is_query=False)
        kv = jnp.einsum('bhnm,bhnd->bhmd', k1, v)
        ksum = jnp.sum(k1, axis=2)
        z = 1.0 / jnp.einsum('bhnm,bhm->bhn', q1, ksum)
        out = jnp.einsum('bhnm,bhmd->bhnd', q1, kv) * z[..., None]
        out = jnp.transpose(out, (0, 2, 1, 3)).reshape(B, N, C)
        return out @ W_proj + b_proj

    def _L0_ffn_ref(hidden_states, router_w, wi, wo):
        import jax, jax.numpy as jnp
        import numpy as np
        D_MODEL = 192
        D_FF = 768
        NUM_EXPERTS = 8
        EXPERT_CAPACITY = 256
        B, S, d = hidden_states.shape
        E = router_w.shape[1]
        x = hidden_states.reshape(-1, d)
        logits = x.astype(jnp.float32) @ router_w.astype(jnp.float32)
        probs = jax.nn.softmax(logits, axis=-1).astype(x.dtype)
        p = jnp.max(probs, axis=-1)
        e_idx = jnp.argmax(probs, axis=-1)
        mask = jax.nn.one_hot(e_idx, E, dtype=x.dtype)
        token_priority = jnp.cumsum(mask[:, None, :], axis=-2)[:, 0, :]
        mask = mask * (token_priority <= EXPERT_CAPACITY).astype(x.dtype)
        combine = mask * p[:, None]

        def body(acc, ew):
            Wi_e, Wo_e, w_e = ew
            h = jax.nn.relu(x @ Wi_e) @ Wo_e
            return (acc + w_e[:, None] * h, None)
        out, _ = jax.lax.scan(body, jnp.zeros_like(x), (wi, wo, combine.T))
        return out.reshape(B, S, d)
    h = _L0_tok_ref(x, L0_tok_basin_coords, L0_tok_proj_w, L0_tok_norm_w)
    h = h + _L0_attn_ref(_layernorm(h, axis=-1), L0_attn_W_qkv, L0_attn_W_proj, L0_attn_b_proj, L0_attn_proj_mat)
    h = h + _L0_ffn_ref(_layernorm(h, axis=-1), L0_ffn_router_w, L0_ffn_wi, L0_ffn_wo)
    return h

_drawn_inputs = setup_inputs


def setup_inputs(seed=0):
    import zlib

    import numpy as np

    out = dict(_drawn_inputs(seed))
    spreads = {'L0_tok_norm_w': (1.0, 0.2), 'L0_attn_b_proj': (0.0, 0.1)}
    factors = {}
    for name, (base, spread) in spreads.items():
        noise = np.random.default_rng([zlib.crc32(name.encode()), seed]).standard_normal(out[name].shape)
        drawn = base * np.exp(spread * noise) if base else spread * noise
        out[name] = jnp.asarray(drawn.astype(out[name].dtype))
    for name, factor in factors.items():
        out[name] = (out[name] * factor).astype(out[name].dtype)
    return out
```

```python
from contextlib import ExitStack

import numpy as np

import concourse.bass as bass
from concourse import mybir

F32, F32R = mybir.dt.float32, mybir.dt.float32r
I32, U32 = mybir.dt.int32, mybir.dt.uint32
ALU = mybir.AluOpType
ACT = mybir.ActivationFunctionType
AX = mybir.AxisListType

P = 128
NB, SEQ = 8, 512
TPB = SEQ // P
VOCAB, DB, D = 32000, 64, 192
H, HD, M = 12, 16, 44
NF = H * M
CH = 5
F0 = [0, 128, 256, 384, NF - P]
HW = 6
W0 = [0, 0, 4, 6, 6]
VC = HD + 1
NE, DF = 8, 768
TOK = NB * SEQ
SEG = TOK + P
NT = (TOK + NE * (P - 1)) // P
SPARE = NT - TOK // P
CNTS = TOK // P
KC = D // 2
EXT = D + NE
ROW = EXT + 4
R_MEAN, R_STD, R_GATE, R_ROW = EXT, EXT + 1, EXT + 2, EXT + 3
EPS_RMS, EPS_LN, EPS_FEAT = 1e-8, 1e-5, 1e-4
NORM = HD ** -0.25
FAR = float(1 << 20)
C_ID, C_TRI, C_IND = 0, P, 2 * P
C_MASK = C_IND + CH * P
C_HM = C_MASK + CH * HW
C_E8 = C_HM + HW
C_ROW = C_E8 + NE
C_PAD = C_ROW + NB * TPB
C_THR = C_PAD + NE
C_LE = C_THR + CNTS
C_T = C_LE + NE * NE
C_N = C_T + NT


def constants():
    c = np.zeros((P, C_N), np.float32)
    c[:, C_ID:C_ID + P] = np.eye(P)
    c[:, C_TRI:C_TRI + P] = np.triu(np.ones((P, P)), 1)
    for i in range(CH):
        for f in range(P):
            feat = F0[i] + f
            for part in range(2):
                c[part * H + feat // M, C_IND + i * P + f] = -1.0
            if i < CH - 1 or feat >= F0[3] + P:
                if 0 <= feat // M - W0[i] < HW:
                    c[f, C_MASK + i * HW + feat // M - W0[i]] = 1.0
    for p in range(KC):
        c[p, C_HM + p // HD] = 1.0
    c[:, C_E8:C_E8 + NE] = NE - np.arange(NE)
    p, b, j = np.meshgrid(np.arange(P), np.arange(NB), np.arange(TPB), indexing="ij")
    c[:, C_PAD:C_THR] = np.arange(NE) * SEG + np.arange(P)[:, None]
    c[:, C_THR:C_LE] = np.arange(CNTS) * P
    c[:, C_LE:C_T] = np.tril(np.ones((NE, NE))).reshape(-1)
    c[:, C_T:C_N] = np.arange(NT)
    c[:, C_ROW:C_PAD] = (b * SEQ + p * TPB + j).reshape(P, -1)
    return c


def bc(ap, axis, n):
    a = ap.unsqueeze(axis)
    shape = list(a.shape)
    shape[axis] = n
    return a.to_broadcast(shape)


def lm_tower(nc, ids, coords, proj_w, norm_w, w_qkv, w_proj, b_proj, proj_mat, router_w, wi, wo, consts, out):
    with ExitStack() as ctx:
        def sb(name, shape, dt=F32):
            return ctx.enter_context(nc.sbuf_tensor(name, shape, dt))

        def sem(name):
            return ctx.enter_context(nc.semaphore(name))

        slots = nc.dram_tensor("slots", [NE * SEG + SPARE * P, ROW], F32).ap()
        out_rows = out.rearrange("b n d -> (b n) d")

        psum = ctx.enter_context(nc.psum_tensor("psum", [P, 8, 512], F32))

        n_wi, n_wo = 2 * DF, DF // P * D
        AT_ONCE, AFTER_B = 3, 3
        base = -(-nc.sbuf_base // 32) * 32
        w_all = sb("w_all", [P, NE * (n_wi + n_wo)])
        wi_all = w_all[0:KC, 0:NE * n_wi].rearrange("p (e k f) -> p e k f", e=NE, k=2)
        wo_all = w_all[:, NE * n_wi:NE * (n_wi + n_wo)].rearrange("p (e c n) -> p e c n", e=NE, n=D)
        taken = {"A": (AT_ONCE + AFTER_B) * n_wi, "B": AT_ONCE * n_wi}
        limit = {"A": NE * (n_wi + n_wo), "B": (AT_ONCE + AFTER_B) * n_wi}

        def early(name, shape, dt=F32, until="A"):
            a = taken[until]
            taken[until] += -(-int(np.prod(shape[1:])) // 8) * 8
            assert taken[until] <= limit[until]
            return nc.alloc_sbuf_tensor_at(name, shape, dt, offset=base + 4 * a)[:]

        cst = sb("cst", [P, C_N])
        ident = cst[:, C_ID:C_ID + P]
        tri = cst[:, C_TRI:C_TRI + P]
        mask = cst[:, C_MASK:C_MASK + CH * HW]
        e8 = cst[:, C_E8:C_E8 + NE]
        rows_of = cst[:, C_ROW:C_PAD].rearrange("p (b j) -> p b j", j=TPB)
        ones = sb("ones", [P, P])
        inv_d = sb("inv_d", [P, KC])
        neg_half = sb("neg_half", [P, 2 * TPB])
        ind = early("ind", [P, CH * P], F32R, "B")
        proj_in = sb("proj_in", [KC, 2, DB])
        proj_dup = early("proj_dup", [KC, 2, P])
        nw = sb("nw", [KC, 2])
        pw = early("pw", [KC, 2, P])
        gt = early("gt", [KC, 2, P])
        wqkv = early("wqkv", [KC, 2, 3 * D])
        rw = sb("rw", [KC, 2, NE])
        rc = sb("rc", [KC, 2, NE])
        pm = sb("pm", [M, HD])
        pm_rep = sb("pm_rep", [M, HW, HD])
        bd = early("bd", [KC, HW, M], F32, "B")
        ft = early("ft", [KC, 4, P])
        wp = sb("wp", [P, 2, EXT])
        wpt = early("wpt", [KC, 2, D + 1])
        f_hi = {}
        f_lo = {}
        for name, n in (("qd", NF), ("kd", NF), ("qkv", 3 * D), ("h", EXT + P)):
            for part, f in (("hi", f_hi), ("lo", f_lo)):
                until = {"kd": "A", "qd": "B"}
                f[name] = (early(f"f_{name}_{part}", [P, n], F32R, until[name]) if name in until
                           else sb(f"f_{name}_{part}", [P, n], F32R)[:])

        idx_i = sb("idx_i", [P, NB, TPB], I32)
        idx_f = sb("idx_f", [P, NB, TPB])
        idx_w = sb("idx_w", [P, NB, TPB])
        idx = sb("idx", [P, NB, TPB], U32)
        idx_b = [sb(f"idx_b{u}", [P, TPB], U32) for u in range(2)]
        basin = [sb(f"basin{u}", [P, TPB, DB]) for u in range(2)]
        basin_all = sb("basin_all", [P, NB, TPB, DB])
        split = [sb(f"split{u}", [P, TPB, 2 * DB]) for u in range(2)]
        bt = [early(f"bt{u}", [P, SEQ], F32R) for u in range(2)]
        quad = early("quad", [P, TPB, 2, DB])
        qs = sb("qs", [P, TPB, 2])
        pow_in = sb("pow_in", [P, 2 * TPB])
        scales = sb("scales", [P, NB, 2 * TPB])
        h0 = sb("h0", [P, NB, TPB, EXT])
        rmax = [sb(f"rmax{u}", [P, TPB]) for u in range(2)]
        nmax = [sb(f"nmax{u}", [P, TPB]) for u in range(2)]
        features_sb = sb("features_sb", [P, CH * SEQ])
        ek = [features_sb[:, 0:TPB * NF].rearrange("p (j f) -> p j f", j=TPB), early("ek1", [P, TPB, NF])]
        ksq = [early(f"ksq{u}", [P, TPB, D]) for u in range(2)]
        val = [early(f"val{u}", [P, TPB, D]) for u in range(2)]
        vsum2 = sb("vsum2", [P, 2, D])
        vsum = sb("vsum", [P, D])
        vp = [early(f"vp{u}", [P, TPB * H, VC]) for u in range(2)]
        nmin = sb("nmin", [P, 1])
        gmin = sb("gmin", [1, 1])
        nbatch = sb("nbatch", [P, NB])
        nb_now = sb("nb_now", [P, 1])
        rms2 = sb("rms2", [P, TPB])
        dmax = sb("dmax", [P, TPB])
        kq = sb("kq", [P, TPB * H])
        farg = sb("farg", [P, TPB * H])
        s_flat = sb("s_flat", [P, NB * CH * HW * VC])
        s_all = s_flat[:].rearrange("p (b c v) -> p b c v", b=NB, v=VC)
        ev_flat = sb("ev_flat", [P, NB * CH * HW * VC])
        ev_all = ev_flat[:].rearrange("p (b c v) -> p b c v", b=NB, v=VC)
        mask_eps = sb("mask_eps", [P, CH * HW])
        mask_den = sb("mask_den", [P, CH * HW])

        nglob = sb("nglob", [P, 1])
        dcb = sb("dcb", [P, NB])
        cb = sb("cb", [P, NB])
        xs = [sb(f"xs{u}", [P, TPB, DB]) for u in range(2)]
        xt = [early(f"xt{u}", [P, SEQ], F32R, "B") for u in range(2)]
        qsq = early("qsq", [P, TPB, D], F32, "B")
        qr = sb("qr", [P, TPB * H])
        smax = sb("smax", [P, TPB, H])
        sd = sb("sd", [P, TPB, H])
        sdh = sb("sdh", [P, TPB, 2 * H])
        sdt = early("sdt", [P, SEQ], F32R, "B")
        eq = features_sb[:, 0:CH * SEQ].rearrange("p (c n) -> p c n", c=CH)
        kv = [sb(f"kv{u}", [P, CH * HW * VC]) for u in range(2)]
        zr = sb("zr", [P, 2, H])
        attn = [sb(f"attn{u}", [P, 2, D]) for u in range(2)]
        at = [sb(f"at{u}", [P, 2 * 2 * P]) for u in range(2)]
        row = [sb(f"row{u}", [P, TPB, ROW]) for u in range(2)]
        bn = sb("bn", [P, TPB, 6])
        ve = sb("ve", [P, TPB])
        dlog = sb("dlog", [P, TPB, NE])
        dscl = sb("dscl", [P, TPB, NE])
        pexp = sb("pexp", [P, TPB, NE])
        psm = sb("psm", [P, TPB])
        lmax = sb("lmax", [P, TPB])
        m8 = sb("m8", [P, TPB, NE])
        mm8 = sb("mm8", [P, TPB])
        onehot = sb("onehot", [P, TPB, NE])
        cnt = sb("cnt", [P, TPB + 1, NE])
        carry = sb("carry", [P, NE])
        pos = sb("pos", [P, TPB, NE])
        rank = sb("rank", [P, TPB])
        sbase = sb("sbase", [P, TPB])
        slot = [sb(f"slot{u}", [P, TPB], U32) for u in range(2)]

        flat0, flat1 = (split[u][:].rearrange("p j d -> p (j d)")[0:1] for u in range(2))
        over = flat0[:, 0:NE * CNTS].rearrange("p (e k) -> p e k", e=NE)
        past = flat1[:, 0:NT * NE].rearrange("p (t e) -> p t e", e=NE)
        past_n = flat0[:, 0:NT * NE].rearrange("p (t e) -> p t e", e=NE)
        upto = xs[0][:].rearrange("p j d -> p (j d)")[0:1, 0:NE * NE].rearrange("p (e f) -> p e f", e=NE)
        tiles_of = sb("tiles_of", [1, NE])
        ends = sb("ends", [1, NE])
        t_exp = sb("t_exp", [1, NT])
        t_first = sb("t_first", [1, NT])
        t_within = sb("t_within", [1, NT])
        tile_slot = sb("tile_slot", [1, NT], I32)
        tile_expert = sb("tile_expert", [1, NT], I32)
        fill = sb("fill", [P, NE], U32)

        ROT = 3
        x_rows = [ev_flat[:, u * ROW:(u + 1) * ROW] for u in range(ROT)]
        orow = [ev_flat[:, ROT * ROW + u * D:ROT * ROW + (u + 1) * D] for u in range(ROT)]
        xn = ev_flat[:, ROT * (ROW + D):ROT * (ROW + D) + D]
        xe = ev_flat[0:KC, ROT * (ROW + D) + D:ROT * (ROW + D) + D + 2 * P].rearrange("p (k n) -> p k n", k=2)
        hid = s_flat[:, 0:DF].rearrange("p (f n) -> p f n", n=P)
        n2 = ROT * (ROW + D) + D + 2 * P
        wi_now = [m.rearrange("p (k f) -> p k f", k=2) for m in (
            s_flat[0:KC, DF:DF + n_wi], s_flat[0:KC, DF + n_wi:DF + 2 * n_wi], ev_flat[0:KC, n2:n2 + n_wi])]
        oidx = [sb(f"oidx{u}", [P, 1], U32) for u in range(ROT)]
        blank = sb("blank", [P, ROW])

        names = """w_in ids_in gathered0 gathered1 blank_out filled sent0 sent1 wi_in w_late x_in0 x_in1 x_in2 fin0 fin1 fin2
        pool_const prep_pe prep_hi prep_v steps idx_r idxb_r split_r tr_r bt_r ph_r h0_r quad_r pow_in_r scale_r kept
        pd_r pkv_r nmax_r exp_r kv_r nmin_r nt_r gmin_r nbc_r farg_r f_r vs_half vs_r vp_r s_r sev_r
        dcb_r cb_r kvb_r xs_r xsplit_r tc_r t_ev qd_r qq_r smax_r qsq_r sd_r fm_r fe_r eps_r
        ek_r norm_r pj_r h1_r ve_r std_r cnt_r pref_r pref_used dscl_r pexp_r slot_r sent_r fin_r
        carry_r tot_r fill_r table_r wi_r xn_r ct_r xe_r hid_r relu_r y_r o_r oidx_r settled""".split()
        S = {n: sem(n) for n in names}
        (w_in, ids_in, gathered0, gathered1, blank_out, filled, sent0, sent1, wi_in, w_late, x_in0, x_in1, x_in2, fin0, fin1, fin2,
         pool_const, prep_pe, prep_hi, prep_v, steps, idx_r, idxb_r, split_r, tr_r, bt_r, ph_r, h0_r, quad_r, pow_in_r, scale_r, kept,
         pd_r, pkv_r, nmax_r, exp_r, kv_r, nmin_r, nt_r, gmin_r, nbc_r, farg_r, f_r, vs_half, vs_r, vp_r, s_r, sev_r,
         dcb_r, cb_r, kvb_r, xs_r, xsplit_r, tc_r, t_ev, qd_r, qq_r, smax_r, qsq_r, sd_r, fm_r, fe_r, eps_r,
         ek_r, norm_r, pj_r, h1_r, ve_r, std_r, cnt_r, pref_r, pref_used, dscl_r, pexp_r, slot_r, sent_r, fin_r,
         carry_r, tot_r, fill_r, table_r, wi_r, xn_r, ct_r, xe_r, hid_r, relu_r, y_r, o_r, oidx_r, settled) = S.values()
        gathered, sent = (gathered0, gathered1), (sent0, sent1)
        x_in, fin = (x_in0, x_in1, x_in2), (fin0, fin1, fin2)

        block = ctx.enter_context(nc.Block())

        def steps_of(eng, n, body, ahead=1, cycle=2):
            body(0, 0, 0)
            rounds = (n - 1 - ahead) // cycle
            with eng.Fori(0, rounds) as i:
                for m in range(1, cycle + 1):
                    body(i * cycle + m, i + m // cycle, m % cycle)
            for k in range(1 + cycle * rounds, n):
                body(k, k // cycle, k % cycle)

        def settle(eng):
            eng.sem_inc(settled, 1)

        def has(k, n, steps=NB):
            return not isinstance(k, int) or 0 <= k + n < steps

        def bank(k, n=512):
            return psum[:, k, 0:n]

        T, PS = bank(6), bank(7)
        prefix = psum[:, 2, 2 * D:2 * D + NE]
        HALF = NF // 2

        @block.sync
        def _(sp):
            with nc.allow_non_contiguous_dma(reason="runs of 4 ids, and 192 norm weights"):
                sp.dma_start(idx_i[:], ids.rearrange("b (p j) -> p b j", j=TPB)).then_inc(ids_in, 16)
                sp.dma_start(nw[:], norm_w.rearrange("(k p) -> p k", p=KC)).then_inc(w_in, 16)
            sp.dma_start(cst[:], consts).then_inc(w_in, 16)
            sp.dma_start(proj_in[:], proj_w.rearrange("(k p) d -> p k d", p=KC)).then_inc(w_in, 16)
            sp.dma_start(rw[:], router_w.rearrange("(k p) e -> p k e", p=KC)).then_inc(w_in, 16)
            sp.dma_start(pm[:], proj_mat).then_inc(w_in, 16)
            sp.dma_start(wqkv, w_qkv.rearrange("(k p) n -> p k n", p=KC)).then_inc(w_in, 16)
            sp.dma_start(wp[0:KC, :, 0:D], w_proj.rearrange("(k p) n -> p k n", p=KC)).then_inc(w_in, 16)
            sp.dma_start(wp[KC:KC + 1, 1, 0:D], b_proj.rearrange("(a n) -> a n", a=1)).then_inc(w_in, 16)
            sp.wait_ge(pool_const, 2)
            sp.dma_start(slots[NE * SEG:, :].rearrange("(t p) r -> p t r", p=P), bc(blank[:, :], 1, SPARE)).then_inc(blank_out, 16)
            sp.dma_start(wi_all[:, 0:AT_ONCE], wi[0:AT_ONCE].rearrange("e (k p) f -> p e k f", p=KC)).then_inc(wi_in, 16)
            sp.wait_ge(sev_r, NB)
            sp.dma_start(wi_all[:, AT_ONCE + AFTER_B:NE], wi[AT_ONCE + AFTER_B:NE].rearrange("e (k p) f -> p e k f", p=KC)).then_inc(w_late, 16)
            for e in range(NE):
                sp.dma_start(wo_all[:, e], wo[e].rearrange("(c p) n -> p c n", p=P)).then_inc(w_late, 16)
            sp.wait_ge(fm_r, NB * CH)
            for e in range(AT_ONCE, AT_ONCE + AFTER_B):
                sp.dma_start(wi_all[:, e], wi[e].rearrange("(k p) f -> p k f", p=KC)).then_inc(w_late, 16)

            def load_rows(t, u):
                first = sp.value_load(tile_slot[0:1, bass.ds(t, 1)], min_val=0, max_val=NE * SEG + (SPARE - 1) * P)
                sp.dma_start(x_rows[u], slots[bass.ds(first, P), :]).then_inc(x_in[u], 16)

            sp.wait_ge(blank_out, 16)
            sp.wait_ge(table_r, 2)
            for u in range(2):
                sp.wait_ge(sent[u], 16 * TPB * NB // 2)
            sp.wait_ge(filled, 16 * NE)
            load_rows(0, 0)
            load_rows(1, 1)

            def ahead_rows(t, h, u):
                if has(t, 2, NT):
                    if has(t, -1):
                        sp.wait_ge(o_r, t)
                        settle(sp)
                    load_rows(t + 2, (u + 2) % ROT)

            steps_of(sp, NT, ahead_rows, ahead=2, cycle=ROT)
            for u in range(ROT):
                sp.wait_ge(fin[u], 16 * len(range(u, NT, ROT)))

        @block.gpsimd
        def _(pool):
            g = nc.gpsimd
            g.memset(blank[:, 0:R_ROW], 0.0).then_inc(pool_const, 1)
            g.memset(blank[:, R_ROW:ROW], FAR).then_inc(pool_const, 1)
            g.memset(ones[:], 1.0).then_inc(pool_const, 1)
            g.memset(inv_d[:], 1.0 / D).then_inc(pool_const, 1)
            g.memset(neg_half[:], -0.5).then_inc(pool_const, 1)
            g.memset(at[0][:], 1.0).then_inc(pool_const, 1)
            g.memset(at[1][:], 1.0).then_inc(pool_const, 1)
            g.memset(carry[:], 0.0).then_inc(pool_const, 1)
            g.memset(cnt[:], 0.0).then_inc(pool_const, 1)
            pool.sem_inc(sent_r, 1)
            pool.sem_inc(fin_r, ROT - 1)

            def gather(b, u):
                g.tensor_copy(idx_b[u][:], idx[:, b, :]).then_inc(idxb_r, 1)
                pool.wait_ge(idxb_r, b + 1)
                settle(pool)
                for j in range(TPB):
                    g.indirect_dma_start(
                        out=basin[u][:, j, :], out_offset=None, in_=coords,
                        in_offset=bass.IndirectOffsetOnAxis(ap=idx_b[u][:, j:j + 1], axis=0),
                    ).then_inc(gathered[u], 16)

            def keep(b, h, u):
                pool.wait_ge(gathered[u], (h + 1) * (16 * TPB))
                g.tensor_copy(basin_all[:, b, :, :], basin[u][:]).then_inc(kept, 1)

            def power(b):
                pool.wait_ge(pow_in_r, b + 1)
                g.tensor_tensor(scales[:, b, :], pow_in[:], neg_half[:], ALU.pow).then_inc(scale_r, 1)

            pool.wait_ge(idx_r, 1)
            gather(0, 0)
            gather(1, 1)
            keep(0, 0, 0)
            power(0)
            pool.wait_ge(prep_v, 1)
            g.tensor_copy(ev_all[:, :, :, HD], bc(mask_den[:], 1, NB)).then_inc(pool_const, 1)

            def step_a(b, h, u):
                if has(b, 2):
                    pool.wait_ge(quad_r, b * TPB + TPB)
                    pool.wait_ge(kept, b + 1)
                    gather(b + 2, u)
                if has(b, 1):
                    keep(b + 1, h + u, 1 - u)
                    power(b + 1)
                pool.wait_ge(kv_r, b * TPB + TPB)
                if has(b, -1):
                    pool.wait_ge(s_r, b)
                g.tensor_tensor(vsum2[:], val[u][:, 0:2, :], val[u][:, 2:4, :], ALU.add).then_inc(vs_half, 1)
                pool.wait_ge(vs_half, b + 1)
                g.tensor_tensor(vsum[:], vsum2[:, 0, :], vsum2[:, 1, :], ALU.add).then_inc(vs_r, 1)
                pool.wait_ge(f_r, b + 1)
                g.tensor_tensor(vp[u][:, :, 0:HD], val[u].rearrange("p j (h d) -> p (j h) d", d=HD),
                                bc(vp[u][:, :, HD], 2, HD), ALU.mult).then_inc(vp_r, 1)

            steps_of(pool, NB, step_a, ahead=3)

            def scaled(b, u):
                if not isinstance(b, int) or b >= 2:
                    pool.wait_ge(xsplit_r, b - 1)
                g.tensor_tensor(xs[u][:], basin_all[:, b, :, :], bc(scales[:, b, TPB:2 * TPB], 2, DB), ALU.mult
                                ).then_inc(xs_r, 1)

            def send(b, u):
                pool.wait_ge(std_r, b * 2 + 2)
                pool.wait_ge(slot_r, b + 1)
                settle(pool)
                for j in range(TPB):
                    g.indirect_dma_start(
                        out=slots, out_offset=bass.IndirectOffsetOnAxis(ap=slot[u][:, j:j + 1], axis=0),
                        in_=row[u][:, j, :], in_offset=None, bounds_check=NE * SEG - 1, oob_is_err=False,
                    ).then_inc(sent[u], 16)

            pool.wait_ge(kept, NB)
            pool.wait_ge(scale_r, NB)
            scaled(0, 0)

            def step_b(b, h, u):
                if has(b, 1):
                    scaled(b + 1, 1 - u)
                for n, (lo, hi) in enumerate(((0, 2), (2, 4), (4, 5))):
                    pool.wait_ge(fe_r, b * CH + hi)
                    settle(pool)
                    g.tensor_scalar(eq[:, lo:hi, :], eq[:, lo:hi, :], EPS_FEAT, 1.0, ALU.add, ALU.mult).then_inc(eps_r, 1)
                if has(b, -1):
                    send(b - 1, 1 - u)
                pool.wait_ge(ve_r, b + 1)
                g.tensor_tensor(row[u][:, :, R_STD], ve[:], neg_half[:, 0:TPB], ALU.pow).then_inc(std_r, 1)
                g.tensor_copy(row[u][:, :, R_ROW], rows_of[:, b, :]).then_inc(std_r, 1)
                if has(b, -1):
                    pool.wait_ge(sent[1 - u], (h + u) * (16 * TPB))
                    pool.sem_inc(sent_r, 1)

            steps_of(pool, NB, step_b)
            send(NB - 1, (NB - 1) % 2)

            pool.wait_ge(fill_r, 1)
            for e in range(NE):
                g.indirect_dma_start(
                    out=slots, out_offset=bass.IndirectOffsetOnAxis(ap=fill[:, e:e + 1], axis=0),
                    in_=blank[:, :], in_offset=None, bounds_check=NE * SEG - 1, oob_is_err=False,
                ).then_inc(filled, 16)

            def fetch(t, u):
                e = pool.value_load(tile_expert[0:1, bass.ds(t, 1)], min_val=0, max_val=NE - 1)
                g.tensor_copy(wi_now[u], wi_all[:, bass.ds(e, 1), :, :].rearrange("p e k f -> p (e k) f")).then_inc(wi_r, 1)

            pool.wait_ge(wi_in, 16)
            pool.wait_ge(w_late, 16 * (1 + NE + AFTER_B))
            pool.wait_ge(table_r, 1)
            fetch(0, 0)
            fetch(1, 1)

            def step_c(t, h, u):
                if has(t, 2, NT):
                    if has(t, -1):
                        pool.wait_ge(hid_r, t * 2)
                        settle(pool)
                    fetch(t + 2, (u + 2) % ROT)
                if has(t, -1, NT):
                    pool.wait_ge(fin[(u - 1) % ROT], (h + (1 if u else 0)) * 16)
                    pool.sem_inc(fin_r, 1)
                pool.wait_ge(oidx_r, t + 1)
                pool.wait_ge(o_r, t + 1)
                settle(pool)
                g.indirect_dma_start(
                    out=out_rows, out_offset=bass.IndirectOffsetOnAxis(ap=oidx[u][:, 0:1], axis=0),
                    in_=orow[u], in_offset=None, bounds_check=TOK - 1, oob_is_err=False,
                ).then_inc(fin[u], 16)

            steps_of(pool, NT, step_c, ahead=2, cycle=ROT)

        @block.scalar
        def _(act):
            a = nc.scalar
            act.wait_ge(prep_pe, 2)
            a.activation(f_hi["h"][:, 0:EXT], psum[:, 0, 0:EXT], ACT.Copy).then_inc(prep_hi, 1)
            a.activation(f_hi["h"][:, EXT:EXT + P], psum[:, 0, EXT:EXT + P], ACT.Copy, scale=1.0 / D).then_inc(prep_hi, 1)
            a.activation(f_hi["qkv"].rearrange("p (a n) -> p a n", a=2), psum[:, 4:6, 0:3 * D // 2],
                         ACT.Copy).then_inc(prep_hi, 1)
            act.wait_ge(prep_pe, 3)
            a.activation(f_hi["kd"].rearrange("p (a n) -> p a n", a=2), psum[:, 6:8, 0:HALF], ACT.Copy).then_inc(prep_hi, 1)
            a.activation(f_hi["qd"].rearrange("p (a n) -> p a n", a=2), psum[:, 1:3, 0:HALF], ACT.Copy).then_inc(prep_hi, 1)

            def basin_t(b, u):
                act.wait_ge(tr_r, b + 1)
                a.activation(bt[u], T, ACT.Copy).then_inc(bt_r, 1)

            def keep_h0(b, j):
                act.wait_ge(quad_r, b * TPB + (j + 1))
                settle(act)
                a.activation(h0[:, b, j, :], psum[:, 5, 0:EXT], ACT.Copy).then_inc(h0_r, 1)

            basin_t(0, 0)
            for j in range(TPB):
                keep_h0(0, j)

            def step_a(b, h, u):
                for j in range(TPB):
                    act.wait_ge(nmax_r, b * TPB + (j + 1))
                    settle(act)
                    q = 2 * (j % 2)
                    sc = scales[:, b, TPB + j:TPB + j + 1]
                    a.activation(ek[u][:, j, :].rearrange("p (a n) -> p a n", a=2), psum[:, q:q + 2, 0:HALF],
                                 ACT.Exp, bias=nmax[u][:, j:j + 1], scale=sc).then_inc(exp_r, 1)
                    act.wait_ge(pkv_r, b * TPB + (j + 1))
                    settle(act)
                    a.activation(ksq[u][:, j, :], psum[:, 4, 0:D], ACT.Square, scale=sc)
                    a.activation(val[u][:, j, :], psum[:, 4, D:2 * D], ACT.Copy, scale=sc).then_inc(kv_r, 1)
                if has(b, 1):
                    basin_t(b + 1, 1 - u)
                    keep_h0(b + 1, 0)
                act.wait_ge(farg_r, b + 1)
                a.activation(vp[u][:, :, HD], farg[:], ACT.Exp).then_inc(f_r, 1)
                if has(b, 1):
                    for j in range(1, TPB):
                        keep_h0(b + 1, j)

            steps_of(act, NB, step_a)

            act.wait_ge(dcb_r, 1)
            a.activation(cb[:], dcb[:], ACT.Exp).then_inc(cb_r, 1)

            def evacuate(n, dst, src):
                act.wait_ge(tc_r, n + 1)
                a.activation(dst, src, ACT.Copy).then_inc(t_ev, 1)

            def q_squares(b, pair):
                act.wait_ge(qq_r, b * 2 + (pair + 1))
                a.activation(qsq[:, 2 * pair:2 * pair + 2, :], psum[:, 2, 0:2 * D], ACT.Square).then_inc(qsq_r, 1)

            evacuate(0, xt[0], T)
            q_squares(0, 0)
            q_squares(0, 1)
            evacuate(1, sdt[0:2 * H, :], T[0:2 * H, :])

            def step_b(b, h, u):
                more = has(b, 1)
                n = b * 4 + 2
                if more:
                    evacuate(n, xt[1 - u], T)
                for i in range(CH):
                    act.wait_ge(fm_r, b * CH + (i + 1))
                    a.activation(eq[:, i, :], bank(3 + (CH * u + i) % 2), ACT.Exp).then_inc(fe_r, 1)
                    if more and i == 3:
                        q_squares(b + 1, 0)
                if more:
                    q_squares(b + 1, 1)
                if has(b, -1):
                    act.wait_ge(dscl_r, b)
                    a.activation(pexp[:], dscl[:], ACT.Exp).then_inc(pexp_r, 1)
                evacuate(n + 1 if more else n, at[0][0:KC, :], T[0:KC, :])
                if more:
                    evacuate(n + 2, sdt[0:2 * H, :], T[0:2 * H, :])
                evacuate(n + 3 if more else n + 1, at[1][0:KC, :], T[0:KC, :])

            steps_of(act, NB, step_b)
            act.wait_ge(dscl_r, NB)
            a.activation(pexp[:], dscl[:], ACT.Exp).then_inc(pexp_r, 1)

            def x_t(t):
                act.wait_ge(ct_r, t + 1)
                a.activation(xe.rearrange("p k n -> p (k n)"), T[0:KC, 0:2 * P], ACT.Copy).then_inc(xe_r, 1)

            x_t(0)

            def step_c(t, h, u):
                act.wait_ge(hid_r, t * 2 + 1)
                a.activation(hid[:, 0:4, :].rearrange("p f n -> p (f n)"), bank(3), ACT.Relu).then_inc(relu_r, 1)
                act.wait_ge(hid_r, t * 2 + 2)
                a.activation(hid[:, 4:6, :].rearrange("p f n -> p (f n)"), bank(4, 2 * P), ACT.Relu).then_inc(relu_r, 1)
                if has(t, 1, NT):
                    x_t(t + 1)

            steps_of(act, NT, step_c, cycle=ROT)

        @block.vector
        def _(dve):
            v = nc.vector
            base = [0]
            done = [0]

            def link(ins):
                done[0] += 1
                ins.then_inc(steps, 1)
                dve.wait_ge(steps, base[0] + done[0])

            dve.wait_ge(ids_in, 16)
            link(v.tensor_copy(idx_f[:], idx_i[:]))
            link(v.tensor_scalar(idx_w[:], idx_f[:], 0.0, float(VOCAB), ALU.is_lt, ALU.mult))
            link(v.tensor_tensor(idx_w[:], idx_w[:], idx_f[:], ALU.add))
            v.tensor_scalar(idx[:], idx_w[:], 0.0, float(VOCAB - 1), ALU.max, ALU.min).then_inc(idx_r, 1)

            dve.wait_ge(w_in, 16 * 8)
            v.tensor_scalar(mask_den[:], mask, EPS_FEAT * SEQ, None, ALU.mult)
            v.tensor_scalar(mask_eps[:], mask, EPS_FEAT, None, ALU.mult).then_inc(prep_v, 1)
            v.tensor_copy(ind, cst[:, C_IND:C_IND + CH * P])
            for k in range(2):
                v.tensor_scalar(pw[:, k, :].rearrange("p (a d) -> p a d", a=2), bc(proj_in[:, k, :], 1, 2), nw[:, k:k + 1], None,
                                ALU.mult)
                v.tensor_copy(proj_dup[:, k, :].rearrange("p (a d) -> p a d", a=2), bc(proj_in[:, k, :], 1, 2))
            v.tensor_copy(pm_rep[:], bc(pm[:], 1, HW)).then_inc(prep_v, 1)
            dve.wait_ge(prep_pe, 1)
            v.tensor_tensor(gt.rearrange("p k (a d) -> p k a d", a=2).rearrange("p k a d -> p (k a) d"),
                            pw.rearrange("p k (a d) -> p (k a) d", a=2), bc(psum[0:KC, 0, 0:DB], 1, 4), ALU.subtract)
            v.tensor_tensor(rc[:], rw[:], bc(psum[0:KC, 0, DB:DB + NE], 1, 2), ALU.subtract)
            v.scalar_tensor_tensor(out=bd, in0=bc(psum[0:KC, 2, 0:M], 1, HW), scalar=NORM,
                                   in1=bc(cst[0:KC, C_HM:C_HM + HW], 2, M), op0=ALU.mult, op1=ALU.mult)
            v.tensor_copy(wpt, psum[0:KC, 3, 0:2 * (D + 1)].rearrange("p (k n) -> p k n", k=2)).then_inc(prep_v, 1)
            dve.wait_ge(prep_pe, 2)
            v.tensor_copy(wp[0:KC, 0, D:EXT], psum[0:KC, 2, 0:NE])
            v.tensor_copy(wp[0:KC + 1, 1, D:EXT], psum[0:KC + 1, 2, NE:2 * NE])
            v.tensor_copy(ft.rearrange("p c n -> p (c n)"), psum[0:KC, 1, :]).then_inc(prep_v, 1)
            dve.wait_ge(prep_hi, 2)
            v.tensor_tensor(f_lo["h"][:, 0:EXT], psum[:, 0, 0:EXT], f_hi["h"][:, 0:EXT].bitcast(F32), ALU.subtract)
            v.scalar_tensor_tensor(out=f_lo["h"][:, EXT:EXT + P], in0=psum[:, 0, EXT:EXT + P], scalar=1.0 / D,
                                   in1=f_hi["h"][:, EXT:EXT + P].bitcast(F32), op0=ALU.mult, op1=ALU.subtract
                                   ).then_inc(prep_v, 1)
            dve.wait_ge(prep_hi, 3)
            v.tensor_tensor(f_lo["qkv"].rearrange("p (a n) -> p a n", a=2), psum[:, 4:6, 0:3 * D // 2],
                            f_hi["qkv"].bitcast(F32).rearrange("p (a n) -> p a n", a=2), ALU.subtract)
            dve.wait_ge(prep_hi, 4)
            v.tensor_tensor(f_lo["kd"].rearrange("p (a n) -> p a n", a=2), psum[:, 6:8, 0:HALF],
                            f_hi["kd"].bitcast(F32).rearrange("p (a n) -> p a n", a=2), ALU.subtract)
            dve.wait_ge(prep_hi, 5)
            v.tensor_tensor(f_lo["qd"].rearrange("p (a n) -> p a n", a=2), psum[:, 1:3, 0:HALF],
                            f_hi["qd"].bitcast(F32).rearrange("p (a n) -> p a n", a=2), ALU.subtract).then_inc(prep_v, 1)

            def split_into(dst, src, signal):
                link(v.tensor_copy(dst[:, :, 0:DB].bitcast(F32R), src))
                v.tensor_tensor(dst[:, :, DB:2 * DB], src, dst[:, :, 0:DB], ALU.subtract).then_inc(signal, 1)

            def split_basin(b, h, u):
                dve.wait_ge(gathered[u], (h + 1) * (16 * TPB))
                if not isinstance(b, int) or b >= 2:
                    dve.wait_ge(tr_r, b - 1)
                split_into(split[u], basin[u][:], split_r)

            def quads(b, u, j):
                dve.wait_ge(ph_r, b * TPB + (j + 1))
                v.tensor_tensor(quad[:, j, :, :], psum[:, 5, EXT:EXT + P].rearrange("p (a d) -> p a d", a=2),
                                bc(basin[u][:, j, :], 1, 2), ALU.mult).then_inc(quad_r, 1)

            def stats(b):
                dve.wait_ge(quad_r, b * TPB + TPB)
                link(v.tensor_reduce(qs[:].rearrange("p j a -> p (j a)"), quad.rearrange("p j a d -> p (j a) d"),
                                     AX.X, ALU.add))
                link(v.tensor_scalar(rms2[:], qs[:, :, 0], EPS_RMS, None, ALU.add))
                v.tensor_copy(pow_in[:, 0:TPB], rms2[:])
                v.scalar_tensor_tensor(out=pow_in[:, TPB:2 * TPB], in0=rms2[:], scalar=EPS_LN, in1=qs[:, :, 1],
                                       op0=ALU.mult, op1=ALU.add).then_inc(pow_in_r, 1)

            def first():
                split_basin(0, 0, 0)
                for j in range(TPB):
                    quads(0, 0, j)
                stats(0)

            first()
            start_a = done[0]

            def keep_s(b):
                dve.wait_ge(s_r, b + 1)
                v.tensor_tensor(s_all[:, b, :, :], PS[:, 0:CH * HW * VC].rearrange("p (c v) -> p c v", v=VC),
                                bc(mask, 2, VC), ALU.mult)
                for i0, i1 in ((0, 2), (2, 3), (3, 5)):
                    w = W0[i0]
                    src = T[:, w * HD:(w + HW) * HD].rearrange("p (h d) -> p h d", d=HD)
                    ins = v.tensor_tensor(
                        ev_all[:, b, i0 * HW:i1 * HW, 0:HD].rearrange("p (i h) d -> p i h d", h=HW), bc(src, 1, i1 - i0),
                        bc(mask_eps[:, i0 * HW:i1 * HW].rearrange("p (i h) -> p i h", h=HW), 3, HD), ALU.mult)
                ins.then_inc(sev_r, 1)

            def step_a(b, h, u):
                base[0], done[0] = (start_a if isinstance(b, int) and b == 0 else
                                    (b - 1) * LINKS_A + start_a + LINKS_A), 0
                if has(b, 1):
                    split_basin(b + 1, h + u, 1 - u)
                for j in range(TPB):
                    dve.wait_ge(pd_r, b * TPB + (j + 1))
                    q = 2 * (j % 2)
                    link(v.tensor_reduce(rmax[u][:, j:j + 1], psum[:, q:q + 2, 0:HALF], AX.XY, ALU.max))
                    if j == 0:
                        dve.wait_ge(scale_r, b + 1)
                    v.tensor_scalar(nmax[u][:, j:j + 1], rmax[u][:, j:j + 1], scales[:, b, TPB + j:TPB + j + 1], -1.0,
                                    ALU.mult, ALU.mult).then_inc(nmax_r, 1)
                    if j == 1 and has(b, -1):
                        keep_s(b - 1)
                dve.wait_ge(nmax_r, b * TPB + TPB)
                v.tensor_reduce(nmin[:], nmax[u][:], AX.X, ALU.min).then_inc(nmin_r, 1)
                dve.wait_ge(nt_r, b + 1)
                v.tensor_reduce(gmin[:], PS[0:1, 0:P], AX.X, ALU.min).then_inc(gmin_r, 1)
                if has(b, 1):
                    quads(b + 1, 1 - u, 0)
                dve.wait_ge(nbc_r, b + 1)
                v.tensor_copy(nbatch[:, bass.ds(b, 1)], PS[:, P:P + 1])
                link(v.tensor_copy(nb_now[:], PS[:, P:P + 1]))
                v.tensor_scalar(dmax[:], nmax[u][:], -1.0, nb_now[:], ALU.mult, ALU.add)
                dve.wait_ge(kv_r, b * TPB + TPB)
                link(v.tensor_reduce(kq[:], ksq[u].rearrange("p j (h d) -> p (j h) d", d=HD), AX.X, ALU.add))
                if has(b, -1):
                    dve.wait_ge(f_r, b)
                v.scalar_tensor_tensor(out=farg[:].rearrange("p (j h) -> p j h", h=H), in0=kq[:].rearrange("p (j h) -> p j h", h=H),
                                       scalar=-0.5 * NORM * NORM, in1=bc(dmax[:], 2, H), op0=ALU.mult, op1=ALU.add
                                       ).then_inc(farg_r, 1)
                if has(b, 1):
                    for j in range(1, TPB):
                        quads(b + 1, 1 - u, j)
                    stats(b + 1)
                    assert done[0] == LINKS_A, done

            LINKS_A = 1 + TPB + 2 + 2
            steps_of(dve, NB, step_a)
            base[0] += done[0]
            done[0] = 0
            keep_s(NB - 1)

            link(v.tensor_reduce(nglob[:], nbatch[:], AX.X, ALU.min))
            v.tensor_scalar(dcb[:], nbatch[:], -1.0, nglob[:], ALU.mult, ALU.add).then_inc(dcb_r, 1)

            def split_x(b, u):
                dve.wait_ge(xs_r, b + 1)
                split_into(split[u], xs[u][:], xsplit_r)

            def q_max(b, j):
                dve.wait_ge(qd_r, b * TPB + (j + 1))
                for q in range(2):
                    ins = v.tensor_reduce(smax[:, j, q * HW:(q + 1) * HW], psum[:, q, 0:HALF].rearrange("p (h m) -> p h m", m=M),
                                          AX.X, ALU.max)
                ins.then_inc(smax_r, 1)

            def q_shift(b):
                dve.wait_ge(qsq_r, b * 2 + 2)
                link(v.tensor_reduce(qr[:], qsq.rearrange("p j (h d) -> p (j h) d", d=HD), AX.X, ALU.add))
                link(v.scalar_tensor_tensor(out=sd[:].rearrange("p j h -> p (j h)"), in0=qr[:], scalar=0.5 * NORM * NORM,
                                            in1=smax[:].rearrange("p j h -> p (j h)"), op0=ALU.mult, op1=ALU.add))
                link(v.tensor_copy(sdh[:, :, 0:H].bitcast(F32R), sd[:]))
                v.tensor_tensor(sdh[:, :, H:2 * H], sd[:], sdh[:, :, 0:H], ALU.subtract).then_inc(sd_r, 1)

            dve.wait_ge(pool_const, 9)
            v.tensor_copy(sdt.rearrange("p (j n) -> p j n", n=P), bc(blank[:, 0:P], 1, TPB)).then_inc(prep_v, 1)
            split_x(0, 0)
            for j in range(TPB):
                q_max(0, j)
            q_shift(0)
            dve.wait_ge(cb_r, 1)
            base[0] += done[0]
            start_b = base[0]

            def route_pick(b, u):
                lg = row[u][:, :, D:EXT]
                link(v.tensor_reduce(lmax[:], lg, AX.X, ALU.max))
                link(v.tensor_tensor(dlog[:], lg, bc(lmax[:], 2, NE), ALU.subtract))
                link(v.scalar_tensor_tensor(out=m8[:], in0=dlog[:], scalar=0.0, in1=bc(e8, 1, TPB), op0=ALU.is_ge, op1=ALU.mult))
                link(v.tensor_reduce(mm8[:], m8[:], AX.X, ALU.max))
                link(v.tensor_tensor(onehot[:], m8[:], bc(mm8[:], 2, NE), ALU.is_equal))
                link(v.tensor_copy(cnt[:, 1, :], onehot[:, 0, :]))
                for j in range(1, TPB):
                    ins = v.tensor_tensor(cnt[:, j + 1, :], cnt[:, j, :], onehot[:, j, :], ALU.add)
                    if j < TPB - 1:
                        link(ins)
                ins.then_inc(cnt_r, 1)

            def route_slot(b, u):
                dve.wait_ge(std_r, b * 2 + 1)
                v.tensor_tensor(dscl[:], dlog[:], bc(row[u][:, :, R_STD], 2, NE), ALU.mult).then_inc(dscl_r, 1)
                dve.wait_ge(pref_r, b + 1)
                v.tensor_tensor(pos[:], cnt[:, 0:TPB, :], bc(prefix, 1, TPB), ALU.add).then_inc(pref_used, 1)
                dve.wait_ge(pref_used, b + 2)
                link(v.tensor_tensor(pos[:], pos[:], onehot[:], ALU.mult))
                link(v.tensor_reduce(rank[:], pos[:], AX.X, ALU.add))
                v.tensor_tensor(carry[:], carry[:], cnt[:, TPB, :], ALU.add).then_inc(carry_r, 1)
                link(v.tensor_scalar(sbase[:], mm8[:], -float(SEG), float(SEG * NE), ALU.mult, ALU.add))
                v.tensor_tensor(slot[u][:], rank[:], sbase[:], ALU.add)
                dve.wait_ge(pexp_r, b + 1)
                link(v.tensor_reduce(psm[:], pexp[:], AX.X, ALU.add))
                v.reciprocal(row[u][:, :, R_GATE], psm[:]).then_inc(slot_r, 1)

            def step_b(b, h, u):
                base[0], done[0] = (start_b if isinstance(b, int) and b == 0 else
                                    (b - 1) * LINKS_B + start_b + LINKS_B0), 0
                if has(b, 1):
                    split_x(b + 1, 1 - u)
                v.scalar_tensor_tensor(out=kv[u][:], in0=s_all[:, b, :, :].rearrange("p c v -> p (c v)"), scalar=cb[:, bass.ds(b, 1)],
                                       in1=ev_all[:, b, :, :].rearrange("p c v -> p (c v)"), op0=ALU.mult, op1=ALU.add
                                       ).then_inc(kvb_r, 1)
                if has(b, 1):
                    for j in range(TPB):
                        q_max(b + 1, j)
                    q_shift(b + 1)
                if has(b, -1):
                    route_slot(b - 1, 1 - u)
                for pair in range(2):
                    dve.wait_ge(ek_r, b * 2 + (pair + 1))
                    ek4 = psum[:, 5, 0:2 * H * VC].rearrange("p (g c) -> p g c", c=VC)
                    link(v.reciprocal(zr[:].rearrange("p j h -> p (j h)"), ek4[:, :, HD]))
                    v.tensor_tensor(attn[pair][:].rearrange("p j (h d) -> p (j h) d", d=HD), ek4[:, :, 0:HD],
                                    bc(zr[:].rearrange("p j h -> p (j h)"), 2, HD), ALU.mult).then_inc(norm_r, 1)
                if has(b, -1):
                    dve.wait_ge(sent_r, b)
                for j in range(TPB):
                    if j % 2 == 0:
                        dve.wait_ge(pj_r, b * 2 + (j // 2 + 1))
                    v.scalar_tensor_tensor(out=row[u][:, j, 0:EXT], in0=h0[:, b, j, :], scalar=scales[:, b, j:j + 1],
                                           in1=psum[:, 7, (j % 2) * EXT:(j % 2 + 1) * EXT], op0=ALU.mult, op1=ALU.add
                                           ).then_inc(h1_r, 1)
                    dve.wait_ge(h1_r, b * TPB + (j + 1))
                    link(v.bn_stats(bn[:, j, :], row[u][:, j, 0:D]))
                    settle(dve)
                    ins = v.bn_aggr(row[u][:, j, R_MEAN:R_MEAN + 2], bn[:, j, :])
                link(ins)
                v.tensor_scalar(ve[:], row[u][:, :, R_STD], EPS_LN, None, ALU.add).then_inc(ve_r, 1)
                route_pick(b, u)
                n = done[0]
                if isinstance(b, int) and b == 0:
                    assert n == LINKS_B0, n
                elif has(b, 1):
                    assert n == LINKS_B, n

            LINKS_B0 = 4 + 2 + 5 + 8
            LINKS_B = LINKS_B0 + 4
            v.sem_inc(pref_used, 1)
            steps_of(dve, NB, step_b)
            base[0] += done[0]
            done[0] = 0
            route_slot(NB - 1, (NB - 1) % 2)

            dve.wait_ge(tot_r, 1)
            v.tensor_tensor(fill[:], prefix, cst[:, C_PAD:C_PAD + NE], ALU.add).then_inc(fill_r, 1)
            row0 = cst[0:1, :]
            link(v.tensor_tensor(over, bc(prefix[0:1], 2, CNTS), bc(row0[:, C_THR:C_THR + CNTS], 1, NE), ALU.is_gt))
            link(v.tensor_reduce(tiles_of[:], over, AX.X, ALU.add))
            link(v.tensor_tensor(upto, bc(tiles_of[:], 1, NE), row0[:, C_LE:C_T].rearrange("p (e f) -> p e f", e=NE), ALU.mult))
            link(v.tensor_reduce(ends[:], upto, AX.X, ALU.add))
            link(v.tensor_tensor(past, bc(row0[:, C_T:C_N], 2, NE), bc(ends[:], 1, NT), ALU.is_ge))
            v.tensor_tensor(past_n, past, bc(tiles_of[:], 1, NT), ALU.mult)
            link(v.tensor_reduce(t_exp[:], past, AX.X, ALU.add))
            v.tensor_scalar(tile_expert[:], t_exp[:], float(NE - 1), None, ALU.min).then_inc(table_r, 1)
            link(v.tensor_reduce(t_first[:], past_n, AX.X, ALU.add))
            link(v.tensor_tensor(t_within[:], row0[:, C_T:C_N], t_first[:], ALU.subtract))
            link(v.tensor_scalar(t_within[:], t_within[:], float(P), None, ALU.mult))
            v.scalar_tensor_tensor(out=tile_slot[:], in0=t_exp[:], scalar=float(SEG), in1=t_within[:], op0=ALU.mult,
                                   op1=ALU.add).then_inc(table_r, 1)

            def normed(t, h, u):
                dve.wait_ge(x_in[u], h * 16 + 16)
                if not isinstance(t, int) or t > 0:
                    dve.wait_ge(ct_r, t)
                v.tensor_scalar(xn, x_rows[u][:, 0:D], x_rows[u][:, R_MEAN:R_MEAN + 1],
                                x_rows[u][:, R_STD:R_STD + 1], ALU.subtract, ALU.mult).then_inc(xn_r, 1)

            normed(0, 0, 0)

            def step_c(t, h, u):
                if has(t, 1, NT):
                    normed(t + 1, h + (u + 1) // ROT, (u + 1) % ROT)
                if has(t, -1, NT):
                    dve.wait_ge(fin_r, t)
                v.tensor_copy(oidx[u][:], x_rows[u][:, R_ROW:ROW]).then_inc(oidx_r, 1)
                dve.wait_ge(y_r, t + 1)
                v.scalar_tensor_tensor(out=orow[u], in0=PS[:, 0:D], scalar=x_rows[u][:, R_GATE:R_GATE + 1],
                                       in1=x_rows[u][:, 0:D], op0=ALU.mult, op1=ALU.add).then_inc(o_r, 1)

            steps_of(dve, NT, step_c, cycle=ROT)

        @block.tensor
        def _(pe):
            mm = nc.tensor.matmul
            pe.wait_ge(pool_const, 4)
            pe.wait_ge(prep_v, 2)
            for k in range(2):
                mm(psum[0:KC, 0, 0:DB], lhsT=inv_d[0:KC, :], rhs=pw[:, k, 0:DB], start=k == 0, stop=k == 1)
            for k in range(2):
                mm(psum[0:KC, 0, DB:DB + NE], lhsT=inv_d[0:KC, :], rhs=rw[:, k, :], start=k == 0, stop=k == 1)
            mm(psum[0:KC, 2, 0:M], lhsT=pm_rep[:].rearrange("m h d -> m (h d)"), rhs=ident[0:M, 0:M], start=True, stop=True)
            for kn in range(2):
                c0 = kn * (D + 1)
                nc.tensor.transpose(psum[0:KC, 3, c0:c0 + KC], wp[0:KC, 0, kn * KC:(kn + 1) * KC], ident[0:KC, 0:KC])
                ins = nc.tensor.transpose(psum[0:KC, 3, c0 + KC:c0 + D + 1], wp[0:KC + 1, 1, kn * KC:(kn + 1) * KC],
                                          ident[0:KC + 1, 0:KC + 1])
            ins.then_inc(prep_pe, 1)
            pe.wait_ge(prep_v, 3)
            for c in range(4):
                for k in range(2):
                    mm(psum[0:KC, 1, c * P:(c + 1) * P], lhsT=wqkv[:, k, c * KC:(c + 1) * KC], rhs=gt[:, k, :],
                       start=k == 0, stop=k == 1)
            for k in range(2):
                mm(psum[:, 0, k * KC:(k + 1) * KC], lhsT=pw[:, k, :], rhs=ident[0:KC, 0:KC], start=True, stop=True)
            for k in range(2):
                mm(psum[:, 0, D:EXT], lhsT=pw[:, k, :], rhs=rc[:, k, :], start=k == 0, stop=k == 1)
            for k in range(2):
                mm(psum[:, 0, EXT:EXT + DB], lhsT=proj_dup[:, k, :], rhs=proj_in[:, k, :], start=k == 0, stop=k == 1)
            for k in range(2):
                mm(psum[:, 0, EXT + DB:EXT + P], lhsT=gt[:, k, :], rhs=gt[:, k, 0:DB], start=k == 0, stop=k == 1)
            for c in range(2):
                n = 3 * D // 2
                for k in range(2):
                    mm(psum[:, 4 + c, 0:n], lhsT=gt[:, k, :], rhs=wqkv[:, k, c * n:(c + 1) * n], start=k == 0, stop=k == 1)
            for c, n in ((0, KC), (1, KC + 1)):
                for kn in range(2):
                    ins = mm(psum[0:n, 2, c * NE:(c + 1) * NE], lhsT=wpt[:, kn, c * KC:c * KC + n], rhs=rc[:, kn, :],
                             start=kn == 0, stop=kn == 1)
            ins.then_inc(prep_pe, 1)
            pe.wait_ge(prep_v, 4)
            for n, where in ((2, 6), (3, 7), (0, 1), (1, 2)):
                ins = mm(psum[:, where, 0:HALF], lhsT=ft[:, n, :], rhs=bd.rearrange("p h m -> p (h m)"), start=True, stop=True)
            ins.then_inc(prep_pe, 1)

            def two_pass(dst, lhsT, name, c0, c1):
                mm(dst, lhsT=lhsT, rhs=f_hi[name][:, c0:c1], start=True, stop=False)
                return mm(dst, lhsT=lhsT, rhs=f_lo[name][:, c0:c1], start=False, stop=True)

            def basin_t(b, u):
                pe.wait_ge(split_r, b + 1)
                if not isinstance(b, int) or b >= 2:
                    pe.wait_ge(sev_r, b - 1)
                for j in range(TPB):
                    ins = nc.tensor.transpose(T[:, j * P:(j + 1) * P], split[u][:, j, :], ident)
                ins.then_inc(tr_r, 1)

            def embed(b, u, j):
                if j == 0:
                    pe.wait_ge(bt_r, b + 1)
                if not isinstance(b, int) or b + j:
                    pe.wait_ge(h0_r, b * TPB + j)
                two_pass(psum[:, 5, 0:EXT + P], bt[u][:, j * P:(j + 1) * P], "h", 0, EXT + P).then_inc(ph_r, 1)

            pe.wait_ge(prep_v, 5)
            pe.wait_ge(prep_hi, 2)
            basin_t(0, 0)
            for j in range(TPB):
                embed(0, 0, j)
            pe.wait_ge(prep_v, 6)

            def step_a(b, h, u):
                for j in range(TPB):
                    lhsT = bt[u][:, j * P:(j + 1) * P]
                    if not isinstance(b, int) or b * TPB + j >= 2:
                        pe.wait_ge(exp_r, b * TPB + (j - 1))
                    q = 2 * (j % 2)
                    two_pass(psum[:, q, 0:HALF], lhsT, "kd", 0, HALF)
                    two_pass(psum[:, q + 1, 0:HALF], lhsT, "kd", HALF, NF).then_inc(pd_r, 1)
                    if not isinstance(b, int) or b + j:
                        pe.wait_ge(kv_r, b * TPB + j)
                    two_pass(psum[:, 4, 0:2 * D], lhsT, "qkv", D, 3 * D).then_inc(pkv_r, 1)
                if has(b, 1):
                    basin_t(b + 1, 1 - u)
                pe.wait_ge(nmin_r, b + 1)
                if has(b, -1):
                    pe.wait_ge(sev_r, b)
                nc.tensor.transpose(PS[0:1, 0:P], nmin[:], ident).then_inc(nt_r, 1)
                if has(b, 1):
                    embed(b + 1, 1 - u, 0)
                pe.wait_ge(gmin_r, b + 1)
                mm(PS[:, P:P + 1], lhsT=ones[0:1, :], rhs=gmin[:], start=True, stop=True).then_inc(nbc_r, 1)
                if has(b, 1):
                    for j in range(1, TPB):
                        embed(b + 1, 1 - u, j)
                pe.wait_ge(vs_r, b + 1)
                mm(T[:, 0:D], lhsT=ones[:], rhs=vsum[:], start=True, stop=True)
                pe.wait_ge(vp_r, b + 1)
                for i in range(CH):
                    for j in range(TPB):
                        ins = mm(PS[:, i * HW * VC:(i + 1) * HW * VC], lhsT=ek[u][:, j, F0[i]:F0[i] + P],
                                 rhs=vp[u][:, j * H + W0[i]:j * H + W0[i] + HW, :].rearrange("p h c -> p (h c)"),
                                 start=i == 0 and j == 0, stop=i == CH - 1 and j == TPB - 1, skip_group_check=True)
                ins.then_inc(s_r, 1)

            steps_of(pe, NB, step_a)

            def x_t(b, u, n):
                pe.wait_ge(xsplit_r, b + 1)
                if not isinstance(n, int) or n:
                    pe.wait_ge(t_ev, n)
                for j in range(TPB):
                    ins = nc.tensor.transpose(T[:, j * P:(j + 1) * P], split[u][:, j, :], ident)
                ins.then_inc(tc_r, 1)

            def queries(b, u, j):
                lhsT = xt[u][:, j * P:(j + 1) * P]
                if not isinstance(b, int) or b + j:
                    pe.wait_ge(smax_r, b * TPB + j)
                two_pass(psum[:, 0, 0:HALF], lhsT, "qd", 0, HALF)
                two_pass(psum[:, 1, 0:HALF], lhsT, "qd", HALF, NF).then_inc(qd_r, 1)
                if j % 2 == 0:
                    if not isinstance(b, int) or b + j:
                        pe.wait_ge(qsq_r, b * 2 + j // 2)
                ins = two_pass(psum[:, 2, (j % 2) * D:(j % 2 + 1) * D], lhsT, "qkv", 0, D)
                if j % 2:
                    ins.then_inc(qq_r, 1)

            def shift_t(b, n):
                pe.wait_ge(sd_r, b + 1)
                pe.wait_ge(t_ev, n)
                for j in range(TPB):
                    ins = nc.tensor.transpose(T[0:2 * H, j * P:(j + 1) * P], sdh[:, j, :], ident)
                ins.then_inc(tc_r, 1)

            def features(b, u, i):
                if not isinstance(b, int) or b * CH + i >= 2:
                    pe.wait_ge(fe_r, b * CH + (i - 1))
                dst = bank(3 + (CH * u + i) % 2)
                mm(dst, lhsT=f_hi["qd"][:, F0[i]:F0[i] + P], rhs=xt[u], start=True, stop=False)
                mm(dst, lhsT=f_lo["qd"][:, F0[i]:F0[i] + P], rhs=xt[u], start=False, stop=False)
                mm(dst, lhsT=ind[:, i * P:(i + 1) * P], rhs=sdt, start=False, stop=True).then_inc(fm_r, 1)

            def attend(b, u, pair):
                if pair == 0:
                    pe.wait_ge(kvb_r, b + 1)
                    pe.wait_ge(eps_r, b * 3 + 3)
                if not isinstance(b, int) or b + pair:
                    pe.wait_ge(norm_r, b * 2 + pair)
                for jj in range(2):
                    j = 2 * pair + jj
                    for i in range(CH):
                        c0 = jj * H * VC + W0[i] * VC
                        ins = mm(psum[:, 5, c0:c0 + HW * VC], lhsT=eq[:, i, j * P:(j + 1) * P],
                                 rhs=kv[u][:, i * HW * VC:(i + 1) * HW * VC], start=jj == 0 and i == 0,
                                 stop=jj == 1 and i == CH - 1, skip_group_check=True)
                ins.then_inc(ek_r, 1)

            def attn_t(b, pair, n):
                pe.wait_ge(norm_r, b * 2 + (pair + 1))
                pe.wait_ge(t_ev, n)
                for jj in range(2):
                    for k in range(2):
                        ins = nc.tensor.transpose(T[0:KC, (jj * 2 + k) * P:(jj * 2 + k + 1) * P],
                                                  attn[pair][:, jj, k * KC:(k + 1) * KC], ident)
                ins.then_inc(tc_r, 1)

            def project(b, pair, n):
                pe.wait_ge(t_ev, n + 1)
                if not isinstance(b, int) or b + pair:
                    pe.wait_ge(h1_r, b * TPB + 2 * pair)
                for jj in range(2):
                    for k in range(2):
                        rows = KC + k
                        ins = mm(psum[:, 7, jj * EXT:(jj + 1) * EXT], lhsT=at[pair][0:rows, (jj * 2 + k) * P:(jj * 2 + k + 1) * P],
                                 rhs=wp[0:rows, k, :], start=jj == 0 and k == 0, stop=jj == 1 and k == 1, skip_group_check=True)
                ins.then_inc(pj_r, 1)

            def earlier(b, more):
                pe.wait_ge(cnt_r, b + 1)
                if more:
                    pe.wait_ge(qsq_r, b * 2 + 6)
                mm(prefix, lhsT=tri, rhs=cnt[:, TPB, :], start=True, stop=False)
                mm(prefix, lhsT=ones[:], rhs=carry[:], start=False, stop=True).then_inc(pref_r, 1)

            pe.wait_ge(sev_r, NB)
            x_t(0, 0, 0)
            pe.wait_ge(t_ev, 1)
            for j in range(TPB):
                queries(0, 0, j)
            shift_t(0, 1)
            pe.wait_ge(prep_v, 7)

            def step_b(b, h, u):
                more = has(b, 1)
                n = b * 4 + 2
                if more:
                    x_t(b + 1, 1 - u, n)
                else:
                    pe.wait_ge(t_ev, n)
                features(b, u, 0)
                features(b, u, 1)
                if more:
                    if has(b, -1):
                        pe.wait_ge(pref_used, b)
                    pe.wait_ge(t_ev, n + 1)
                for j in range(TPB):
                    if more:
                        queries(b + 1, 1 - u, j)
                    if j < 3:
                        features(b, u, j + 2)
                attend(b, u, 0)
                if has(b, -1):
                    earlier(b - 1, more)
                attend(b, u, 1)
                attn_t(b, 0, n + 1 if more else n)
                if more:
                    shift_t(b + 1, n + 2)
                project(b, 0, n + 1 if more else n)
                attn_t(b, 1, n + 3 if more else n + 1)
                project(b, 1, n + 3 if more else n + 1)

            steps_of(pe, NB, step_b)
            earlier(NB - 1, False)

            pe.wait_ge(carry_r, NB)
            mm(prefix, lhsT=ones[:], rhs=carry[:], start=True, stop=True).then_inc(tot_r, 1)

            def rows_t(t):
                pe.wait_ge(xn_r, t + 1)
                if not isinstance(t, int) or t:
                    pe.wait_ge(xe_r, t)
                for k in range(2):
                    ins = nc.tensor.transpose(T[0:KC, k * P:(k + 1) * P], xn[:, k * KC:(k + 1) * KC], ident)
                ins.then_inc(ct_r, 1)

            pe.wait_ge(w_late, 16 * (1 + NE + AFTER_B))
            pe.wait_ge(table_r, 1)
            rows_t(0)

            def step_c(t, h, u):
                e = pe.value_load(tile_expert[0:1, bass.ds(t, 1)], min_val=0, max_val=NE - 1)
                pe.wait_ge(wi_r, t + 1)
                pe.wait_ge(xe_r, t + 1)
                for f in range(DF // P):
                    for k in range(2):
                        ins = mm(psum[:, 3 + f // 4, f % 4 * P:(f % 4 + 1) * P],
                                 lhsT=wi_now[u][:, k, f * P:(f + 1) * P],
                                 rhs=xe[:, k, :], start=k == 0, stop=k == 1)
                    if f in (3, 5):
                        ins.then_inc(hid_r, 1)
                if has(t, 1, NT):
                    rows_t(t + 1)
                if has(t, -1, NT):
                    pe.wait_ge(o_r, t)
                for f in range(DF // P):
                    if f in (0, 4):
                        pe.wait_ge(relu_r, t * 2 + (1 + f // 4))
                        settle(pe)
                    ins = mm(PS[:, 0:D], lhsT=hid[:, f, :],
                             rhs=wo_all[:, bass.ds(e, 1), f, :].rearrange("p e n -> p (e n)"), start=f == 0, stop=f == DF // P - 1)
                ins.then_inc(y_r, 1)

            steps_of(pe, NT, step_c, cycle=ROT)


_INS = ["x", "L0_tok_basin_coords", "L0_tok_proj_w", "L0_tok_norm_w", "L0_attn_W_qkv", "L0_attn_W_proj",
        "L0_attn_b_proj", "L0_attn_proj_mat", "L0_ffn_router_w", "L0_ffn_wi", "L0_ffn_wo"]


def kernel(**inputs):
    import concourse.bacc as bacc
    from concourse.bass_utils import run_bass_kernel_spmd

    nc = bacc.Bacc("TRN2", target_bir_lowering=False, num_devices=1)
    arrays, args = {}, []
    for name in _INS:
        a = np.ascontiguousarray(inputs[name])
        arrays[f"in_{name}"] = a
        args.append(nc.dram_tensor(f"in_{name}", a.shape, mybir.dt.from_np(a.dtype), kind="ExternalInput").ap())
    c = constants()
    arrays["in_consts"] = c
    args.append(nc.dram_tensor("in_consts", c.shape, F32, kind="ExternalInput").ap())
    out = nc.dram_tensor("out", (NB, SEQ, D), F32, kind="ExternalOutput").ap()
    lm_tower(nc, *args, out)
    r = run_bass_kernel_spmd(nc, [arrays], core_ids=[0])
    return r.results[0]["out"]
```

```python
from contextlib import ExitStack

import numpy as np

import concourse.bass as bass
from concourse import mybir

F32, F32R = mybir.dt.float32, mybir.dt.float32r
I32, U32 = mybir.dt.int32, mybir.dt.uint32
ALU = mybir.AluOpType
ACT = mybir.ActivationFunctionType
AX = mybir.AxisListType

P = 128
NB, SEQ = 8, 512
TPB = SEQ // P
VOCAB, DB, D = 32000, 64, 192
H, HD, M = 12, 16, 44
NF = H * M
CH = 5
F0 = [0, 128, 256, 384, NF - P]
HW = 6
W0 = [0, 0, 4, 6, 6]
VC = HD + 1
NE, DF = 8, 768
TOK = NB * SEQ
SEG = TOK + P
NT = (TOK + NE * (P - 1)) // P
SPARE = NT - TOK // P
CNTS = TOK // P
KC = D // 2
EXT = D + NE
ROW = EXT + 4
R_MEAN, R_STD, R_GATE, R_ROW = EXT, EXT + 1, EXT + 2, EXT + 3
EPS_RMS, EPS_LN, EPS_FEAT = 1e-8, 1e-5, 1e-4
NORM = HD ** -0.25
FAR = float(1 << 20)
C_ID, C_TRI, C_IND = 0, P, 2 * P
C_MASK = C_IND + CH * P
C_HM = C_MASK + CH * HW
C_E8 = C_HM + HW
C_ROW = C_E8 + NE
C_PAD = C_ROW + NB * TPB
C_THR = C_PAD + NE
C_LE = C_THR + CNTS
C_T = C_LE + NE * NE
C_N = C_T + NT


def constants():
    c = np.zeros((P, C_N), np.float32)
    c[:, C_ID:C_ID + P] = np.eye(P)
    c[:, C_TRI:C_TRI + P] = np.triu(np.ones((P, P)), 1)
    for i in range(CH):
        for f in range(P):
            feat = F0[i] + f
            for part in range(2):
                c[part * H + feat // M, C_IND + i * P + f] = -1.0
            if i < CH - 1 or feat >= F0[3] + P:
                if 0 <= feat // M - W0[i] < HW:
                    c[f, C_MASK + i * HW + feat // M - W0[i]] = 1.0
    for p in range(KC):
        c[p, C_HM + p // HD] = 1.0
    c[:, C_E8:C_E8 + NE] = NE - np.arange(NE)
    p, b, j = np.meshgrid(np.arange(P), np.arange(NB), np.arange(TPB), indexing="ij")
    c[:, C_PAD:C_THR] = np.arange(NE) * SEG
    c[:, C_THR:C_LE] = np.arange(CNTS) * P
    c[:, C_LE:C_T] = np.tril(np.ones((NE, NE))).reshape(-1)
    c[:, C_T:C_N] = np.arange(NT)
    c[:, C_ROW:C_PAD] = (b * SEQ + p * TPB + j).reshape(P, -1)
    return c


def bc(ap, axis, n):
    a = ap.unsqueeze(axis)
    shape = list(a.shape)
    shape[axis] = n
    return a.to_broadcast(shape)


def lm_tower(nc, ids, coords, proj_w, norm_w, w_qkv, w_proj, b_proj, proj_mat, router_w, wi, wo, consts, out):
    with ExitStack() as ctx:
        def sb(name, shape, dt=F32):
            return ctx.enter_context(nc.sbuf_tensor(name, shape, dt))

        def sem(name):
            return ctx.enter_context(nc.semaphore(name))

        slots = nc.dram_tensor("slots", [NE * SEG + SPARE * P, ROW], F32).ap()
        out_rows = out.rearrange("b n d -> (b n) d")

        psum = ctx.enter_context(nc.psum_tensor("psum", [P, 8, 512], F32))

        n_wi, n_wo = 2 * DF, DF // P * D
        AT_ONCE, AFTER_B = 3, 3
        base = -(-nc.sbuf_base // 32) * 32
        w_all = sb("w_all", [P, NE * (n_wi + n_wo)])
        wi_all = w_all[0:KC, 0:NE * n_wi].rearrange("p (e k f) -> p e k f", e=NE, k=2)
        wo_all = w_all[:, NE * n_wi:NE * (n_wi + n_wo)].rearrange("p (e c n) -> p e c n", e=NE, n=D)
        taken = {"A": (AT_ONCE + AFTER_B) * n_wi, "B": AT_ONCE * n_wi}
        limit = {"A": NE * (n_wi + n_wo), "B": (AT_ONCE + AFTER_B) * n_wi}

        def early(name, shape, dt=F32, until="A"):
            a = taken[until]
            taken[until] += -(-int(np.prod(shape[1:])) // 8) * 8
            assert taken[until] <= limit[until]
            return nc.alloc_sbuf_tensor_at(name, shape, dt, offset=base + 4 * a)[:]

        cst = sb("cst", [P, C_N])
        ident = cst[:, C_ID:C_ID + P]
        tri = cst[:, C_TRI:C_TRI + P]
        mask = cst[:, C_MASK:C_MASK + CH * HW]
        e8 = cst[:, C_E8:C_E8 + NE]
        rows_of = cst[:, C_ROW:C_PAD].rearrange("p (b j) -> p b j", j=TPB)
        ones = sb("ones", [P, P])
        inv_d = sb("inv_d", [P, KC])
        neg_half = sb("neg_half", [P, 2 * TPB])
        ind = early("ind", [P, CH * P], F32R, "B")
        proj_in = sb("proj_in", [KC, 2, DB])
        proj_dup = early("proj_dup", [KC, 2, P])
        nw = sb("nw", [KC, 2])
        pw = early("pw", [KC, 2, P])
        gt = early("gt", [KC, 2, P])
        wqkv = early("wqkv", [KC, 2, 3 * D])
        rw = sb("rw", [KC, 2, NE])
        rc = sb("rc", [KC, 2, NE])
        pm = sb("pm", [M, HD])
        pm_rep = sb("pm_rep", [M, HW, HD])
        bd = early("bd", [KC, HW, M], F32, "B")
        ft = early("ft", [KC, 4, P])
        wp = sb("wp", [P, 2, EXT])
        wpt = early("wpt", [KC, 2, D + 1])
        f_hi = {}
        f_lo = {}
        for name, n in (("qd", NF), ("kd", NF), ("qkv", 3 * D), ("h", EXT + P)):
            for part, f in (("hi", f_hi), ("lo", f_lo)):
                until = {"kd": "A", "qd": "B"}
                f[name] = (early(f"f_{name}_{part}", [P, n], F32R, until[name]) if name in until
                           else sb(f"f_{name}_{part}", [P, n], F32R)[:])

        idx_i = sb("idx_i", [P, NB, TPB], I32)
        idx_f = sb("idx_f", [P, NB, TPB])
        idx_w = sb("idx_w", [P, NB, TPB])
        idx = sb("idx", [P, NB, TPB], U32)
        idx_b = [sb(f"idx_b{u}", [P, TPB], U32) for u in range(2)]
        basin = [sb(f"basin{u}", [P, TPB, DB]) for u in range(2)]
        basin_all = sb("basin_all", [P, NB, TPB, DB])
        split = [sb(f"split{u}", [P, TPB, 2 * DB]) for u in range(2)]
        bt = [early(f"bt{u}", [P, SEQ], F32R) for u in range(2)]
        quad = early("quad", [P, TPB, 2, DB])
        qs = sb("qs", [P, TPB, 2])
        pow_in = sb("pow_in", [P, 2 * TPB])
        scales = sb("scales", [P, NB, 2 * TPB])
        h0 = sb("h0", [P, NB, TPB, EXT])
        rmax = [sb(f"rmax{u}", [P, TPB]) for u in range(2)]
        nmax = [sb(f"nmax{u}", [P, TPB]) for u in range(2)]
        features_sb = sb("features_sb", [P, CH * SEQ])
        ek = [features_sb[:, 0:TPB * NF].rearrange("p (j f) -> p j f", j=TPB), early("ek1", [P, TPB, NF])]
        ksq = [early(f"ksq{u}", [P, TPB, D]) for u in range(2)]
        val = [early(f"val{u}", [P, TPB, D]) for u in range(2)]
        vsum2 = sb("vsum2", [P, 2, D])
        vsum = sb("vsum", [P, D])
        vp = [early(f"vp{u}", [P, TPB * H, VC]) for u in range(2)]
        nmin = sb("nmin", [P, 1])
        gmin = sb("gmin", [1, 1])
        nbatch = sb("nbatch", [P, NB])
        nb_now = sb("nb_now", [P, 1])
        rms2 = sb("rms2", [P, TPB])
        dmax = sb("dmax", [P, TPB])
        kq = sb("kq", [P, TPB * H])
        farg = sb("farg", [P, TPB * H])
        s_flat = sb("s_flat", [P, NB * CH * HW * VC])
        s_all = s_flat[:].rearrange("p (b c v) -> p b c v", b=NB, v=VC)
        ev_flat = sb("ev_flat", [P, NB * CH * HW * VC])
        ev_all = ev_flat[:].rearrange("p (b c v) -> p b c v", b=NB, v=VC)
        mask_eps = sb("mask_eps", [P, CH * HW])
        mask_den = sb("mask_den", [P, CH * HW])

        nglob = sb("nglob", [P, 1])
        dcb = sb("dcb", [P, NB])
        cb = sb("cb", [P, NB])
        xs = [sb(f"xs{u}", [P, TPB, DB]) for u in range(2)]
        xt = [early(f"xt{u}", [P, SEQ], F32R, "B") for u in range(2)]
        qsq = early("qsq", [P, TPB, D], F32, "B")
        qr = sb("qr", [P, TPB * H])
        smax = sb("smax", [P, TPB, H])
        sd = sb("sd", [P, TPB, H])
        sdh = sb("sdh", [P, TPB, 2 * H])
        sdt = early("sdt", [P, SEQ], F32R, "B")
        eq = features_sb[:, 0:CH * SEQ].rearrange("p (c n) -> p c n", c=CH)
        kv = [sb(f"kv{u}", [P, CH * HW * VC]) for u in range(2)]
        zr = sb("zr", [P, 2, 2 * H])
        attn = [sb(f"attn{u}", [P, 2, D]) for u in range(2)]
        at = [sb(f"at{u}", [P, 2 * 2 * P]) for u in range(2)]
        row = [sb(f"row{u}", [P, TPB, ROW]) for u in range(2)]
        bn = sb("bn", [P, TPB, 6])
        ve = sb("ve", [P, TPB])
        dlog = sb("dlog", [P, TPB, NE])
        dscl = sb("dscl", [P, TPB, NE])
        pexp = sb("pexp", [P, TPB, NE])
        psm = sb("psm", [P, TPB])
        lmax = sb("lmax", [P, TPB])
        m8 = sb("m8", [P, TPB, NE])
        mm8 = sb("mm8", [P, TPB])
        onehot = sb("onehot", [P, TPB, NE])
        cnt = sb("cnt", [P, TPB + 1, NE])
        carry = sb("carry", [P, NE])
        pos = sb("pos", [P, TPB, NE])
        rank = sb("rank", [P, TPB])
        sbase = sb("sbase", [P, TPB])
        slot = [sb(f"slot{u}", [P, TPB], U32) for u in range(2)]

        flat0, flat1 = (split[u][:].rearrange("p j d -> p (j d)")[0:1] for u in range(2))
        over = flat0[:, 0:NE * CNTS].rearrange("p (e k) -> p e k", e=NE)
        past = flat1[:, 0:NT * NE].rearrange("p (t e) -> p t e", e=NE)
        past_n = flat0[:, 0:NT * NE].rearrange("p (t e) -> p t e", e=NE)
        upto = xs[0][:].rearrange("p j d -> p (j d)")[0:1, 0:NE * NE].rearrange("p (e f) -> p e f", e=NE)
        tiles_of = sb("tiles_of", [1, NE])
        ends = sb("ends", [1, NE])
        t_exp = sb("t_exp", [1, NT])
        t_first = sb("t_first", [1, NT])
        t_within = sb("t_within", [1, NT])
        tile_slot = sb("tile_slot", [1, NT], I32)
        tile_expert = sb("tile_expert", [1, NT], I32)
        fill = sb("fill", [1, NE], I32)

        ROT = 3
        x_rows = [ev_flat[:, u * ROW:(u + 1) * ROW] for u in range(ROT)]
        orow = [ev_flat[:, ROT * ROW + u * D:ROT * ROW + (u + 1) * D] for u in range(ROT)]
        xn = ev_flat[:, ROT * (ROW + D):ROT * (ROW + D) + D]
        xe = ev_flat[0:KC, ROT * (ROW + D) + D:ROT * (ROW + D) + D + 2 * P].rearrange("p (k n) -> p k n", k=2)
        hid = s_flat[:, 0:DF].rearrange("p (f n) -> p f n", n=P)
        n2 = ROT * (ROW + D) + D + 2 * P
        wi_now = [m.rearrange("p (k f) -> p k f", k=2) for m in (
            s_flat[0:KC, DF:DF + n_wi], s_flat[0:KC, DF + n_wi:DF + 2 * n_wi], ev_flat[0:KC, n2:n2 + n_wi])]
        oidx = [sb(f"oidx{u}", [P, 1], U32) for u in range(ROT)]
        blank = sb("blank", [P, ROW])

        names = """w_in ids_in gathered0 gathered1 blank_out filled sent0 sent1 wi_in w_late x_in0 x_in1 x_in2 fin0 fin1 fin2
        pool_const prep_pe prep_hi prep_v steps idx_r idxb_r split_r tr_r bt_r ph_r h0_r quad_r pow_in_r scale_r kept
        pd_r pkv_r nmax_r exp_r kv_r nmin_r nt_r gmin_r nbc_r nb_r farg_r f_r vs_half vs_r vsm_r ev_r vp_r s_r s_free
        dcb_r cb_r kvb_r xs_r xsplit_r tc_r t_ev qd_r qq_r smax_r qsq_r sd_r fm_r fe_r eps_r
        ek_r norm_r pj_r h1_r ve_r std_r cnt_r pref_r pref_used dscl_r pexp_r slot_r sent_r fin_r
        carry_r tot_r fill_r table_r wi_a wi_v xn_r ct_r xe_r hid_r relu_r y_r o_r oidx_r settled""".split()
        S = {n: sem(n) for n in names}
        (w_in, ids_in, gathered0, gathered1, blank_out, filled, sent0, sent1, wi_in, w_late, x_in0, x_in1, x_in2, fin0, fin1, fin2,
         pool_const, prep_pe, prep_hi, prep_v, steps, idx_r, idxb_r, split_r, tr_r, bt_r, ph_r, h0_r, quad_r, pow_in_r, scale_r, kept,
         pd_r, pkv_r, nmax_r, exp_r, kv_r, nmin_r, nt_r, gmin_r, nbc_r, nb_r, farg_r, f_r, vs_half, vs_r, vsm_r, ev_r, vp_r, s_r, s_free,
         dcb_r, cb_r, kvb_r, xs_r, xsplit_r, tc_r, t_ev, qd_r, qq_r, smax_r, qsq_r, sd_r, fm_r, fe_r, eps_r,
         ek_r, norm_r, pj_r, h1_r, ve_r, std_r, cnt_r, pref_r, pref_used, dscl_r, pexp_r, slot_r, sent_r, fin_r,
         carry_r, tot_r, fill_r, table_r, wi_a, wi_v, xn_r, ct_r, xe_r, hid_r, relu_r, y_r, o_r, oidx_r, settled) = S.values()
        gathered, sent = (gathered0, gathered1), (sent0, sent1)
        x_in, fin = (x_in0, x_in1, x_in2), (fin0, fin1, fin2)

        block = ctx.enter_context(nc.Block())

        def steps_of(eng, n, body, ahead=1, cycle=2):
            body(0, 0, 0)
            rounds = (n - 1 - ahead) // cycle
            with eng.Fori(0, rounds) as i:
                for m in range(1, cycle + 1):
                    body(i * cycle + m, i + m // cycle, m % cycle)
            for k in range(1 + cycle * rounds, n):
                body(k, k // cycle, k % cycle)

        def settle(eng):
            eng.sem_inc(settled, 1)

        def first_t(b):
            return 3 + b * 4 if has(b, 1) else 2 + b * 4

        def has(k, n, steps=NB):
            return not isinstance(k, int) or 0 <= k + n < steps

        def bank(k, n=512):
            return psum[:, k, 0:n]

        T, PS = bank(6), bank(7)
        prefix = psum[:, 7, 2 * EXT:2 * EXT + NE]
        MX = psum[:, 4, 2 * D:512]
        HALF = NF // 2

        @block.sync
        def _(sp):
            with nc.allow_non_contiguous_dma(reason="runs of 4 ids, and 192 norm weights"):
                sp.dma_start(idx_i[:], ids.rearrange("b (p j) -> p b j", j=TPB)).then_inc(ids_in, 16)
                sp.dma_start(nw[:], norm_w.rearrange("(k p) -> p k", p=KC)).then_inc(w_in, 16)
            sp.dma_start(cst[:], consts).then_inc(w_in, 16)
            sp.dma_start(proj_in[:], proj_w.rearrange("(k p) d -> p k d", p=KC)).then_inc(w_in, 16)
            sp.dma_start(rw[:], router_w.rearrange("(k p) e -> p k e", p=KC)).then_inc(w_in, 16)
            sp.dma_start(pm[:], proj_mat).then_inc(w_in, 16)
            sp.dma_start(wqkv, w_qkv.rearrange("(k p) n -> p k n", p=KC)).then_inc(w_in, 16)
            sp.dma_start(wp[0:KC, :, 0:D], w_proj.rearrange("(k p) n -> p k n", p=KC)).then_inc(w_in, 16)
            sp.dma_start(wp[KC:KC + 1, 1, 0:D], b_proj.rearrange("(a n) -> a n", a=1)).then_inc(w_in, 16)
            sp.wait_ge(pool_const, 2)
            sp.dma_start(slots[NE * SEG:, :].rearrange("(t p) r -> p t r", p=P), bc(blank[:, :], 1, SPARE)).then_inc(blank_out, 16)
            sp.dma_start(wi_all[:, 0:AT_ONCE], wi[0:AT_ONCE].rearrange("e (k p) f -> p e k f", p=KC)).then_inc(wi_in, 16)
            sp.wait_ge(s_free, NB + 1)
            sp.wait_ge(kept, NB)
            sp.dma_start(wi_all[:, AT_ONCE + AFTER_B:NE], wi[AT_ONCE + AFTER_B:NE].rearrange("e (k p) f -> p e k f", p=KC)).then_inc(w_late, 16)
            for e in range(NE):
                sp.dma_start(wo_all[:, e], wo[e].rearrange("(c p) n -> p c n", p=P)).then_inc(w_late, 16)
            sp.wait_ge(fm_r, NB * CH)
            for e in range(AT_ONCE, AT_ONCE + AFTER_B):
                sp.dma_start(wi_all[:, e], wi[e].rearrange("(k p) f -> p k f", p=KC)).then_inc(w_late, 16)

            def load_rows(t, u):
                first = sp.value_load(tile_slot[0:1, bass.ds(t, 1)], min_val=0, max_val=NE * SEG + (SPARE - 1) * P)
                sp.dma_start(x_rows[u], slots[bass.ds(first, P), :]).then_inc(x_in[u], 16)

            sp.wait_ge(fill_r, 1)
            for e in range(NE):
                first = sp.value_load(fill[0:1, e:e + 1], min_val=0, max_val=(NE - 1) * SEG + TOK)
                sp.dma_start(slots[bass.ds(first, P), :], blank[:, :]).then_inc(filled, 16)
            sp.wait_ge(blank_out, 16)
            sp.wait_ge(table_r, 2)
            for u in range(2):
                sp.wait_ge(sent[u], 16 * TPB * NB // 2)
            sp.wait_ge(filled, 16 * NE)
            load_rows(0, 0)
            load_rows(1, 1)

            def ahead_rows(t, h, u):
                if has(t, 2, NT):
                    if has(t, -1):
                        sp.wait_ge(o_r, t)
                        settle(sp)
                    load_rows(t + 2, (u + 2) % ROT)

            steps_of(sp, NT, ahead_rows, ahead=2, cycle=ROT)
            for u in range(ROT):
                sp.wait_ge(fin[u], 16 * len(range(u, NT, ROT)))

        @block.gpsimd
        def _(pool):
            g = nc.gpsimd
            g.memset(blank[:, 0:R_ROW], 0.0).then_inc(pool_const, 1)
            g.memset(blank[:, R_ROW:ROW], FAR).then_inc(pool_const, 1)
            g.memset(ones[:], 1.0).then_inc(pool_const, 1)
            g.memset(inv_d[:], 1.0 / D).then_inc(pool_const, 1)
            g.memset(neg_half[:], -0.5).then_inc(pool_const, 1)
            g.memset(at[0][:], 1.0).then_inc(pool_const, 1)
            g.memset(at[1][:], 1.0).then_inc(pool_const, 1)
            g.memset(carry[:], 0.0).then_inc(pool_const, 1)
            g.memset(cnt[:], 0.0).then_inc(pool_const, 1)
            pool.sem_inc(sent_r, 1)
            pool.sem_inc(fin_r, ROT - 1)

            def gather(b, u):
                g.tensor_copy(idx_b[u][:], idx[:, b, :]).then_inc(idxb_r, 1)
                pool.wait_ge(idxb_r, b + 1)
                settle(pool)
                for j in range(TPB):
                    g.indirect_dma_start(
                        out=basin[u][:, j, :], out_offset=None, in_=coords,
                        in_offset=bass.IndirectOffsetOnAxis(ap=idx_b[u][:, j:j + 1], axis=0),
                    ).then_inc(gathered[u], 16)

            def power(b):
                pool.wait_ge(pow_in_r, b + 1)
                g.tensor_tensor(scales[:, b, :], pow_in[:], neg_half[:], ALU.pow).then_inc(scale_r, 1)

            pool.wait_ge(idx_r, 1)
            gather(0, 0)
            gather(1, 1)
            power(0)

            def next_rows(b, u):
                pool.wait_ge(quad_r, (b - 1) * TPB)
                pool.wait_ge(kept, b - 1)
                gather(b, u)

            next_rows(2, 0)
            pool.wait_ge(prep_v, 1)
            g.tensor_copy(ev_all[:, :, :, HD], bc(mask_den[:], 1, NB)).then_inc(pool_const, 1)

            def values(b, u):
                pool.wait_ge(kv_r, b * TPB + TPB)
                g.tensor_tensor(vsum2[:], val[u][:, 0:2, :], val[u][:, 2:4, :], ALU.add).then_inc(vs_half, 1)
                pool.wait_ge(vs_half, b + 1)
                g.tensor_tensor(vsum[:], vsum2[:, 0, :], vsum2[:, 1, :], ALU.add).then_inc(vs_r, 1)
                pool.wait_ge(f_r, b + 1)
                g.tensor_tensor(vp[u][:, :, 0:HD], val[u].rearrange("p j (h d) -> p (j h) d", d=HD),
                                bc(vp[u][:, :, HD], 2, HD), ALU.mult).then_inc(vp_r, 1)

            def step_a(b, h, u):
                if has(b, -1):
                    values(b - 1, 1 - u)
                if has(b, 1):
                    power(b + 1)
                if has(b, 3):
                    next_rows(b + 3, 1 - u)

            steps_of(pool, NB, step_a, ahead=3)
            values(NB - 1, (NB - 1) % 2)

            def scaled(b, u):
                if not isinstance(b, int) or b >= 2:
                    pool.wait_ge(xsplit_r, b - 1)
                g.tensor_tensor(xs[u][:], basin_all[:, b, :, :], bc(scales[:, b, TPB:2 * TPB], 2, DB), ALU.mult
                                ).then_inc(xs_r, 1)

            def send(b, u):
                pool.wait_ge(std_r, b * 2 + 2)
                pool.wait_ge(slot_r, b + 1)
                settle(pool)
                for j in range(TPB):
                    g.indirect_dma_start(
                        out=slots, out_offset=bass.IndirectOffsetOnAxis(ap=slot[u][:, j:j + 1], axis=0),
                        in_=row[u][:, j, :], in_offset=None, bounds_check=NE * SEG - 1, oob_is_err=False,
                    ).then_inc(sent[u], 16)

            pool.wait_ge(kept, NB)
            pool.wait_ge(scale_r, NB)
            scaled(0, 0)
            scaled(1, 1)

            def row_tail(b, u):
                pool.wait_ge(ve_r, b + 1)
                g.tensor_tensor(row[u][:, :, R_STD], ve[:], neg_half[:, 0:TPB], ALU.pow).then_inc(std_r, 1)
                g.tensor_copy(row[u][:, :, R_ROW], rows_of[:, b, :]).then_inc(std_r, 1)

            def step_b(b, h, u):
                for n, (lo, hi) in enumerate(((0, 2), (2, 4), (4, 5))):
                    pool.wait_ge(fe_r, b * CH + hi)
                    settle(pool)
                    g.tensor_scalar(eq[:, lo:hi, :], eq[:, lo:hi, :], EPS_FEAT, 1.0, ALU.add, ALU.mult).then_inc(eps_r, 1)
                    if n == 0 and has(b, -1):
                        row_tail(b - 1, 1 - u)
                    if n == 1 and has(b, 2):
                        scaled(b + 2, u)
                if has(b, -1):
                    send(b - 1, 1 - u)
                    pool.wait_ge(sent[1 - u], (h + u) * (16 * TPB))
                    pool.sem_inc(sent_r, 1)

            steps_of(pool, NB, step_b, ahead=2)
            row_tail(NB - 1, (NB - 1) % 2)
            send(NB - 1, (NB - 1) % 2)

            def step_c(t, h, u):
                if has(t, -1, NT):
                    pool.wait_ge(fin[(u - 1) % ROT], (h + (1 if u else 0)) * 16)
                    pool.sem_inc(fin_r, 1)
                pool.wait_ge(oidx_r, t + 1)
                pool.wait_ge(o_r, t + 1)
                settle(pool)
                g.indirect_dma_start(
                    out=out_rows, out_offset=bass.IndirectOffsetOnAxis(ap=oidx[u][:, 0:1], axis=0),
                    in_=orow[u], in_offset=None, bounds_check=TOK - 1, oob_is_err=False,
                ).then_inc(fin[u], 16)

            steps_of(pool, NT, step_c, cycle=ROT)

        @block.scalar
        def _(act):
            a = nc.scalar
            act.wait_ge(prep_pe, 2)
            a.activation(f_hi["h"][:, 0:EXT], psum[:, 0, 0:EXT], ACT.Copy).then_inc(prep_hi, 1)
            a.activation(f_hi["h"][:, EXT:EXT + P], psum[:, 0, EXT:EXT + P], ACT.Copy, scale=1.0 / D).then_inc(prep_hi, 1)
            a.activation(f_hi["qkv"].rearrange("p (a n) -> p a n", a=2), psum[:, 4:6, 0:3 * D // 2],
                         ACT.Copy).then_inc(prep_hi, 1)
            act.wait_ge(prep_pe, 3)
            a.activation(f_hi["kd"].rearrange("p (a n) -> p a n", a=2), psum[:, 6:8, 0:HALF], ACT.Copy).then_inc(prep_hi, 1)
            a.activation(f_hi["qd"].rearrange("p (a n) -> p a n", a=2), psum[:, 1:3, 0:HALF], ACT.Copy).then_inc(prep_hi, 1)

            def basin_t(b, u):
                act.wait_ge(tr_r, b + 1)
                a.activation(bt[u], T, ACT.Copy).then_inc(bt_r, 1)

            def keep_h0(b, j):
                act.wait_ge(quad_r, b * TPB + (j + 1))
                settle(act)
                a.activation(h0[:, b, j, :], psum[:, 5, 0:EXT], ACT.Copy).then_inc(h0_r, 1)

            def keep(b, h, u):
                act.wait_ge(gathered[u], (h + 1) * (16 * TPB))
                settle(act)
                a.activation(basin_all[:, b, :, :], basin[u][:], ACT.Copy).then_inc(kept, 1)

            def factors(b, u):
                act.wait_ge(farg_r, b + 1)
                a.activation(vp[u][:, :, HD], farg[:], ACT.Exp).then_inc(f_r, 1)

            basin_t(0, 0)
            keep(0, 0, 0)
            for j in range(TPB):
                keep_h0(0, j)
            basin_t(1, 1)
            keep(1, 0, 1)

            def step_a(b, h, u):
                for j in range(TPB):
                    act.wait_ge(nmax_r, b * TPB + (j + 1))
                    settle(act)
                    q = 2 * (j % 2)
                    sc = scales[:, b, TPB + j:TPB + j + 1]
                    a.activation(ek[u][:, j, :].rearrange("p (a n) -> p a n", a=2), psum[:, q:q + 2, 0:HALF],
                                 ACT.Exp, bias=nmax[u][:, j:j + 1], scale=sc).then_inc(exp_r, 1)
                    act.wait_ge(pkv_r, b * TPB + (j + 1))
                    settle(act)
                    a.activation(ksq[u][:, j, :], psum[:, 4, 0:D], ACT.Square, scale=sc)
                    a.activation(val[u][:, j, :], psum[:, 4, D:2 * D], ACT.Copy, scale=sc).then_inc(kv_r, 1)
                    if has(b, 1):
                        keep_h0(b + 1, j)
                    if j == 1 and has(b, -1):
                        factors(b - 1, 1 - u)
                if has(b, 2):
                    keep(b + 2, h + 1, u)
                    basin_t(b + 2, u)

            steps_of(act, NB, step_a, ahead=2)
            factors(NB - 1, (NB - 1) % 2)

            act.wait_ge(dcb_r, 1)
            a.activation(cb[:], dcb[:], ACT.Exp).then_inc(cb_r, 1)

            def evacuate(n, dst, src):
                act.wait_ge(tc_r, n + 1)
                a.activation(dst, src, ACT.Copy).then_inc(t_ev, 1)

            def q_squares(b, pair):
                act.wait_ge(qq_r, b * 2 + (pair + 1))
                a.activation(qsq[:, 2 * pair:2 * pair + 2, :], psum[:, 2, 0:2 * D], ACT.Square).then_inc(qsq_r, 1)

            T3, T4 = bank(3), bank(4)
            evacuate(0, xt[0], T)
            q_squares(0, 0)
            q_squares(0, 1)
            evacuate(1, sdt[0:2 * H, :], T3[0:2 * H, :])
            evacuate(2, xt[1], T)

            def step_b(b, h, u):
                more = has(b, 1)
                n = first_t(b)
                for i in range(CH):
                    act.wait_ge(fm_r, b * CH + (i + 1))
                    a.activation(eq[:, i, :], bank(3 + (CH * u + i) % 2), ACT.Exp).then_inc(fe_r, 1)
                    if more and i == 3:
                        q_squares(b + 1, 0)
                if more:
                    q_squares(b + 1, 1)
                if has(b, -1):
                    act.wait_ge(dscl_r, b)
                    a.activation(pexp[:], dscl[:], ACT.Exp).then_inc(pexp_r, 1)
                evacuate(n, at[0][0:KC, :], T[0:KC, :])
                if more:
                    evacuate(n + 1, sdt[0:2 * H, :], T3[0:2 * H, :])
                evacuate(n + 2 if more else n + 1, at[1][0:KC, :], T4[0:KC, :])
                if has(b, 2):
                    evacuate(n + 3, xt[u], T)

            steps_of(act, NB, step_b, ahead=2)
            act.wait_ge(dscl_r, NB)
            a.activation(pexp[:], dscl[:], ACT.Exp).then_inc(pexp_r, 1)

            def x_t(t):
                act.wait_ge(ct_r, t + 1)
                a.activation(xe.rearrange("p k n -> p (k n)"), T[0:KC, 0:2 * P], ACT.Copy).then_inc(xe_r, 1)

            def fetch(t, u):
                e = act.value_load(tile_expert[0:1, bass.ds(t, 1)], min_val=0, max_val=NE - 1)
                settle(act)
                a.activation(wi_now[u][:, 0, :], wi_all[:, bass.ds(e, 1), 0, :].rearrange("p e f -> p (e f)"),
                             ACT.Copy).then_inc(wi_a, 1)

            act.wait_ge(wi_in, 16)
            act.wait_ge(w_late, 16 * (1 + NE + AFTER_B))
            act.wait_ge(table_r, 1)
            fetch(0, 0)
            fetch(1, 1)
            x_t(0)

            def step_c(t, h, u):
                act.wait_ge(hid_r, t * 2 + 1)
                a.activation(hid[:, 0:4, :].rearrange("p f n -> p (f n)"), bank(3), ACT.Relu).then_inc(relu_r, 1)
                act.wait_ge(hid_r, t * 2 + 2)
                a.activation(hid[:, 4:6, :].rearrange("p f n -> p (f n)"), bank(4, 2 * P), ACT.Relu).then_inc(relu_r, 1)
                if has(t, 1, NT):
                    x_t(t + 1)
                if has(t, 2, NT):
                    fetch(t + 2, (u + 2) % ROT)

            steps_of(act, NT, step_c, ahead=2, cycle=ROT)

        @block.vector
        def _(dve):
            v = nc.vector
            base = [0]
            done = [0]

            def link(ins):
                done[0] += 1
                ins.then_inc(steps, 1)
                dve.wait_ge(steps, base[0] + done[0])

            dve.wait_ge(ids_in, 16)
            link(v.tensor_copy(idx_f[:], idx_i[:]))
            link(v.tensor_scalar(idx_w[:], idx_f[:], 0.0, float(VOCAB), ALU.is_lt, ALU.mult))
            link(v.tensor_tensor(idx_w[:], idx_w[:], idx_f[:], ALU.add))
            v.tensor_scalar(idx[:], idx_w[:], 0.0, float(VOCAB - 1), ALU.max, ALU.min).then_inc(idx_r, 1)

            dve.wait_ge(w_in, 16 * 8)
            v.tensor_scalar(mask_den[:], mask, EPS_FEAT * SEQ, None, ALU.mult)
            v.tensor_scalar(mask_eps[:], mask, EPS_FEAT, None, ALU.mult).then_inc(prep_v, 1)
            v.tensor_copy(ind, cst[:, C_IND:C_IND + CH * P])
            for k in range(2):
                v.tensor_scalar(pw[:, k, :].rearrange("p (a d) -> p a d", a=2), bc(proj_in[:, k, :], 1, 2), nw[:, k:k + 1], None,
                                ALU.mult)
                v.tensor_copy(proj_dup[:, k, :].rearrange("p (a d) -> p a d", a=2), bc(proj_in[:, k, :], 1, 2))
            v.tensor_copy(pm_rep[:], bc(pm[:], 1, HW)).then_inc(prep_v, 1)
            dve.wait_ge(prep_pe, 1)
            v.tensor_tensor(gt.rearrange("p k (a d) -> p k a d", a=2).rearrange("p k a d -> p (k a) d"),
                            pw.rearrange("p k (a d) -> p (k a) d", a=2), bc(psum[0:KC, 0, 0:DB], 1, 4), ALU.subtract)
            v.tensor_tensor(rc[:], rw[:], bc(psum[0:KC, 0, DB:DB + NE], 1, 2), ALU.subtract)
            v.scalar_tensor_tensor(out=bd, in0=bc(psum[0:KC, 2, 0:M], 1, HW), scalar=NORM,
                                   in1=bc(cst[0:KC, C_HM:C_HM + HW], 2, M), op0=ALU.mult, op1=ALU.mult)
            v.tensor_copy(wpt, psum[0:KC, 3, 0:2 * (D + 1)].rearrange("p (k n) -> p k n", k=2)).then_inc(prep_v, 1)
            dve.wait_ge(prep_pe, 2)
            v.tensor_copy(wp[0:KC, 0, D:EXT], psum[0:KC, 2, 0:NE])
            v.tensor_copy(wp[0:KC + 1, 1, D:EXT], psum[0:KC + 1, 2, NE:2 * NE])
            v.tensor_copy(ft.rearrange("p c n -> p (c n)"), psum[0:KC, 1, :]).then_inc(prep_v, 1)
            dve.wait_ge(prep_hi, 2)
            v.tensor_tensor(f_lo["h"][:, 0:EXT], psum[:, 0, 0:EXT], f_hi["h"][:, 0:EXT].bitcast(F32), ALU.subtract)
            v.scalar_tensor_tensor(out=f_lo["h"][:, EXT:EXT + P], in0=psum[:, 0, EXT:EXT + P], scalar=1.0 / D,
                                   in1=f_hi["h"][:, EXT:EXT + P].bitcast(F32), op0=ALU.mult, op1=ALU.subtract
                                   ).then_inc(prep_v, 1)
            dve.wait_ge(prep_hi, 3)
            v.tensor_tensor(f_lo["qkv"].rearrange("p (a n) -> p a n", a=2), psum[:, 4:6, 0:3 * D // 2],
                            f_hi["qkv"].bitcast(F32).rearrange("p (a n) -> p a n", a=2), ALU.subtract)
            dve.wait_ge(prep_hi, 4)
            v.tensor_tensor(f_lo["kd"].rearrange("p (a n) -> p a n", a=2), psum[:, 6:8, 0:HALF],
                            f_hi["kd"].bitcast(F32).rearrange("p (a n) -> p a n", a=2), ALU.subtract)
            dve.wait_ge(prep_hi, 5)
            v.tensor_tensor(f_lo["qd"].rearrange("p (a n) -> p a n", a=2), psum[:, 1:3, 0:HALF],
                            f_hi["qd"].bitcast(F32).rearrange("p (a n) -> p a n", a=2), ALU.subtract).then_inc(prep_v, 1)

            def split_into(dst, src, signal):
                link(v.tensor_copy(dst[:, :, 0:DB].bitcast(F32R), src))
                v.tensor_tensor(dst[:, :, DB:2 * DB], src, dst[:, :, 0:DB], ALU.subtract).then_inc(signal, 1)

            def split_basin(b, h, u):
                dve.wait_ge(gathered[u], (h + 1) * (16 * TPB))
                if not isinstance(b, int) or b >= 2:
                    dve.wait_ge(tr_r, b - 1)
                split_into(split[u], basin[u][:], split_r)

            def quads(b, u, j):
                dve.wait_ge(ph_r, b * TPB + (j + 1))
                v.tensor_tensor(quad[:, j, :, :], psum[:, 5, EXT:EXT + P].rearrange("p (a d) -> p a d", a=2),
                                bc(basin[u][:, j, :], 1, 2), ALU.mult).then_inc(quad_r, 1)

            def stats(b):
                dve.wait_ge(quad_r, b * TPB + TPB)
                link(v.tensor_reduce(qs[:].rearrange("p j a -> p (j a)"), quad.rearrange("p j a d -> p (j a) d"),
                                     AX.X, ALU.add))
                link(v.tensor_scalar(rms2[:], qs[:, :, 0], EPS_RMS, None, ALU.add))
                v.tensor_copy(pow_in[:, 0:TPB], rms2[:])
                v.scalar_tensor_tensor(out=pow_in[:, TPB:2 * TPB], in0=rms2[:], scalar=EPS_LN, in1=qs[:, :, 1],
                                       op0=ALU.mult, op1=ALU.add).then_inc(pow_in_r, 1)

            def first():
                split_basin(0, 0, 0)
                for j in range(TPB):
                    quads(0, 0, j)
                stats(0)

            first()
            before = [None]

            def begin(b, start, first, each):
                if isinstance(b, int) and b == 0:
                    base[0] = start
                elif isinstance(b, int) and before[0] == b - 1:
                    base[0] += done[0]
                else:
                    base[0] = (b - 1) * each + (start + first)
                done[0] = 0
                before[0] = b if isinstance(b, int) else None

            def end(b, first, each):
                if isinstance(b, int) and b == 0:
                    assert done[0] == first, done
                elif not isinstance(b, int):
                    assert done[0] == each, done

            def keep_s(b):
                dve.wait_ge(s_r, b + 1)
                v.tensor_tensor(s_all[:, b, :, :], PS[:, 0:CH * HW * VC].rearrange("p (c v) -> p c v", v=VC),
                                bc(mask, 2, VC), ALU.mult).then_inc(s_free, 1)

            def keep_ev(b):
                dve.wait_ge(vsm_r, b + 1)
                for i0, i1 in ((0, 2), (2, 3), (3, 5)):
                    w = W0[i0]
                    src = T[:, w * HD:(w + HW) * HD].rearrange("p (h d) -> p h d", d=HD)
                    ins = v.tensor_tensor(
                        ev_all[:, b, i0 * HW:i1 * HW, 0:HD].rearrange("p (i h) d -> p i h d", h=HW), bc(src, 1, i1 - i0),
                        bc(mask_eps[:, i0 * HW:i1 * HW].rearrange("p (i h) -> p i h", h=HW), 3, HD), ALU.mult)
                ins.then_inc(ev_r, 1)

            def batch_max(b):
                dve.wait_ge(nt_r, b + 1)
                v.tensor_reduce(gmin[:], MX[0:1, 0:P], AX.X, ALU.min).then_inc(gmin_r, 1)

            def factor_arg(b, u):
                dve.wait_ge(kv_r, b * TPB + TPB)
                link(v.tensor_reduce(kq[:], ksq[u].rearrange("p j (h d) -> p (j h) d", d=HD), AX.X, ALU.add))
                v.scalar_tensor_tensor(out=farg[:].rearrange("p (j h) -> p j h", h=H), in0=kq[:].rearrange("p (j h) -> p j h", h=H),
                                       scalar=-0.5 * NORM * NORM, in1=bc(dmax[:], 2, H), op0=ALU.mult, op1=ALU.add
                                       ).then_inc(farg_r, 1)

            def take_max(b, u):
                dve.wait_ge(nbc_r, b + 1)
                link(v.tensor_copy(nb_now[:], MX[:, 0:1]))
                v.tensor_copy(nbatch[:, bass.ds(b, 1)], nb_now[:]).then_inc(nb_r, 1)
                v.tensor_scalar(dmax[:], nmax[u][:], -1.0, nb_now[:], ALU.mult, ALU.add)

            split_basin(1, 0, 1)
            start_a = done[0]
            v.sem_inc(s_free, 1)

            def step_a(b, h, u):
                begin(b, start_a, LINKS_A0, LINKS_A)
                for j in range(TPB):
                    dve.wait_ge(pd_r, b * TPB + (j + 1))
                    q = 2 * (j % 2)
                    link(v.tensor_reduce(rmax[u][:, j:j + 1], psum[:, q:q + 2, 0:HALF], AX.XY, ALU.max))
                    if j == 0:
                        dve.wait_ge(scale_r, b + 1)
                    v.tensor_scalar(nmax[u][:, j:j + 1], rmax[u][:, j:j + 1], scales[:, b, TPB + j:TPB + j + 1], -1.0,
                                    ALU.mult, ALU.mult).then_inc(nmax_r, 1)
                    if j == 0 and has(b, -1):
                        take_max(b - 1, 1 - u)
                    if has(b, 1):
                        quads(b + 1, 1 - u, j)
                    if j == 0 and has(b, -1):
                        factor_arg(b - 1, 1 - u)
                    if j == 2 and has(b, -1):
                        keep_ev(b - 1)
                dve.wait_ge(nmax_r, b * TPB + TPB)
                v.tensor_reduce(nmin[:], nmax[u][:], AX.X, ALU.min).then_inc(nmin_r, 1)
                if has(b, 1):
                    stats(b + 1)
                if has(b, 2):
                    split_basin(b + 2, h + 1, u)
                batch_max(b)
                if has(b, -1):
                    keep_s(b - 1)
                end(b, LINKS_A0, LINKS_A)

            LINKS_A0 = TPB + 2 + 1
            LINKS_A = LINKS_A0 + 2
            steps_of(dve, NB, step_a, ahead=2)
            take_max(NB - 1, (NB - 1) % 2)
            factor_arg(NB - 1, (NB - 1) % 2)
            keep_ev(NB - 1)
            keep_s(NB - 1)

            link(v.tensor_reduce(nglob[:], nbatch[:], AX.X, ALU.min))
            v.tensor_scalar(dcb[:], nbatch[:], -1.0, nglob[:], ALU.mult, ALU.add).then_inc(dcb_r, 1)

            def split_x(b, u):
                dve.wait_ge(xs_r, b + 1)
                split_into(split[u], xs[u][:], xsplit_r)

            def q_max(b, j):
                dve.wait_ge(qd_r, b * TPB + (j + 1))
                for q in range(2):
                    ins = v.tensor_reduce(smax[:, j, q * HW:(q + 1) * HW], psum[:, q, 0:HALF].rearrange("p (h m) -> p h m", m=M),
                                          AX.X, ALU.max)
                ins.then_inc(smax_r, 1)

            def q_shift(b):
                dve.wait_ge(qsq_r, b * 2 + 2)
                link(v.tensor_reduce(qr[:], qsq.rearrange("p j (h d) -> p (j h) d", d=HD), AX.X, ALU.add))
                link(v.scalar_tensor_tensor(out=sd[:].rearrange("p j h -> p (j h)"), in0=qr[:], scalar=0.5 * NORM * NORM,
                                            in1=smax[:].rearrange("p j h -> p (j h)"), op0=ALU.mult, op1=ALU.add))
                link(v.tensor_copy(sdh[:, :, 0:H].bitcast(F32R), sd[:]))
                v.tensor_tensor(sdh[:, :, H:2 * H], sd[:], sdh[:, :, 0:H], ALU.subtract).then_inc(sd_r, 1)

            dve.wait_ge(pool_const, 9)
            v.tensor_copy(sdt.rearrange("p (j n) -> p j n", n=P), bc(blank[:, 0:P], 1, TPB)).then_inc(prep_v, 1)
            split_x(0, 0)
            for j in range(TPB):
                q_max(0, j)
            q_shift(0)
            split_x(1, 1)
            dve.wait_ge(cb_r, 1)

            def total_state(b, u):
                v.scalar_tensor_tensor(out=kv[u][:], in0=s_all[:, b, :, :].rearrange("p c v -> p (c v)"), scalar=cb[:, bass.ds(b, 1)],
                                       in1=ev_all[:, b, :, :].rearrange("p c v -> p (c v)"), op0=ALU.mult, op1=ALU.add
                                       ).then_inc(kvb_r, 1)

            def pick(b, u):
                v.tensor_scalar(ve[:], row[u][:, :, R_STD], EPS_LN, None, ALU.add).then_inc(ve_r, 1)
                lg = row[u][:, :, D:EXT]
                link(v.tensor_reduce(lmax[:], lg, AX.X, ALU.max))
                link(v.tensor_tensor(dlog[:], lg, bc(lmax[:], 2, NE), ALU.subtract))
                link(v.scalar_tensor_tensor(out=m8[:], in0=dlog[:], scalar=0.0, in1=bc(e8, 1, TPB), op0=ALU.is_ge, op1=ALU.mult))

            def count(b, u):
                link(v.tensor_reduce(mm8[:], m8[:], AX.X, ALU.max))
                link(v.tensor_tensor(onehot[:], m8[:], bc(mm8[:], 2, NE), ALU.is_equal))
                link(v.tensor_copy(cnt[:, 1, :], onehot[:, 0, :]))
                for j in range(1, TPB):
                    ins = v.tensor_tensor(cnt[:, j + 1, :], cnt[:, j, :], onehot[:, j, :], ALU.add)
                    if j < TPB - 1:
                        link(ins)
                ins.then_inc(cnt_r, 1)

            def route_slot(b, u):
                dve.wait_ge(std_r, b * 2 + 1)
                v.tensor_tensor(dscl[:], dlog[:], bc(row[u][:, :, R_STD], 2, NE), ALU.mult).then_inc(dscl_r, 1)
                dve.wait_ge(pref_r, b + 1)
                v.tensor_tensor(pos[:], cnt[:, 0:TPB, :], bc(prefix, 1, TPB), ALU.add).then_inc(pref_used, 1)
                v.tensor_tensor(carry[:], carry[:], cnt[:, TPB, :], ALU.add).then_inc(carry_r, 1)
                v.tensor_scalar(sbase[:], mm8[:], -float(SEG), float(SEG * NE), ALU.mult, ALU.add)
                dve.wait_ge(pref_used, b + 2)
                link(v.tensor_tensor(pos[:], pos[:], onehot[:], ALU.mult))
                link(v.tensor_reduce(rank[:], pos[:], AX.X, ALU.add))
                v.tensor_tensor(slot[u][:], rank[:], sbase[:], ALU.add)
                dve.wait_ge(pexp_r, b + 1)
                link(v.tensor_reduce(psm[:], pexp[:], AX.X, ALU.add))
                v.reciprocal(row[u][:, :, R_GATE], psm[:]).then_inc(slot_r, 1)

            def normalise(b, pair):
                dve.wait_ge(ek_r, b * 2 + (pair + 1))
                ek4 = psum[:, (5, 2)[pair], 0:2 * H * VC].rearrange("p (g c) -> p g c", c=VC)
                link(v.reciprocal(zr[:, pair, :], ek4[:, :, HD]))
                v.tensor_tensor(attn[pair][:].rearrange("p j (h d) -> p (j h) d", d=HD), ek4[:, :, 0:HD],
                                bc(zr[:, pair, :], 2, HD), ALU.mult).then_inc(norm_r, 1)

            def finish_rows(b, u, pair):
                if pair == 0 and has(b, -1):
                    dve.wait_ge(sent_r, b)
                dve.wait_ge(pj_r, b * 2 + (pair + 1))
                for jj in range(2):
                    j = 2 * pair + jj
                    v.scalar_tensor_tensor(out=row[u][:, j, 0:EXT], in0=h0[:, b, j, :], scalar=scales[:, b, j:j + 1],
                                           in1=psum[:, (7, 5)[pair], jj * EXT:(jj + 1) * EXT], op0=ALU.mult, op1=ALU.add
                                           ).then_inc(h1_r, 1)
                for jj in range(2):
                    j = 2 * pair + jj
                    dve.wait_ge(h1_r, b * TPB + (j + 1))
                    ins = v.bn_stats(bn[:, j, :], row[u][:, j, 0:D])
                link(ins)
                settle(dve)
                for jj in range(2):
                    j = 2 * pair + jj
                    ins = v.bn_aggr(row[u][:, j, R_MEAN:R_MEAN + 2], bn[:, j, :])
                if pair:
                    link(ins)

            total_state(0, 0)
            base[0] += done[0]
            done[0] = 0
            start_b = base[0]

            def step_b(b, h, u):
                begin(b, start_b, LINKS_B0, LINKS_B)
                more, prior = has(b, 1), has(b, -1)
                if prior:
                    finish_rows(b - 1, 1 - u, 1)
                if more:
                    q_max(b + 1, 0)
                if prior:
                    pick(b - 1, 1 - u)
                if more:
                    q_max(b + 1, 1)
                if prior:
                    count(b - 1, 1 - u)
                if more:
                    q_max(b + 1, 2)
                    total_state(b + 1, 1 - u)
                    q_max(b + 1, 3)
                    q_shift(b + 1)
                if prior:
                    route_slot(b - 1, 1 - u)
                normalise(b, 0)
                normalise(b, 1)
                if has(b, 2):
                    split_x(b + 2, u)
                finish_rows(b, u, 0)
                end(b, LINKS_B0, LINKS_B)

            LINKS_B0 = 3 + 2 + 1 + 1
            LINKS_B = LINKS_B0 + 2 + 3 + 5 + 3
            v.sem_inc(pref_used, 1)
            steps_of(dve, NB, step_b, ahead=2)
            finish_rows(NB - 1, (NB - 1) % 2, 1)
            pick(NB - 1, (NB - 1) % 2)
            count(NB - 1, (NB - 1) % 2)
            route_slot(NB - 1, (NB - 1) % 2)

            dve.wait_ge(tot_r, 1)
            v.tensor_tensor(fill[:], prefix[0:1], cst[0:1, C_PAD:C_PAD + NE], ALU.add).then_inc(fill_r, 1)
            row0 = cst[0:1, :]
            link(v.tensor_tensor(over, bc(prefix[0:1], 2, CNTS), bc(row0[:, C_THR:C_THR + CNTS], 1, NE), ALU.is_gt))
            link(v.tensor_reduce(tiles_of[:], over, AX.X, ALU.add))
            link(v.tensor_tensor(upto, bc(tiles_of[:], 1, NE), row0[:, C_LE:C_T].rearrange("p (e f) -> p e f", e=NE), ALU.mult))
            link(v.tensor_reduce(ends[:], upto, AX.X, ALU.add))
            link(v.tensor_tensor(past, bc(row0[:, C_T:C_N], 2, NE), bc(ends[:], 1, NT), ALU.is_ge))
            v.tensor_tensor(past_n, past, bc(tiles_of[:], 1, NT), ALU.mult)
            link(v.tensor_reduce(t_exp[:], past, AX.X, ALU.add))
            v.tensor_scalar(tile_expert[:], t_exp[:], float(NE - 1), None, ALU.min).then_inc(table_r, 1)
            link(v.tensor_reduce(t_first[:], past_n, AX.X, ALU.add))
            link(v.tensor_tensor(t_within[:], row0[:, C_T:C_N], t_first[:], ALU.subtract))
            link(v.tensor_scalar(t_within[:], t_within[:], float(P), None, ALU.mult))
            v.scalar_tensor_tensor(out=tile_slot[:], in0=t_exp[:], scalar=float(SEG), in1=t_within[:], op0=ALU.mult,
                                   op1=ALU.add).then_inc(table_r, 1)

            def normed(t, h, u):
                dve.wait_ge(x_in[u], h * 16 + 16)
                if not isinstance(t, int) or t > 0:
                    dve.wait_ge(ct_r, t)
                v.tensor_scalar(xn, x_rows[u][:, 0:D], x_rows[u][:, R_MEAN:R_MEAN + 1],
                                x_rows[u][:, R_STD:R_STD + 1], ALU.subtract, ALU.mult).then_inc(xn_r, 1)

            def fetch(t, u):
                e = dve.value_load(tile_expert[0:1, bass.ds(t, 1)], min_val=0, max_val=NE - 1)
                settle(dve)
                v.tensor_copy(wi_now[u][:, 1, :], wi_all[:, bass.ds(e, 1), 1, :].rearrange("p e f -> p (e f)")).then_inc(wi_v, 1)

            dve.wait_ge(wi_in, 16)
            dve.wait_ge(w_late, 16 * (1 + NE + AFTER_B))
            dve.wait_ge(table_r, 1)
            fetch(0, 0)
            fetch(1, 1)
            normed(0, 0, 0)

            def step_c(t, h, u):
                if has(t, 1, NT):
                    normed(t + 1, h + (u + 1) // ROT, (u + 1) % ROT)
                if has(t, -1, NT):
                    dve.wait_ge(fin_r, t)
                v.tensor_copy(oidx[u][:], x_rows[u][:, R_ROW:ROW]).then_inc(oidx_r, 1)
                if has(t, 2, NT):
                    dve.wait_ge(hid_r, t * 2 + 1)
                    fetch(t + 2, (u + 2) % ROT)
                dve.wait_ge(y_r, t + 1)
                v.scalar_tensor_tensor(out=orow[u], in0=PS[:, 0:D], scalar=x_rows[u][:, R_GATE:R_GATE + 1],
                                       in1=x_rows[u][:, 0:D], op0=ALU.mult, op1=ALU.add).then_inc(o_r, 1)

            steps_of(dve, NT, step_c, ahead=2, cycle=ROT)

        @block.tensor
        def _(pe):
            mm = nc.tensor.matmul
            pe.wait_ge(pool_const, 4)
            pe.wait_ge(prep_v, 2)
            for k in range(2):
                mm(psum[0:KC, 0, 0:DB], lhsT=inv_d[0:KC, :], rhs=pw[:, k, 0:DB], start=k == 0, stop=k == 1)
            for k in range(2):
                mm(psum[0:KC, 0, DB:DB + NE], lhsT=inv_d[0:KC, :], rhs=rw[:, k, :], start=k == 0, stop=k == 1)
            mm(psum[0:KC, 2, 0:M], lhsT=pm_rep[:].rearrange("m h d -> m (h d)"), rhs=ident[0:M, 0:M], start=True, stop=True)
            for kn in range(2):
                c0 = kn * (D + 1)
                nc.tensor.transpose(psum[0:KC, 3, c0:c0 + KC], wp[0:KC, 0, kn * KC:(kn + 1) * KC], ident[0:KC, 0:KC])
                ins = nc.tensor.transpose(psum[0:KC, 3, c0 + KC:c0 + D + 1], wp[0:KC + 1, 1, kn * KC:(kn + 1) * KC],
                                          ident[0:KC + 1, 0:KC + 1])
            ins.then_inc(prep_pe, 1)
            pe.wait_ge(prep_v, 3)
            for c in range(4):
                for k in range(2):
                    mm(psum[0:KC, 1, c * P:(c + 1) * P], lhsT=wqkv[:, k, c * KC:(c + 1) * KC], rhs=gt[:, k, :],
                       start=k == 0, stop=k == 1)
            for k in range(2):
                mm(psum[:, 0, k * KC:(k + 1) * KC], lhsT=pw[:, k, :], rhs=ident[0:KC, 0:KC], start=True, stop=True)
            for k in range(2):
                mm(psum[:, 0, D:EXT], lhsT=pw[:, k, :], rhs=rc[:, k, :], start=k == 0, stop=k == 1)
            for k in range(2):
                mm(psum[:, 0, EXT:EXT + DB], lhsT=proj_dup[:, k, :], rhs=proj_in[:, k, :], start=k == 0, stop=k == 1)
            for k in range(2):
                mm(psum[:, 0, EXT + DB:EXT + P], lhsT=gt[:, k, :], rhs=gt[:, k, 0:DB], start=k == 0, stop=k == 1)
            for c in range(2):
                n = 3 * D // 2
                for k in range(2):
                    mm(psum[:, 4 + c, 0:n], lhsT=gt[:, k, :], rhs=wqkv[:, k, c * n:(c + 1) * n], start=k == 0, stop=k == 1)
            for c, n in ((0, KC), (1, KC + 1)):
                for kn in range(2):
                    ins = mm(psum[0:n, 2, c * NE:(c + 1) * NE], lhsT=wpt[:, kn, c * KC:c * KC + n], rhs=rc[:, kn, :],
                             start=kn == 0, stop=kn == 1)
            ins.then_inc(prep_pe, 1)
            pe.wait_ge(prep_v, 4)
            for n, where in ((2, 6), (3, 7), (0, 1), (1, 2)):
                ins = mm(psum[:, where, 0:HALF], lhsT=ft[:, n, :], rhs=bd.rearrange("p h m -> p (h m)"), start=True, stop=True)
            ins.then_inc(prep_pe, 1)

            def two_pass(dst, lhsT, name, c0, c1):
                mm(dst, lhsT=lhsT, rhs=f_hi[name][:, c0:c1], start=True, stop=False)
                return mm(dst, lhsT=lhsT, rhs=f_lo[name][:, c0:c1], start=False, stop=True)

            def basin_t(b, u):
                pe.wait_ge(split_r, b + 1)
                for j in range(TPB):
                    ins = nc.tensor.transpose(T[:, j * P:(j + 1) * P], split[u][:, j, :], ident)
                ins.then_inc(tr_r, 1)

            def embed(b, u, j):
                if j == 0:
                    pe.wait_ge(bt_r, b + 1)
                if not isinstance(b, int) or b + j:
                    pe.wait_ge(h0_r, b * TPB + j)
                two_pass(psum[:, 5, 0:EXT + P], bt[u][:, j * P:(j + 1) * P], "h", 0, EXT + P).then_inc(ph_r, 1)

            def spread_max(b):
                pe.wait_ge(gmin_r, b + 1)
                mm(MX[:, 0:1], lhsT=ones[0:1, :], rhs=gmin[:], start=True, stop=True).then_inc(nbc_r, 1)

            def sum_values(b):
                pe.wait_ge(vs_r, b + 1)
                mm(T[:, 0:D], lhsT=ones[:], rhs=vsum[:], start=True, stop=True).then_inc(vsm_r, 1)

            def state(b, u):
                pe.wait_ge(s_free, b + 1)
                pe.wait_ge(vp_r, b + 1)
                for i in range(CH):
                    for j in range(TPB):
                        ins = mm(PS[:, i * HW * VC:(i + 1) * HW * VC], lhsT=ek[u][:, j, F0[i]:F0[i] + P],
                                 rhs=vp[u][:, j * H + W0[i]:j * H + W0[i] + HW, :].rearrange("p h c -> p (h c)"),
                                 start=i == 0 and j == 0, stop=i == CH - 1 and j == TPB - 1, skip_group_check=True)
                ins.then_inc(s_r, 1)

            pe.wait_ge(prep_v, 5)
            pe.wait_ge(prep_hi, 2)
            basin_t(0, 0)
            for j in range(TPB):
                embed(0, 0, j)
            basin_t(1, 1)
            pe.wait_ge(prep_v, 6)

            def step_a(b, h, u):
                for j in range(TPB):
                    lhsT = bt[u][:, j * P:(j + 1) * P]
                    if not isinstance(b, int) or b * TPB + j >= 2:
                        pe.wait_ge(exp_r, b * TPB + (j - 1))
                    q = 2 * (j % 2)
                    two_pass(psum[:, q, 0:HALF], lhsT, "kd", 0, HALF)
                    two_pass(psum[:, q + 1, 0:HALF], lhsT, "kd", HALF, NF).then_inc(pd_r, 1)
                    if j == 0 and has(b, -1):
                        spread_max(b - 1)
                    if has(b, 1):
                        embed(b + 1, 1 - u, j)
                    if j == 0 and has(b, -1):
                        pe.wait_ge(nb_r, b)
                    if not isinstance(b, int) or b + j:
                        pe.wait_ge(kv_r, b * TPB + j)
                    two_pass(psum[:, 4, 0:2 * D], lhsT, "qkv", D, 3 * D).then_inc(pkv_r, 1)
                    if j == 1 and has(b, -1):
                        sum_values(b - 1)
                if has(b, -1):
                    state(b - 1, 1 - u)
                pe.wait_ge(nmin_r, b + 1)
                pe.wait_ge(kv_r, b * TPB + TPB)
                nc.tensor.transpose(MX[0:1, 0:P], nmin[:], ident).then_inc(nt_r, 1)
                if has(b, 2):
                    if has(b, -1):
                        pe.wait_ge(ev_r, b)
                    basin_t(b + 2, u)

            steps_of(pe, NB, step_a, ahead=2)
            spread_max(NB - 1)
            sum_values(NB - 1)
            state(NB - 1, (NB - 1) % 2)

            def x_t(b, u):
                pe.wait_ge(xsplit_r, b + 1)
                for j in range(TPB):
                    ins = nc.tensor.transpose(T[:, j * P:(j + 1) * P], split[u][:, j, :], ident)
                ins.then_inc(tc_r, 1)

            def queries(b, u, j):
                lhsT = xt[u][:, j * P:(j + 1) * P]
                if not isinstance(b, int) or b + j:
                    pe.wait_ge(smax_r, b * TPB + j)
                two_pass(psum[:, 0, 0:HALF], lhsT, "qd", 0, HALF)
                two_pass(psum[:, 1, 0:HALF], lhsT, "qd", HALF, NF).then_inc(qd_r, 1)
                if j % 2 == 0:
                    if not isinstance(b, int) or b + j:
                        pe.wait_ge(qsq_r, b * 2 + j // 2)
                ins = two_pass(psum[:, 2, (j % 2) * D:(j % 2 + 1) * D], lhsT, "qkv", 0, D)
                if j % 2:
                    ins.then_inc(qq_r, 1)

            def shift_t(b):
                pe.wait_ge(sd_r, b + 1)
                for j in range(TPB):
                    ins = nc.tensor.transpose(psum[0:2 * H, 3, j * P:(j + 1) * P], sdh[:, j, :], ident)
                ins.then_inc(tc_r, 1)

            def features(b, u, i):
                if not isinstance(b, int) or b * CH + i >= 2:
                    pe.wait_ge(fe_r, b * CH + (i - 1))
                dst = bank(3 + (CH * u + i) % 2)
                mm(dst, lhsT=f_hi["qd"][:, F0[i]:F0[i] + P], rhs=xt[u], start=True, stop=False)
                mm(dst, lhsT=f_lo["qd"][:, F0[i]:F0[i] + P], rhs=xt[u], start=False, stop=False)
                mm(dst, lhsT=ind[:, i * P:(i + 1) * P], rhs=sdt, start=False, stop=True).then_inc(fm_r, 1)

            def attend(b, u, pair):
                if pair == 0:
                    pe.wait_ge(kvb_r, b + 1)
                    pe.wait_ge(eps_r, b * 3 + 2)
                for jj in range(2):
                    j = 2 * pair + jj
                    for i in range(CH):
                        c0 = jj * H * VC + W0[i] * VC
                        if j == 0 and i == CH - 1:
                            pe.wait_ge(eps_r, b * 3 + 3)
                        ins = mm(psum[:, (5, 2)[pair], c0:c0 + HW * VC], lhsT=eq[:, i, j * P:(j + 1) * P],
                                 rhs=kv[u][:, i * HW * VC:(i + 1) * HW * VC], start=jj == 0 and i == 0,
                                 stop=jj == 1 and i == CH - 1, skip_group_check=True)
                ins.then_inc(ek_r, 1)

            def attn_t(b, pair):
                pe.wait_ge(norm_r, b * 2 + (pair + 1))
                dst = bank((6, 4)[pair])
                for jj in range(2):
                    for k in range(2):
                        ins = nc.tensor.transpose(dst[0:KC, (jj * 2 + k) * P:(jj * 2 + k + 1) * P],
                                                  attn[pair][:, jj, k * KC:(k + 1) * KC], ident)
                ins.then_inc(tc_r, 1)

            def project(b, pair, n):
                pe.wait_ge(t_ev, n)
                if pair == 0:
                    pe.wait_ge(pref_used, b + 1)
                for jj in range(2):
                    for k in range(2):
                        rows = KC + k
                        ins = mm(psum[:, (7, 5)[pair], jj * EXT:(jj + 1) * EXT],
                                 lhsT=at[pair][0:rows, (jj * 2 + k) * P:(jj * 2 + k + 1) * P],
                                 rhs=wp[0:rows, k, :], start=jj == 0 and k == 0, stop=jj == 1 and k == 1, skip_group_check=True)
                ins.then_inc(pj_r, 1)

            def earlier(b):
                pe.wait_ge(cnt_r, b + 1)
                mm(prefix, lhsT=tri, rhs=cnt[:, TPB, :], start=True, stop=False)
                mm(prefix, lhsT=ones[:], rhs=carry[:], start=False, stop=True).then_inc(pref_r, 1)

            pe.wait_ge(s_free, NB + 1)
            pe.wait_ge(ev_r, NB)
            x_t(0, 0)
            pe.wait_ge(t_ev, 1)
            for j in range(TPB):
                queries(0, 0, j)
            shift_t(0)
            x_t(1, 1)
            pe.wait_ge(prep_v, 7)

            def step_b(b, h, u):
                more = has(b, 1)
                n = first_t(b)
                pe.wait_ge(t_ev, n)
                features(b, u, 0)
                features(b, u, 1)
                for j in range(TPB):
                    if more:
                        queries(b + 1, 1 - u, j)
                    if j < 3:
                        features(b, u, j + 2)
                if has(b, -1):
                    earlier(b - 1)
                attend(b, u, 0)
                if more:
                    pe.wait_ge(qsq_r, b * 2 + 4)
                attend(b, u, 1)
                attn_t(b, 0)
                if more:
                    shift_t(b + 1)
                project(b, 0, n + 1)
                attn_t(b, 1)
                if has(b, 2):
                    x_t(b + 2, u)
                project(b, 1, n + 3 if more else n + 2)

            steps_of(pe, NB, step_b, ahead=2)
            earlier(NB - 1)
            pe.wait_ge(carry_r, NB)
            mm(prefix, lhsT=ones[:], rhs=carry[:], start=True, stop=True).then_inc(tot_r, 1)

            def rows_t(t):
                pe.wait_ge(xn_r, t + 1)
                if not isinstance(t, int) or t:
                    pe.wait_ge(xe_r, t)
                for k in range(2):
                    ins = nc.tensor.transpose(T[0:KC, k * P:(k + 1) * P], xn[:, k * KC:(k + 1) * KC], ident)
                ins.then_inc(ct_r, 1)

            pe.wait_ge(w_late, 16 * (1 + NE + AFTER_B))
            pe.wait_ge(table_r, 1)
            rows_t(0)

            def step_c(t, h, u):
                e = pe.value_load(tile_expert[0:1, bass.ds(t, 1)], min_val=0, max_val=NE - 1)
                pe.wait_ge(wi_a, t + 1)
                pe.wait_ge(wi_v, t + 1)
                pe.wait_ge(xe_r, t + 1)
                for f in range(DF // P):
                    for k in range(2):
                        ins = mm(psum[:, 3 + f // 4, f % 4 * P:(f % 4 + 1) * P],
                                 lhsT=wi_now[u][:, k, f * P:(f + 1) * P],
                                 rhs=xe[:, k, :], start=k == 0, stop=k == 1)
                    if f in (3, 5):
                        ins.then_inc(hid_r, 1)
                if has(t, 1, NT):
                    rows_t(t + 1)
                if has(t, -1, NT):
                    pe.wait_ge(o_r, t)
                for f in range(DF // P):
                    if f in (0, 4):
                        pe.wait_ge(relu_r, t * 2 + (1 + f // 4))
                        settle(pe)
                    ins = mm(PS[:, 0:D], lhsT=hid[:, f, :],
                             rhs=wo_all[:, bass.ds(e, 1), f, :].rearrange("p e n -> p (e n)"), start=f == 0, stop=f == DF // P - 1)
                ins.then_inc(y_r, 1)

            steps_of(pe, NT, step_c, cycle=ROT)


_INS = ["x", "L0_tok_basin_coords", "L0_tok_proj_w", "L0_tok_norm_w", "L0_attn_W_qkv", "L0_attn_W_proj",
        "L0_attn_b_proj", "L0_attn_proj_mat", "L0_ffn_router_w", "L0_ffn_wi", "L0_ffn_wo"]


def kernel(**inputs):
    import concourse.bacc as bacc
    from concourse.bass_utils import run_bass_kernel_spmd

    nc = bacc.Bacc("TRN2", target_bir_lowering=False, num_devices=1)
    arrays, args = {}, []
    for name in _INS:
        a = np.ascontiguousarray(inputs[name])
        arrays[f"in_{name}"] = a
        args.append(nc.dram_tensor(f"in_{name}", a.shape, mybir.dt.from_np(a.dtype), kind="ExternalInput").ap())
    c = constants()
    arrays["in_consts"] = c
    args.append(nc.dram_tensor("in_consts", c.shape, F32, kind="ExternalInput").ap())
    out = nc.dram_tensor("out", (NB, SEQ, D), F32, kind="ExternalOutput").ap()
    lm_tower(nc, *args, out)
    r = run_bass_kernel_spmd(nc, [arrays], core_ids=[0])
    return r.results[0]["out"]
```

```python
from contextlib import ExitStack

import numpy as np

import concourse.bass as bass
from concourse import mybir

F32, F32R = mybir.dt.float32, mybir.dt.float32r
I32, U32 = mybir.dt.int32, mybir.dt.uint32
ALU = mybir.AluOpType
ACT = mybir.ActivationFunctionType
AX = mybir.AxisListType

P = 128
NB, SEQ = 8, 512
TPB = SEQ // P
VOCAB, DB, D = 32000, 64, 192
H, HD, M = 12, 16, 44
NF = H * M
CH = 5
F0 = [0, 128, 256, 384, NF - P]
HW = 6
W0 = [0, 0, 4, 6, 6]
VC = HD + 1
NE, DF = 8, 768
TOK = NB * SEQ
SEG = TOK + P
NT = (TOK + NE * (P - 1)) // P
SPARE = NT - TOK // P
CNTS = TOK // P
KC = D // 2
EXT = D + NE
ROW = EXT + 4
R_MEAN, R_STD, R_GATE, R_ROW = EXT, EXT + 1, EXT + 2, EXT + 3
EPS_RMS, EPS_LN, EPS_FEAT = 1e-8, 1e-5, 1e-4
NORM = HD ** -0.25
FAR = float(1 << 20)
C_ID, C_TRI, C_IND = 0, P, 2 * P
C_MASK = C_IND + CH * P
C_HM = C_MASK + CH * HW
C_E8 = C_HM + HW
C_ROW = C_E8 + NE
C_PAD = C_ROW + NB * TPB
C_THR = C_PAD + NE
C_LE = C_THR + CNTS
C_T = C_LE + NE * NE
C_N = C_T + NT


def constants():
    c = np.zeros((P, C_N), np.float32)
    c[:, C_ID:C_ID + P] = np.eye(P)
    c[:, C_TRI:C_TRI + P] = np.triu(np.ones((P, P)), 1)
    for i in range(CH):
        for f in range(P):
            feat = F0[i] + f
            for part in range(2):
                c[part * H + feat // M, C_IND + i * P + f] = -1.0
            if i < CH - 1 or feat >= F0[3] + P:
                if 0 <= feat // M - W0[i] < HW:
                    c[f, C_MASK + i * HW + feat // M - W0[i]] = 1.0
    for p in range(KC):
        c[p, C_HM + p // HD] = 1.0
    c[:, C_E8:C_E8 + NE] = NE - np.arange(NE)
    p, b, j = np.meshgrid(np.arange(P), np.arange(NB), np.arange(TPB), indexing="ij")
    c[:, C_PAD:C_THR] = np.arange(NE) * SEG
    c[:, C_THR:C_LE] = np.arange(CNTS) * P
    c[:, C_LE:C_T] = np.tril(np.ones((NE, NE))).reshape(-1)
    c[:, C_T:C_N] = np.arange(NT)
    c[:, C_ROW:C_PAD] = (b * SEQ + p * TPB + j).reshape(P, -1)
    return c


def bc(ap, axis, n):
    a = ap.unsqueeze(axis)
    shape = list(a.shape)
    shape[axis] = n
    return a.to_broadcast(shape)


def lm_tower(nc, ids, coords, proj_w, norm_w, w_qkv, w_proj, b_proj, proj_mat, router_w, wi, wo, consts, out):
    with ExitStack() as ctx:
        def sb(name, shape, dt=F32):
            return ctx.enter_context(nc.sbuf_tensor(name, shape, dt))

        def sem(name):
            return ctx.enter_context(nc.semaphore(name))

        slots = nc.dram_tensor("slots", [NE * SEG + SPARE * P, ROW], F32).ap()
        out_rows = out.rearrange("b n d -> (b n) d")

        psum = ctx.enter_context(nc.psum_tensor("psum", [P, 8, 512], F32))

        n_wi, n_wo = 2 * DF, DF // P * D
        AT_ONCE, AFTER_B = 3, 3
        base = -(-nc.sbuf_base // 32) * 32
        w_all = sb("w_all", [P, NE * (n_wi + n_wo)])
        wi_all = w_all[0:KC, 0:NE * n_wi].rearrange("p (e k f) -> p e k f", e=NE, k=2)
        wo_all = w_all[:, NE * n_wi:NE * (n_wi + n_wo)].rearrange("p (e c n) -> p e c n", e=NE, n=D)
        taken = {"A": (AT_ONCE + AFTER_B) * n_wi, "B": AT_ONCE * n_wi}
        limit = {"A": NE * (n_wi + n_wo), "B": (AT_ONCE + AFTER_B) * n_wi}

        def early(name, shape, dt=F32, until="A"):
            a = taken[until]
            taken[until] += -(-int(np.prod(shape[1:])) // 8) * 8
            assert taken[until] <= limit[until]
            return nc.alloc_sbuf_tensor_at(name, shape, dt, offset=base + 4 * a)[:]

        cst = sb("cst", [P, C_N])
        ident = cst[:, C_ID:C_ID + P]
        tri = cst[:, C_TRI:C_TRI + P]
        mask = cst[:, C_MASK:C_MASK + CH * HW]
        e8 = cst[:, C_E8:C_E8 + NE]
        rows_of = cst[:, C_ROW:C_PAD].rearrange("p (b j) -> p b j", j=TPB)
        ones = sb("ones", [P, P])
        inv_d = sb("inv_d", [P, KC])
        neg_half = sb("neg_half", [P, 2 * TPB])
        ind = early("ind", [P, CH * P], F32R, "B")
        proj_in = sb("proj_in", [KC, 2, DB])
        proj_dup = early("proj_dup", [KC, 2, P])
        nw = sb("nw", [KC, 2])
        pw = early("pw", [KC, 2, P])
        gt = early("gt", [KC, 2, P])
        wqkv = early("wqkv", [KC, 2, 3 * D])
        rw = sb("rw", [KC, 2, NE])
        rc = sb("rc", [KC, 2, NE])
        pm = sb("pm", [M, HD])
        pm_rep = sb("pm_rep", [M, HW, HD])
        bd = early("bd", [KC, HW, M], F32, "B")
        ft = early("ft", [KC, 4, P])
        wp = sb("wp", [P, 2, EXT])
        wpt = early("wpt", [KC, 2, D + 1])
        f_hi = {}
        f_lo = {}
        for name, n in (("qd", NF), ("kd", NF), ("qkv", 3 * D), ("h", EXT + P)):
            for part, f in (("hi", f_hi), ("lo", f_lo)):
                until = {"kd": "A", "qd": "B"}
                f[name] = (early(f"f_{name}_{part}", [P, n], F32R, until[name]) if name in until
                           else sb(f"f_{name}_{part}", [P, n], F32R)[:])

        idx_i = sb("idx_i", [P, NB, TPB], I32)
        idx_f = sb("idx_f", [P, NB, TPB])
        idx_w = sb("idx_w", [P, NB, TPB])
        idx = sb("idx", [P, NB, TPB], U32)
        idx_b = [sb(f"idx_b{u}", [P, TPB], U32) for u in range(2)]
        basin = [sb(f"basin{u}", [P, TPB, DB]) for u in range(2)]
        basin_all = sb("basin_all", [P, NB, TPB, DB])
        split = [sb(f"split{u}", [P, TPB, 2 * DB]) for u in range(2)]
        bt = [early(f"bt{u}", [P, SEQ], F32R) for u in range(2)]
        quad = early("quad", [P, TPB, 2, DB])
        qs = sb("qs", [P, TPB, 2])
        pow_in = sb("pow_in", [P, 2 * TPB])
        scales = sb("scales", [P, NB, 2 * TPB])
        h0 = sb("h0", [P, NB, TPB, EXT])
        rmax = [sb(f"rmax{u}", [P, TPB]) for u in range(2)]
        nmax = [sb(f"nmax{u}", [P, TPB]) for u in range(2)]
        features_sb = sb("features_sb", [P, CH * SEQ])
        ek = [features_sb[:, 0:TPB * NF].rearrange("p (j f) -> p j f", j=TPB), early("ek1", [P, TPB, NF])]
        ksq = [early(f"ksq{u}", [P, TPB, D]) for u in range(2)]
        val = [early(f"val{u}", [P, TPB, D]) for u in range(2)]
        vsum2 = sb("vsum2", [P, 2, D])
        vsum = sb("vsum", [P, D])
        vp = [early(f"vp{u}", [P, TPB * H, VC]) for u in range(2)]
        nmin = sb("nmin", [P, 1])
        gmin = sb("gmin", [1, 1])
        nbatch = sb("nbatch", [P, NB])
        nb_now = sb("nb_now", [P, 1])
        rms2 = sb("rms2", [P, TPB])
        dmax = sb("dmax", [P, TPB])
        kq = sb("kq", [P, TPB * H])
        farg = sb("farg", [P, TPB * H])
        s_flat = sb("s_flat", [P, NB * CH * HW * VC])
        s_all = s_flat[:].rearrange("p (b c v) -> p b c v", b=NB, v=VC)
        n_s = CH * HW * VC
        ev_flat = sb("ev_flat", [P, NB * n_s])
        ev = [ev_flat[:, u * n_s:(u + 1) * n_s] for u in range(2)]
        v_sums = ev_flat[:, 2 * n_s:2 * n_s + NB * D].rearrange("p (b d) -> p b d", b=NB)
        mask_den = sb("mask_den", [P, CH * HW])

        nglob = sb("nglob", [P, 1])
        dcb = sb("dcb", [P, NB])
        cb = sb("cb", [P, NB])
        xs = [sb(f"xs{u}", [P, TPB, DB]) for u in range(2)]
        xt = [early(f"xt{u}", [P, SEQ], F32R, "B") for u in range(2)]
        qsq = early("qsq", [P, TPB, D], F32, "B")
        qr = sb("qr", [P, TPB * H])
        smax = sb("smax", [P, TPB, H])
        sd = sb("sd", [P, TPB, H])
        sdh = sb("sdh", [P, TPB, 2 * H])
        sdt = early("sdt", [P, SEQ], F32R, "B")
        eq = features_sb[:, 0:CH * SEQ].rearrange("p (c n) -> p c n", c=CH)
        kv = [sb(f"kv{u}", [P, CH * HW * VC]) for u in range(2)]
        zr = sb("zr", [P, 2, 2 * H])
        attn = [sb(f"attn{u}", [P, 2, D]) for u in range(2)]
        at = [sb(f"at{u}", [P, 2 * 2 * P]) for u in range(2)]
        row = [sb(f"row{u}", [P, TPB, ROW]) for u in range(2)]
        bn = sb("bn", [P, TPB, 6])
        ve = sb("ve", [P, TPB])
        dlog = sb("dlog", [P, TPB, NE])
        dscl = sb("dscl", [P, TPB, NE])
        pexp = sb("pexp", [P, TPB, NE])
        psm = sb("psm", [P, TPB])
        lmax = sb("lmax", [P, TPB])
        m8 = sb("m8", [P, TPB, NE])
        mm8 = sb("mm8", [P, TPB])
        onehot = sb("onehot", [P, TPB, NE])
        cnt = sb("cnt", [P, TPB + 1, NE])
        carry = sb("carry", [P, NE])
        pos = sb("pos", [P, TPB, NE])
        rank = sb("rank", [P, TPB])
        sbase = sb("sbase", [P, TPB])
        slot = [sb(f"slot{u}", [P, TPB], U32) for u in range(2)]

        flat0, flat1 = (split[u][:].rearrange("p j d -> p (j d)")[0:1] for u in range(2))
        over = flat0[:, 0:NE * CNTS].rearrange("p (e k) -> p e k", e=NE)
        past = flat1[:, 0:NT * NE].rearrange("p (t e) -> p t e", e=NE)
        past_n = flat0[:, 0:NT * NE].rearrange("p (t e) -> p t e", e=NE)
        upto = xs[0][:].rearrange("p j d -> p (j d)")[0:1, 0:NE * NE].rearrange("p (e f) -> p e f", e=NE)
        tiles_of = sb("tiles_of", [1, NE])
        ends = sb("ends", [1, NE])
        t_exp = sb("t_exp", [1, NT])
        t_first = sb("t_first", [1, NT])
        t_within = sb("t_within", [1, NT])
        tile_slot = sb("tile_slot", [1, NT], I32)
        tile_expert = sb("tile_expert", [1, NT], I32)
        fill = sb("fill", [1, NE], I32)

        ROT = 3
        x_rows = [ev_flat[:, u * ROW:(u + 1) * ROW] for u in range(ROT)]
        orow = [ev_flat[:, ROT * ROW + u * D:ROT * ROW + (u + 1) * D] for u in range(ROT)]
        xn = ev_flat[:, ROT * (ROW + D):ROT * (ROW + D) + D]
        xe = ev_flat[0:KC, ROT * (ROW + D) + D:ROT * (ROW + D) + D + 2 * P].rearrange("p (k n) -> p k n", k=2)
        hid = s_flat[:, 0:DF].rearrange("p (f n) -> p f n", n=P)
        n2 = ROT * (ROW + D) + D + 2 * P
        wi_now = [m.rearrange("p (k f) -> p k f", k=2) for m in (
            s_flat[0:KC, DF:DF + n_wi], s_flat[0:KC, DF + n_wi:DF + 2 * n_wi], ev_flat[0:KC, n2:n2 + n_wi])]
        oidx = [sb(f"oidx{u}", [P, 1], U32) for u in range(ROT)]
        blank = sb("blank", [P, ROW])

        names = """w_in ids_in gathered0 gathered1 blank_out filled sent0 sent1 wi_in w_late x_in0 x_in1 x_in2 fin0 fin1 fin2
        pool_const prep_pe prep_hi prep_v steps idx_r idxb_r split_r tr_r bt_r ph_r h0_r quad_r pow_in_r scale_r kept
        pd_r pkv_r nmax_r exp_r kv_r nmin_r nt_r gmin_r nbc_r nb_r farg_r f_r vs_half vs_r vsm_r ev_r spread_r kvs_r vp_r s_r s_free
        dcb_r cb_r kvb_r xs_r xsplit_r tc_r t_ev qd_r qq_r smax_r qsq_r sd_r fm_r fe_r eps_r
        ek_r norm_r pj_r h1_r ve_r std_r cnt_r pref_r pref_used dscl_r pexp_r slot_r sent_r fin_r
        carry_r tot_r fill_r table_r wi_a wi_v xn_r ct_r xe_r hid_r relu_r y_r o_r oidx_r settled""".split()
        S = {n: sem(n) for n in names}
        (w_in, ids_in, gathered0, gathered1, blank_out, filled, sent0, sent1, wi_in, w_late, x_in0, x_in1, x_in2, fin0, fin1, fin2,
         pool_const, prep_pe, prep_hi, prep_v, steps, idx_r, idxb_r, split_r, tr_r, bt_r, ph_r, h0_r, quad_r, pow_in_r, scale_r, kept,
         pd_r, pkv_r, nmax_r, exp_r, kv_r, nmin_r, nt_r, gmin_r, nbc_r, nb_r, farg_r, f_r, vs_half, vs_r, vsm_r, ev_r, spread_r, kvs_r, vp_r, s_r, s_free,
         dcb_r, cb_r, kvb_r, xs_r, xsplit_r, tc_r, t_ev, qd_r, qq_r, smax_r, qsq_r, sd_r, fm_r, fe_r, eps_r,
         ek_r, norm_r, pj_r, h1_r, ve_r, std_r, cnt_r, pref_r, pref_used, dscl_r, pexp_r, slot_r, sent_r, fin_r,
         carry_r, tot_r, fill_r, table_r, wi_a, wi_v, xn_r, ct_r, xe_r, hid_r, relu_r, y_r, o_r, oidx_r, settled) = S.values()
        gathered, sent = (gathered0, gathered1), (sent0, sent1)
        x_in, fin = (x_in0, x_in1, x_in2), (fin0, fin1, fin2)

        block = ctx.enter_context(nc.Block())

        def steps_of(eng, n, body, ahead=1, cycle=2, peel=1):
            for k in range(peel):
                body(k, k // cycle, k % cycle)
            rounds = (n - peel - ahead) // cycle
            with eng.Fori(0, rounds) as i:
                for m in range(peel, peel + cycle):
                    body(i * cycle + m, i + m // cycle, m % cycle)
            for k in range(peel + cycle * rounds, n):
                body(k, k // cycle, k % cycle)

        def settle(eng):
            eng.sem_inc(settled, 1)

        def first_t(b):
            return 3 + b * 4 if has(b, 1) else 2 + b * 4

        def has(k, n, steps=NB):
            return not isinstance(k, int) or 0 <= k + n < steps

        def bank(k, n=512):
            return psum[:, k, 0:n]

        T, PS = bank(6), bank(7)
        prefix = psum[:, 7, 2 * EXT:2 * EXT + NE]
        MX = psum[:, 4, 2 * D:512]
        HALF = NF // 2

        @block.sync
        def _(sp):
            with nc.allow_non_contiguous_dma(reason="runs of 4 ids, and 192 norm weights"):
                sp.dma_start(idx_i[:], ids.rearrange("b (p j) -> p b j", j=TPB)).then_inc(ids_in, 16)
                sp.dma_start(nw[:], norm_w.rearrange("(k p) -> p k", p=KC)).then_inc(w_in, 16)
            sp.dma_start(cst[:], consts).then_inc(w_in, 16)
            sp.dma_start(proj_in[:], proj_w.rearrange("(k p) d -> p k d", p=KC)).then_inc(w_in, 16)
            sp.dma_start(rw[:], router_w.rearrange("(k p) e -> p k e", p=KC)).then_inc(w_in, 16)
            sp.dma_start(pm[:], proj_mat).then_inc(w_in, 16)
            sp.dma_start(wqkv, w_qkv.rearrange("(k p) n -> p k n", p=KC)).then_inc(w_in, 16)
            sp.dma_start(wp[0:KC, :, 0:D], w_proj.rearrange("(k p) n -> p k n", p=KC)).then_inc(w_in, 16)
            sp.dma_start(wp[KC:KC + 1, 1, 0:D], b_proj.rearrange("(a n) -> a n", a=1)).then_inc(w_in, 16)
            sp.wait_ge(pool_const, 2)
            sp.dma_start(slots[NE * SEG:, :].rearrange("(t p) r -> p t r", p=P), bc(blank[:, :], 1, SPARE)).then_inc(blank_out, 16)
            sp.dma_start(wi_all[:, 0:AT_ONCE], wi[0:AT_ONCE].rearrange("e (k p) f -> p e k f", p=KC)).then_inc(wi_in, 16)
            sp.wait_ge(s_free, NB + 1)
            sp.wait_ge(kept, NB)
            sp.dma_start(wi_all[:, AT_ONCE + AFTER_B:NE], wi[AT_ONCE + AFTER_B:NE].rearrange("e (k p) f -> p e k f", p=KC)).then_inc(w_late, 16)
            for e in range(NE):
                sp.dma_start(wo_all[:, e], wo[e].rearrange("(c p) n -> p c n", p=P)).then_inc(w_late, 16)
            sp.wait_ge(fm_r, NB * CH)
            for e in range(AT_ONCE, AT_ONCE + AFTER_B):
                sp.dma_start(wi_all[:, e], wi[e].rearrange("(k p) f -> p k f", p=KC)).then_inc(w_late, 16)

            def load_rows(t, u):
                first = sp.value_load(tile_slot[0:1, bass.ds(t, 1)], min_val=0, max_val=NE * SEG + (SPARE - 1) * P)
                sp.dma_start(x_rows[u], slots[bass.ds(first, P), :]).then_inc(x_in[u], 16)

            sp.wait_ge(fill_r, 1)
            for e in range(NE // 2):
                first = sp.value_load(fill[0:1, e:e + 1], min_val=0, max_val=(NE - 1) * SEG + TOK)
                sp.dma_start(slots[bass.ds(first, P), :], blank[:, :]).then_inc(filled, 16)
            sp.wait_ge(table_r, 2)
            first_two = [sp.value_load(tile_slot[0:1, t:t + 1], min_val=0, max_val=NE * SEG + (SPARE - 1) * P) for t in range(2)]
            sp.wait_ge(blank_out, 16)
            for u in range(2):
                sp.wait_ge(sent[u], 16 * TPB * NB // 2)
            sp.wait_ge(filled, 16 * NE)
            for t, first in enumerate(first_two):
                sp.dma_start(x_rows[t], slots[bass.ds(first, P), :]).then_inc(x_in[t], 16)

            def ahead_rows(t, h, u):
                if has(t, 2, NT):
                    if has(t, -1):
                        sp.wait_ge(o_r, t)
                        settle(sp)
                    load_rows(t + 2, (u + 2) % ROT)

            steps_of(sp, NT, ahead_rows, ahead=2, cycle=ROT)
            for u in range(ROT):
                sp.wait_ge(fin[u], 16 * len(range(u, NT, ROT)))

        @block.gpsimd
        def _(pool):
            g = nc.gpsimd
            g.memset(blank[:, 0:R_ROW], 0.0).then_inc(pool_const, 1)
            g.memset(blank[:, R_ROW:ROW], FAR).then_inc(pool_const, 1)
            g.memset(ones[:], 1.0).then_inc(pool_const, 1)
            g.memset(inv_d[:], 1.0 / D).then_inc(pool_const, 1)
            g.memset(neg_half[:], -0.5).then_inc(pool_const, 1)
            g.memset(at[0][:], 1.0).then_inc(pool_const, 1)
            g.memset(at[1][:], 1.0).then_inc(pool_const, 1)
            g.memset(carry[:], 0.0).then_inc(pool_const, 1)
            g.memset(cnt[:], 0.0).then_inc(pool_const, 1)
            pool.sem_inc(sent_r, 1)
            pool.sem_inc(fin_r, ROT - 1)

            def gather(b, u, tiles=range(TPB)):
                if tiles[0] == 0:
                    g.tensor_copy(idx_b[u][:], idx[:, b, :]).then_inc(idxb_r, 1)
                    pool.wait_ge(idxb_r, b + 1)
                    settle(pool)
                for j in tiles:
                    g.indirect_dma_start(
                        out=basin[u][:, j, :], out_offset=None, in_=coords,
                        in_offset=bass.IndirectOffsetOnAxis(ap=idx_b[u][:, j:j + 1], axis=0),
                    ).then_inc(gathered[u], 16)

            def power(b):
                pool.wait_ge(pow_in_r, b + 1)
                g.tensor_tensor(scales[:, b, :], pow_in[:], neg_half[:], ALU.pow).then_inc(scale_r, 1)

            pool.wait_ge(idx_r, 1)
            gather(0, 0)
            gather(1, 1)
            power(0)

            pool.wait_ge(prep_v, 1)
            for u in range(2):
                g.tensor_copy(ev[u].rearrange("p (c v) -> p c v", v=VC)[:, :, HD], mask_den[:]).then_inc(pool_const, 1)

            def sum_values(b, u):
                pool.wait_ge(kv_r, b * TPB + TPB)
                g.tensor_tensor(vsum2[:], val[u][:, 0:2, :], val[u][:, 2:4, :], ALU.add).then_inc(vs_half, 1)
                pool.wait_ge(vs_half, b + 1)
                g.tensor_tensor(vsum[:], vsum2[:, 0, :], vsum2[:, 1, :], ALU.add).then_inc(vs_r, 1)

            def weigh_values(b, u):
                pool.wait_ge(f_r, b + 1)
                g.tensor_tensor(vp[u][:, :, 0:HD], val[u].rearrange("p j (h d) -> p (j h) d", d=HD),
                                bc(vp[u][:, :, HD], 2, HD), ALU.mult).then_inc(vp_r, 1)

            def step_a(b, h, u):
                if has(b, -1):
                    sum_values(b - 1, 1 - u)
                if has(b, 2):
                    pool.wait_ge(quad_r, b + 1)
                    pool.wait_ge(kept, b + 1)
                    gather(b + 2, u, (0, 1))
                if has(b, -1):
                    weigh_values(b - 1, 1 - u)
                if has(b, 2):
                    gather(b + 2, u, (2, 3))
                if has(b, 1):
                    power(b + 1)

            steps_of(pool, NB, step_a, ahead=2)

            def scaled(b, u):
                if not isinstance(b, int) or b >= 2:
                    pool.wait_ge(xsplit_r, b - 1)
                g.tensor_tensor(xs[u][:], basin_all[:, b, :, :], bc(scales[:, b, TPB:2 * TPB], 2, DB), ALU.mult
                                ).then_inc(xs_r, 1)

            def send(b, u):
                pool.wait_ge(std_r, b * 2 + 2)
                pool.wait_ge(slot_r, b + 1)
                settle(pool)
                for j in range(TPB):
                    g.indirect_dma_start(
                        out=slots, out_offset=bass.IndirectOffsetOnAxis(ap=slot[u][:, j:j + 1], axis=0),
                        in_=row[u][:, j, :], in_offset=None, bounds_check=NE * SEG - 1, oob_is_err=False,
                    ).then_inc(sent[u], 16)

            def spread(b, u):
                for i0, i1 in ((0, 2), (2, 3), (3, 5)):
                    w = W0[i0]
                    ins = g.tensor_tensor(
                        ev[u][:, i0 * HW * VC:i1 * HW * VC].rearrange("p (i h v) -> p i h v", h=HW, v=VC)[:, :, :, 0:HD],
                        bc(v_sums[:, b, w * HD:(w + HW) * HD].rearrange("p (h d) -> p h d", d=HD), 1, i1 - i0),
                        bc(mask[:, i0 * HW:i1 * HW].rearrange("p (i h) -> p i h", h=HW), 3, HD), ALU.mult)
                ins.then_inc(spread_r, 1)

            def add_constant(b, u):
                pool.wait_ge(spread_r, b + 1)
                pool.wait_ge(kvs_r, b + 1)
                g.tensor_tensor(kv[u][:], kv[u][:], ev[u], ALU.add).then_inc(kvb_r, 1)

            pool.wait_ge(kept, NB)
            pool.wait_ge(scale_r, NB)
            scaled(0, 0)
            sum_values(NB - 1, (NB - 1) % 2)
            weigh_values(NB - 1, (NB - 1) % 2)
            scaled(1, 1)
            pool.wait_ge(ev_r, NB)
            spread(0, 0)
            add_constant(0, 0)

            def row_tail(b, u):
                pool.wait_ge(ve_r, b + 1)
                g.tensor_tensor(row[u][:, :, R_STD], ve[:], neg_half[:, 0:TPB], ALU.pow).then_inc(std_r, 1)
                g.tensor_copy(row[u][:, :, R_ROW], rows_of[:, b, :]).then_inc(std_r, 1)

            def step_b(b, h, u):
                for n, (lo, hi) in enumerate(((0, 2), (2, 4), (4, 5))):
                    pool.wait_ge(fe_r, b * CH + hi)
                    settle(pool)
                    g.tensor_scalar(eq[:, lo:hi, :], eq[:, lo:hi, :], EPS_FEAT, 1.0, ALU.add, ALU.mult).then_inc(eps_r, 1)
                    if n == 0 and has(b, -1):
                        row_tail(b - 1, 1 - u)
                    if n == 1 and has(b, 2):
                        scaled(b + 2, u)
                if has(b, 1):
                    if has(b, -1):
                        pool.wait_ge(kvb_r, b)
                    spread(b + 1, 1 - u)
                if has(b, -1):
                    send(b - 1, 1 - u)
                if has(b, 1):
                    add_constant(b + 1, 1 - u)
                if has(b, -1):
                    pool.wait_ge(sent[1 - u], (h + u) * (16 * TPB))
                    pool.sem_inc(sent_r, 1)

            steps_of(pool, NB, step_b, ahead=2)
            row_tail(NB - 1, (NB - 1) % 2)
            send(NB - 1, (NB - 1) % 2)

            def step_c(t, h, u):
                if has(t, -1, NT):
                    pool.wait_ge(fin[(u - 1) % ROT], (h + (1 if u else 0)) * 16)
                    pool.sem_inc(fin_r, 1)
                pool.wait_ge(oidx_r, t + 1)
                pool.wait_ge(o_r, t + 1)
                settle(pool)
                g.indirect_dma_start(
                    out=out_rows, out_offset=bass.IndirectOffsetOnAxis(ap=oidx[u][:, 0:1], axis=0),
                    in_=orow[u], in_offset=None, bounds_check=TOK - 1, oob_is_err=False,
                ).then_inc(fin[u], 16)

            steps_of(pool, NT, step_c, cycle=ROT)

        @block.scalar
        def _(act):
            a = nc.scalar
            def basin_t(b, u):
                act.wait_ge(tr_r, b + 1)
                a.activation(bt[u], T, ACT.Copy).then_inc(bt_r, 1)

            def keep_h0(b, j):
                act.wait_ge(ph_r, b * TPB + (j + 1))
                settle(act)
                a.activation(h0[:, b, j, :], psum[:, 5, 0:EXT], ACT.Copy)
                a.activation(quad[:, j].rearrange("p a d -> p (a d)"), psum[:, 5, EXT:EXT + P], ACT.Copy).then_inc(h0_r, 1)

            def keep(b, h, u):
                act.wait_ge(gathered[u], (h + 1) * (16 * TPB))
                settle(act)
                a.activation(basin_all[:, b, :, :], basin[u][:], ACT.Copy).then_inc(kept, 1)

            def keep_sums(b):
                act.wait_ge(vsm_r, b + 1)
                settle(act)
                a.activation(v_sums[:, b, :], T[:, 0:D], ACT.Copy, scale=EPS_FEAT).then_inc(ev_r, 1)

            def factors(b, u):
                act.wait_ge(farg_r, b + 1)
                a.activation(vp[u][:, :, HD], farg[:], ACT.Exp).then_inc(f_r, 1)

            act.wait_ge(prep_pe, 2)
            a.activation(f_hi["h"][:, 0:EXT], psum[:, 0, 0:EXT], ACT.Copy).then_inc(prep_hi, 1)
            a.activation(f_hi["h"][:, EXT:EXT + P], psum[:, 0, EXT:EXT + P], ACT.Copy, scale=1.0 / D).then_inc(prep_hi, 1)
            basin_t(0, 0)
            act.wait_ge(prep_pe, 4)
            a.activation(f_hi["kd"].rearrange("p (a n) -> p a n", a=2), psum[:, 2:4, 0:HALF], ACT.Copy).then_inc(prep_hi, 1)
            keep_h0(0, 0)
            act.wait_ge(prep_pe, 5)
            a.activation(f_hi["qkv"].rearrange("p (a n) -> p a n", a=2), psum[:, 0:2, 0:3 * D // 2], ACT.Copy).then_inc(prep_hi, 1)
            for j in range(1, TPB):
                keep_h0(0, j)
            keep(0, 0, 0)
            act.wait_ge(prep_pe, 7)
            a.activation(f_hi["qd"].rearrange("p (a n) -> p a n", a=2), psum[:, 3:5, 0:HALF], ACT.Copy).then_inc(prep_hi, 1)
            keep(1, 0, 1)

            def step_a(b, h, u):
                if has(b, 1):
                    basin_t(b + 1, 1 - u)
                for j in range(TPB):
                    act.wait_ge(nmax_r, b * TPB + (j + 1))
                    settle(act)
                    q = 2 * (j % 2)
                    sc = scales[:, b, TPB + j:TPB + j + 1]
                    a.activation(ek[u][:, j, :].rearrange("p (a n) -> p a n", a=2), psum[:, q:q + 2, 0:HALF],
                                 ACT.Exp, bias=nmax[u][:, j:j + 1], scale=sc).then_inc(exp_r, 1)
                    if j in (1, 2) and has(b, 1):
                        keep_h0(b + 1, j)
                    act.wait_ge(pkv_r, b * TPB + (j + 1))
                    settle(act)
                    a.activation(ksq[u][:, j, :], psum[:, 4, 0:D], ACT.Square, scale=sc)
                    a.activation(val[u][:, j, :], psum[:, 4, D:2 * D], ACT.Copy, scale=sc).then_inc(kv_r, 1)
                    if j == 0 and has(b, -1):
                        factors(b - 1, 1 - u)
                    if j in (0, 2) and has(b, 1):
                        keep_h0(b + 1, j + j // 2)
                    if j == 1 and has(b, -1):
                        keep_sums(b - 1)
                if has(b, 2):
                    keep(b + 2, h + 1, u)

            steps_of(act, NB, step_a, ahead=2)

            def evacuate(n, dst, src):
                act.wait_ge(tc_r, n + 1)
                a.activation(dst, src, ACT.Copy).then_inc(t_ev, 1)

            def q_squares(b, pair):
                act.wait_ge(qq_r, b * 2 + (pair + 1))
                a.activation(qsq[:, 2 * pair:2 * pair + 2, :], psum[:, 2, 0:2 * D], ACT.Square).then_inc(qsq_r, 1)

            T3, T4 = bank(3), bank(4)

            def scale_state(b, u):
                if has(b, -2):
                    act.wait_ge(ek_r, (b - 1) * 2)
                    settle(act)
                a.activation(kv[u][:], s_all[:, b, :, :].rearrange("p c v -> p (c v)"), ACT.Copy,
                             scale=cb[:, bass.ds(b, 1)]).then_inc(kvs_r, 1)

            evacuate(0, xt[0], T)
            factors(NB - 1, (NB - 1) % 2)
            act.wait_ge(dcb_r, 1)
            a.activation(cb[:], dcb[:], ACT.Exp).then_inc(cb_r, 1)
            q_squares(0, 0)
            q_squares(0, 1)
            keep_sums(NB - 1)
            evacuate(1, sdt[0:2 * H, :], T3[0:2 * H, :])
            evacuate(2, xt[1], T)
            act.wait_ge(cb_r, 1)
            act.wait_ge(s_free, NB + 1)
            scale_state(0, 0)

            def step_b(b, h, u):
                more = has(b, 1)
                n = first_t(b)
                for i in range(CH):
                    act.wait_ge(fm_r, b * CH + (i + 1))
                    a.activation(eq[:, i, :], bank(3 + (CH * u + i) % 2), ACT.Exp).then_inc(fe_r, 1)
                    if more and i == 2:
                        q_squares(b + 1, 0)
                if more:
                    q_squares(b + 1, 1)
                if has(b, -1):
                    act.wait_ge(dscl_r, b)
                    a.activation(pexp[:], dscl[:], ACT.Exp).then_inc(pexp_r, 1)
                evacuate(n, at[0][0:KC, :], T[0:KC, :])
                if more:
                    evacuate(n + 1, sdt[0:2 * H, :], T3[0:2 * H, :])
                    scale_state(b + 1, 1 - u)
                evacuate(n + 2 if more else n + 1, at[1][0:KC, :], T4[0:KC, :])
                if has(b, 2):
                    evacuate(n + 3, xt[u], T)

            steps_of(act, NB, step_b, ahead=2)
            act.wait_ge(dscl_r, NB)
            a.activation(pexp[:], dscl[:], ACT.Exp).then_inc(pexp_r, 1)

            def x_t(t):
                act.wait_ge(ct_r, t + 1)
                a.activation(xe.rearrange("p k n -> p (k n)"), T[0:KC, 0:2 * P], ACT.Copy).then_inc(xe_r, 1)

            act.wait_ge(fill_r, 1)
            for e in range(NE // 2, NE):
                first = act.value_load(fill[0:1, e:e + 1], min_val=0, max_val=(NE - 1) * SEG + TOK)
                a.dma_start(slots[bass.ds(first, P), :], blank[:, :]).then_inc(filled, 16)

            def fetch(t, u):
                e = act.value_load(tile_expert[0:1, bass.ds(t, 1)], min_val=0, max_val=NE - 1)
                settle(act)
                a.activation(wi_now[u][:, 0, :], wi_all[:, bass.ds(e, 1), 0, :].rearrange("p e f -> p (e f)"),
                             ACT.Copy).then_inc(wi_a, 1)

            act.wait_ge(wi_in, 16)
            act.wait_ge(w_late, 16 * (1 + NE + AFTER_B))
            act.wait_ge(table_r, 1)
            fetch(0, 0)
            fetch(1, 1)
            x_t(0)

            def step_c(t, h, u):
                act.wait_ge(hid_r, t * 2 + 1)
                a.activation(hid[:, 0:4, :].rearrange("p f n -> p (f n)"), bank(3), ACT.Relu).then_inc(relu_r, 1)
                act.wait_ge(hid_r, t * 2 + 2)
                a.activation(hid[:, 4:6, :].rearrange("p f n -> p (f n)"), bank(4, 2 * P), ACT.Relu).then_inc(relu_r, 1)
                if has(t, 1, NT):
                    x_t(t + 1)
                if has(t, 2, NT):
                    fetch(t + 2, (u + 2) % ROT)

            steps_of(act, NT, step_c, ahead=2, cycle=ROT)

        @block.vector
        def _(dve):
            v = nc.vector
            base = [0]
            done = [0]

            def link(ins):
                done[0] += 1
                ins.then_inc(steps, 1)
                dve.wait_ge(steps, base[0] + done[0])

            def mark(ins):
                done[0] += 1
                ins.then_inc(steps, 1)
                return base[0] + done[0]

            dve.wait_ge(ids_in, 16)
            link(v.tensor_copy(idx_f[:], idx_i[:]))
            link(v.tensor_scalar(idx_w[:], idx_f[:], 0.0, float(VOCAB), ALU.is_lt, ALU.mult))
            link(v.tensor_tensor(idx_w[:], idx_w[:], idx_f[:], ALU.add))
            v.tensor_scalar(idx[:], idx_w[:], 0.0, float(VOCAB - 1), ALU.max, ALU.min).then_inc(idx_r, 1)

            dve.wait_ge(w_in, 16 * 8)
            v.tensor_scalar(mask_den[:], mask, EPS_FEAT * SEQ, None, ALU.mult).then_inc(prep_v, 1)
            v.tensor_copy(ind, cst[:, C_IND:C_IND + CH * P])
            for k in range(2):
                v.tensor_scalar(pw[:, k, :].rearrange("p (a d) -> p a d", a=2), bc(proj_in[:, k, :], 1, 2), nw[:, k:k + 1], None,
                                ALU.mult)
                v.tensor_copy(proj_dup[:, k, :].rearrange("p (a d) -> p a d", a=2), bc(proj_in[:, k, :], 1, 2))
            v.tensor_copy(pm_rep[:], bc(pm[:], 1, HW)).then_inc(prep_v, 1)
            dve.wait_ge(prep_pe, 1)
            v.tensor_tensor(gt.rearrange("p k (a d) -> p k a d", a=2).rearrange("p k a d -> p (k a) d"),
                            pw.rearrange("p k (a d) -> p (k a) d", a=2), bc(psum[0:KC, 0, 0:DB], 1, 4), ALU.subtract)
            v.tensor_tensor(rc[:], rw[:], bc(psum[0:KC, 0, DB:DB + NE], 1, 2), ALU.subtract)
            v.scalar_tensor_tensor(out=bd, in0=bc(psum[0:KC, 2, 0:M], 1, HW), scalar=NORM,
                                   in1=bc(cst[0:KC, C_HM:C_HM + HW], 2, M), op0=ALU.mult, op1=ALU.mult)
            v.tensor_copy(wpt, psum[0:KC, 3, 0:2 * (D + 1)].rearrange("p (k n) -> p k n", k=2)).then_inc(prep_v, 1)
            def split_into(dst, src, signal):
                link(v.tensor_copy(dst[:, :, 0:DB].bitcast(F32R), src))
                v.tensor_tensor(dst[:, :, DB:2 * DB], src, dst[:, :, 0:DB], ALU.subtract).then_inc(signal, 1)

            def split_basin(b, h, u):
                dve.wait_ge(gathered[u], (h + 1) * (16 * TPB))
                if not isinstance(b, int) or b >= 2:
                    dve.wait_ge(tr_r, b - 1)
                split_into(split[u], basin[u][:], split_r)

            def stats(b, u):
                dve.wait_ge(h0_r, b * TPB + TPB)
                v.tensor_tensor(quad, quad, bc(basin[u][:], 2, 2), ALU.mult).then_inc(quad_r, 1)
                dve.wait_ge(quad_r, b + 1)
                link(v.tensor_reduce(qs[:].rearrange("p j a -> p (j a)"), quad.rearrange("p j a d -> p (j a) d"),
                                     AX.X, ALU.add))
                link(v.tensor_scalar(rms2[:], qs[:, :, 0], EPS_RMS, None, ALU.add))
                v.tensor_copy(pow_in[:, 0:TPB], rms2[:])
                v.scalar_tensor_tensor(out=pow_in[:, TPB:2 * TPB], in0=rms2[:], scalar=EPS_LN, in1=qs[:, :, 1],
                                       op0=ALU.mult, op1=ALU.add).then_inc(pow_in_r, 1)

            split_basin(0, 0, 0)
            ft_n = ft.rearrange("p c n -> p (c n)")
            dve.wait_ge(prep_pe, 3)
            v.tensor_copy(ft_n[:, 2 * P:4 * P], psum[0:KC, 1, 0:2 * P]).then_inc(prep_v, 1)
            dve.wait_ge(prep_hi, 2)
            v.tensor_tensor(f_lo["h"][:, 0:EXT], psum[:, 0, 0:EXT], f_hi["h"][:, 0:EXT].bitcast(F32), ALU.subtract)
            v.scalar_tensor_tensor(out=f_lo["h"][:, EXT:EXT + P], in0=psum[:, 0, EXT:EXT + P], scalar=1.0 / D,
                                   in1=f_hi["h"][:, EXT:EXT + P].bitcast(F32), op0=ALU.mult, op1=ALU.subtract
                                   ).then_inc(prep_v, 1)
            for n, (name, where) in enumerate((("kd", psum[:, 2:4, 0:HALF]), ("qkv", psum[:, 0:2, 0:3 * D // 2]))):
                dve.wait_ge(prep_hi, 3 + n)
                v.tensor_tensor(f_lo[name].rearrange("p (a n) -> p a n", a=2), where,
                                f_hi[name].bitcast(F32).rearrange("p (a n) -> p a n", a=2), ALU.subtract).then_inc(prep_v, 1)
            dve.wait_ge(prep_pe, 6)
            v.tensor_copy(wp[0:KC, 0, D:EXT], psum[0:KC, 7, 0:NE])
            v.tensor_copy(wp[0:KC + 1, 1, D:EXT], psum[0:KC + 1, 7, NE:2 * NE])
            v.tensor_copy(ft_n[:, 0:2 * P], psum[0:KC, 4, 0:2 * P]).then_inc(prep_v, 1)
            stats(0, 0)
            dve.wait_ge(prep_hi, 5)
            v.tensor_tensor(f_lo["qd"].rearrange("p (a n) -> p a n", a=2), psum[:, 3:5, 0:HALF],
                            f_hi["qd"].bitcast(F32).rearrange("p (a n) -> p a n", a=2), ALU.subtract).then_inc(prep_v, 1)
            before = [None]

            def begin(b, start, first, each):
                if isinstance(b, int) and b == 0:
                    base[0] = start
                elif isinstance(b, int) and before[0] == b - 1:
                    base[0] += done[0]
                else:
                    base[0] = (b - 1) * each + (start + first)
                done[0] = 0
                before[0] = b if isinstance(b, int) else None

            def end(b, first, each):
                if isinstance(b, int) and b == 0:
                    assert done[0] == first, done
                elif not isinstance(b, int):
                    assert done[0] == each, done

            def keep_s(b):
                dve.wait_ge(s_r, b + 1)
                v.tensor_tensor(s_all[:, b, :, :], PS[:, 0:CH * HW * VC].rearrange("p (c v) -> p c v", v=VC),
                                bc(mask, 2, VC), ALU.mult).then_inc(s_free, 1)

            def batch_max(b):
                dve.wait_ge(nt_r, b + 1)
                v.tensor_reduce(gmin[:], MX[0:1, 0:P], AX.X, ALU.min).then_inc(gmin_r, 1)

            def squares(b, u):
                dve.wait_ge(kv_r, b * TPB + TPB)
                link(v.tensor_reduce(kq[:], ksq[u].rearrange("p j (h d) -> p (j h) d", d=HD), AX.X, ALU.add))

            def factor_arg(b):
                v.scalar_tensor_tensor(out=farg[:].rearrange("p (j h) -> p j h", h=H), in0=kq[:].rearrange("p (j h) -> p j h", h=H),
                                       scalar=-0.5 * NORM * NORM, in1=bc(dmax[:], 2, H), op0=ALU.mult, op1=ALU.add
                                       ).then_inc(farg_r, 1)

            def take_max(b, u):
                dve.wait_ge(nbc_r, b + 1)
                link(v.tensor_copy(nb_now[:], MX[:, 0:1]))
                v.tensor_copy(nbatch[:, bass.ds(b, 1)], nb_now[:]).then_inc(nb_r, 1)
                link(v.tensor_scalar(dmax[:], nmax[u][:], -1.0, nb_now[:], ALU.mult, ALU.add))

            split_basin(1, 0, 1)
            start_a = done[0]
            v.sem_inc(s_free, 1)

            def step_a(b, h, u):
                begin(b, start_a, LINKS_A0, LINKS_A)
                for j in range(TPB):
                    dve.wait_ge(pd_r, b * TPB + (j + 1))
                    q = 2 * (j % 2)
                    link(v.tensor_reduce(rmax[u][:, j:j + 1], psum[:, q:q + 2, 0:HALF], AX.XY, ALU.max))
                    if j == 0:
                        dve.wait_ge(scale_r, b + 1)
                    v.tensor_scalar(nmax[u][:, j:j + 1], rmax[u][:, j:j + 1], scales[:, b, TPB + j:TPB + j + 1], -1.0,
                                    ALU.mult, ALU.mult).then_inc(nmax_r, 1)
                    if j == 0 and has(b, -1):
                        take_max(b - 1, 1 - u)
                    if j == 0 and has(b, -1):
                        squares(b - 1, 1 - u)
                        factor_arg(b - 1)
                    if j == 2 and has(b, -2):
                        keep_s(b - 2)
                dve.wait_ge(nmax_r, b * TPB + TPB)
                v.tensor_reduce(nmin[:], nmax[u][:], AX.X, ALU.min).then_inc(nmin_r, 1)
                if has(b, 1):
                    stats(b + 1, 1 - u)
                if has(b, 2):
                    split_basin(b + 2, h + 1, u)
                batch_max(b)
                end(b, LINKS_A0, LINKS_A)

            LINKS_A0 = TPB + 2 + 1
            LINKS_A = LINKS_A0 + 3
            steps_of(dve, NB, step_a, ahead=2, peel=2)


            def split_x(b, u):
                dve.wait_ge(xs_r, b + 1)
                split_into(split[u], xs[u][:], xsplit_r)

            def q_max(b, j, banks=(0, 1)):
                for q in banks:
                    dve.wait_ge(qd_r, (b * TPB + j) * 2 + (q + 1))
                    v.tensor_reduce(smax[:, j, q * HW:(q + 1) * HW], psum[:, q, 0:HALF].rearrange("p (h m) -> p h m", m=M),
                                    AX.X, ALU.max).then_inc(smax_r, 1)

            def q_shift(b):
                dve.wait_ge(qsq_r, b * 2 + 2)
                dve.wait_ge(smax_r, (b * TPB + TPB) * 2)
                link(v.tensor_reduce(qr[:], qsq.rearrange("p j (h d) -> p (j h) d", d=HD), AX.X, ALU.add))
                link(v.scalar_tensor_tensor(out=sd[:].rearrange("p j h -> p (j h)"), in0=qr[:], scalar=0.5 * NORM * NORM,
                                            in1=smax[:].rearrange("p j h -> p (j h)"), op0=ALU.mult, op1=ALU.add))
                link(v.tensor_copy(sdh[:, :, 0:H].bitcast(F32R), sd[:]))
                v.tensor_tensor(sdh[:, :, H:2 * H], sd[:], sdh[:, :, 0:H], ALU.subtract).then_inc(sd_r, 1)

            dve.wait_ge(pool_const, 9)
            v.tensor_copy(sdt.rearrange("p (j n) -> p j n", n=P), bc(blank[:, 0:P], 1, TPB)).then_inc(prep_v, 1)
            dve.wait_ge(tr_r, NB)
            split_x(0, 0)
            take_max(NB - 1, (NB - 1) % 2)
            squares(NB - 1, (NB - 1) % 2)
            factor_arg(NB - 1)
            keep_s(NB - 2)
            link(v.tensor_reduce(nglob[:], nbatch[:], AX.X, ALU.min))
            v.tensor_scalar(dcb[:], nbatch[:], -1.0, nglob[:], ALU.mult, ALU.add).then_inc(dcb_r, 1)
            for j in range(TPB):
                q_max(0, j)
            q_shift(0)
            split_x(1, 1)
            keep_s(NB - 1)

            def route(b, u, between):
                v.tensor_scalar(ve[:], row[u][:, :, R_STD], EPS_LN, None, ALU.add).then_inc(ve_r, 1)
                lg = row[u][:, :, D:EXT]
                m = mark(v.tensor_reduce(lmax[:], lg, AX.X, ALU.max))
                between()
                dve.wait_ge(steps, m)
                m = mark(v.tensor_tensor(dlog[:], lg, bc(lmax[:], 2, NE), ALU.subtract))
                between()
                dve.wait_ge(steps, m)
                m = mark(v.scalar_tensor_tensor(out=m8[:], in0=dlog[:], scalar=0.0, in1=bc(e8, 1, TPB), op0=ALU.is_ge, op1=ALU.mult))
                between()
                dve.wait_ge(steps, m)
                m = mark(v.tensor_reduce(mm8[:], m8[:], AX.X, ALU.max))
                between()
                dve.wait_ge(steps, m)
                link(v.tensor_tensor(onehot[:], m8[:], bc(mm8[:], 2, NE), ALU.is_equal))
                m = mark(v.tensor_copy(cnt[:, 1, :], onehot[:, 0, :]))
                between()
                dve.wait_ge(steps, m)
                for j in range(1, TPB):
                    ins = v.tensor_tensor(cnt[:, j + 1, :], cnt[:, j, :], onehot[:, j, :], ALU.add)
                    if j < TPB - 1:
                        link(ins)
                ins.then_inc(cnt_r, 1)

            def route_slot(b, u):
                dve.wait_ge(std_r, b * 2 + 1)
                v.tensor_tensor(dscl[:], dlog[:], bc(row[u][:, :, R_STD], 2, NE), ALU.mult).then_inc(dscl_r, 1)
                dve.wait_ge(pref_r, b + 1)
                v.tensor_tensor(pos[:], cnt[:, 0:TPB, :], bc(prefix, 1, TPB), ALU.add).then_inc(pref_used, 1)
                v.tensor_tensor(carry[:], carry[:], cnt[:, TPB, :], ALU.add).then_inc(carry_r, 1)
                v.tensor_scalar(sbase[:], mm8[:], -float(SEG), float(SEG * NE), ALU.mult, ALU.add)
                dve.wait_ge(pref_used, b + 2)
                link(v.tensor_tensor(pos[:], pos[:], onehot[:], ALU.mult))
                link(v.tensor_reduce(rank[:], pos[:], AX.X, ALU.add))
                v.tensor_tensor(slot[u][:], rank[:], sbase[:], ALU.add)

            def gate(b, u):
                dve.wait_ge(pexp_r, b + 1)
                link(v.tensor_reduce(psm[:], pexp[:], AX.X, ALU.add))
                v.reciprocal(row[u][:, :, R_GATE], psm[:]).then_inc(slot_r, 1)

            def normalise(b, pair):
                dve.wait_ge(ek_r, b * 2 + (pair + 1))
                ek4 = psum[:, (5, 2)[pair], 0:2 * H * VC].rearrange("p (g c) -> p g c", c=VC)
                link(v.reciprocal(zr[:, pair, :], ek4[:, :, HD]))
                v.tensor_tensor(attn[pair][:].rearrange("p j (h d) -> p (j h) d", d=HD), ek4[:, :, 0:HD],
                                bc(zr[:, pair, :], 2, HD), ALU.mult).then_inc(norm_r, 1)

            def row_sums(b, u, pair):
                if pair == 0 and has(b, -1):
                    dve.wait_ge(sent_r, b)
                dve.wait_ge(pj_r, b * 2 + (pair + 1))
                for jj in range(2):
                    j = 2 * pair + jj
                    v.scalar_tensor_tensor(out=row[u][:, j, 0:EXT], in0=h0[:, b, j, :], scalar=scales[:, b, j:j + 1],
                                           in1=psum[:, (7, 5)[pair], jj * EXT:(jj + 1) * EXT], op0=ALU.mult, op1=ALU.add
                                           ).then_inc(h1_r, 1)

            def row_stats(b, u, pair):
                for jj in range(2):
                    j = 2 * pair + jj
                    dve.wait_ge(h1_r, b * TPB + (j + 1))
                    ins = v.bn_stats(bn[:, j, :], row[u][:, j, 0:D])
                link(ins)
                settle(dve)
                for jj in range(2):
                    j = 2 * pair + jj
                    ins = v.bn_aggr(row[u][:, j, R_MEAN:R_MEAN + 2], bn[:, j, :])
                if pair:
                    link(ins)

            base[0] += done[0]
            done[0] = 0
            start_b = base[0]

            def step_b(b, h, u):
                begin(b, start_b, LINKS_B0, LINKS_B)
                more, prior = has(b, 1), has(b, -1)
                if prior:
                    row_sums(b - 1, 1 - u, 1)
                if more:
                    q_max(b + 1, 0)
                if prior:
                    row_stats(b - 1, 1 - u, 1)
                if more:
                    q_max(b + 1, 1, (0,))
                turns = [(1, 1), (2, 0), (2, 1), (3, 0), (3, 1)] if more else []

                def between():
                    if turns:
                        j, q = turns.pop(0)
                        q_max(b + 1, j, (q,))

                if prior:
                    route(b - 1, 1 - u, between)
                while turns:
                    between()
                if more:
                    q_shift(b + 1)
                if prior:
                    route_slot(b - 1, 1 - u)
                normalise(b, 0)
                if prior:
                    gate(b - 1, 1 - u)
                normalise(b, 1)
                if has(b, 2):
                    split_x(b + 2, u)
                row_sums(b, u, 0)
                row_stats(b, u, 0)
                end(b, LINKS_B0, LINKS_B)

            LINKS_B0 = 3 + 2 + 1 + 1
            LINKS_B = LINKS_B0 + 2 + 3 + 5 + 3
            v.sem_inc(pref_used, 1)
            steps_of(dve, NB, step_b, ahead=2)
            row_sums(NB - 1, (NB - 1) % 2, 1)
            row_stats(NB - 1, (NB - 1) % 2, 1)
            route(NB - 1, (NB - 1) % 2, lambda: None)
            route_slot(NB - 1, (NB - 1) % 2)
            gate(NB - 1, (NB - 1) % 2)

            dve.wait_ge(tot_r, 1)
            v.tensor_tensor(fill[:], prefix[0:1], cst[0:1, C_PAD:C_PAD + NE], ALU.add).then_inc(fill_r, 1)
            row0 = cst[0:1, :]
            link(v.tensor_tensor(over, bc(prefix[0:1], 2, CNTS), bc(row0[:, C_THR:C_THR + CNTS], 1, NE), ALU.is_gt))
            link(v.tensor_reduce(tiles_of[:], over, AX.X, ALU.add))
            link(v.tensor_tensor(upto, bc(tiles_of[:], 1, NE), row0[:, C_LE:C_T].rearrange("p (e f) -> p e f", e=NE), ALU.mult))
            link(v.tensor_reduce(ends[:], upto, AX.X, ALU.add))
            link(v.tensor_tensor(past, bc(row0[:, C_T:C_N], 2, NE), bc(ends[:], 1, NT), ALU.is_ge))
            v.tensor_tensor(past_n, past, bc(tiles_of[:], 1, NT), ALU.mult)
            link(v.tensor_reduce(t_exp[:], past, AX.X, ALU.add))
            v.tensor_scalar(tile_expert[:], t_exp[:], float(NE - 1), None, ALU.min).then_inc(table_r, 1)
            link(v.tensor_reduce(t_first[:], past_n, AX.X, ALU.add))
            link(v.tensor_tensor(t_within[:], row0[:, C_T:C_N], t_first[:], ALU.subtract))
            link(v.tensor_scalar(t_within[:], t_within[:], float(P), None, ALU.mult))
            v.scalar_tensor_tensor(out=tile_slot[:], in0=t_exp[:], scalar=float(SEG), in1=t_within[:], op0=ALU.mult,
                                   op1=ALU.add).then_inc(table_r, 1)

            def normed(t, h, u):
                dve.wait_ge(x_in[u], h * 16 + 16)
                if not isinstance(t, int) or t > 0:
                    dve.wait_ge(ct_r, t)
                v.tensor_scalar(xn, x_rows[u][:, 0:D], x_rows[u][:, R_MEAN:R_MEAN + 1],
                                x_rows[u][:, R_STD:R_STD + 1], ALU.subtract, ALU.mult).then_inc(xn_r, 1)

            def fetch(t, u):
                e = dve.value_load(tile_expert[0:1, bass.ds(t, 1)], min_val=0, max_val=NE - 1)
                settle(dve)
                v.tensor_copy(wi_now[u][:, 1, :], wi_all[:, bass.ds(e, 1), 1, :].rearrange("p e f -> p (e f)")).then_inc(wi_v, 1)

            dve.wait_ge(wi_in, 16)
            dve.wait_ge(w_late, 16 * (1 + NE + AFTER_B))
            dve.wait_ge(table_r, 1)
            fetch(0, 0)
            fetch(1, 1)
            normed(0, 0, 0)

            def step_c(t, h, u):
                if has(t, 1, NT):
                    normed(t + 1, h + (u + 1) // ROT, (u + 1) % ROT)
                if has(t, -1, NT):
                    dve.wait_ge(fin_r, t)
                v.tensor_copy(oidx[u][:], x_rows[u][:, R_ROW:ROW]).then_inc(oidx_r, 1)
                if has(t, 2, NT):
                    dve.wait_ge(hid_r, t * 2 + 1)
                    fetch(t + 2, (u + 2) % ROT)
                dve.wait_ge(y_r, t + 1)
                v.scalar_tensor_tensor(out=orow[u], in0=PS[:, 0:D], scalar=x_rows[u][:, R_GATE:R_GATE + 1],
                                       in1=x_rows[u][:, 0:D], op0=ALU.mult, op1=ALU.add).then_inc(o_r, 1)

            steps_of(dve, NT, step_c, ahead=2, cycle=ROT)

        @block.tensor
        def _(pe):
            mm = nc.tensor.matmul
            pe.wait_ge(pool_const, 4)
            pe.wait_ge(prep_v, 2)
            for k in range(2):
                mm(psum[0:KC, 0, 0:DB], lhsT=inv_d[0:KC, :], rhs=pw[:, k, 0:DB], start=k == 0, stop=k == 1)
            for k in range(2):
                mm(psum[0:KC, 0, DB:DB + NE], lhsT=inv_d[0:KC, :], rhs=rw[:, k, :], start=k == 0, stop=k == 1)
            mm(psum[0:KC, 2, 0:M], lhsT=pm_rep[:].rearrange("m h d -> m (h d)"), rhs=ident[0:M, 0:M], start=True, stop=True)
            for kn in range(2):
                c0 = kn * (D + 1)
                nc.tensor.transpose(psum[0:KC, 3, c0:c0 + KC], wp[0:KC, 0, kn * KC:(kn + 1) * KC], ident[0:KC, 0:KC])
                ins = nc.tensor.transpose(psum[0:KC, 3, c0 + KC:c0 + D + 1], wp[0:KC + 1, 1, kn * KC:(kn + 1) * KC],
                                          ident[0:KC + 1, 0:KC + 1])
            ins.then_inc(prep_pe, 1)
            pe.wait_ge(prep_v, 3)
            for k in range(2):
                mm(psum[:, 0, k * KC:(k + 1) * KC], lhsT=pw[:, k, :], rhs=ident[0:KC, 0:KC], start=True, stop=True)
            for k in range(2):
                mm(psum[:, 0, D:EXT], lhsT=pw[:, k, :], rhs=rc[:, k, :], start=k == 0, stop=k == 1)
            for k in range(2):
                mm(psum[:, 0, EXT:EXT + DB], lhsT=proj_dup[:, k, :], rhs=proj_in[:, k, :], start=k == 0, stop=k == 1)
            for k in range(2):
                ins = mm(psum[:, 0, EXT + DB:EXT + P], lhsT=gt[:, k, :], rhs=gt[:, k, 0:DB], start=k == 0, stop=k == 1)
            ins.then_inc(prep_pe, 1)

            def by_channel(dst, chunks):
                for n, c in enumerate(chunks):
                    for k in range(2):
                        ins = mm(dst[0:KC, n * P:(n + 1) * P], lhsT=wqkv[:, k, c * KC:(c + 1) * KC], rhs=gt[:, k, :],
                                 start=k == 0, stop=k == 1)
                return ins

            def random_features(chunks, banks):
                for n, where in zip(chunks, banks):
                    ins = mm(psum[:, where, 0:HALF], lhsT=ft[:, n, :], rhs=bd.rearrange("p h m -> p (h m)"), start=True, stop=True)
                return ins

            by_channel(bank(1), (2, 3)).then_inc(prep_pe, 1)

            def two_pass(dst, lhsT, name, c0, c1):
                mm(dst, lhsT=lhsT, rhs=f_hi[name][:, c0:c1], start=True, stop=False)
                return mm(dst, lhsT=lhsT, rhs=f_lo[name][:, c0:c1], start=False, stop=True)

            def basin_t(b, u):
                pe.wait_ge(split_r, b + 1)
                for j in range(TPB):
                    ins = nc.tensor.transpose(T[:, j * P:(j + 1) * P], split[u][:, j, :], ident)
                ins.then_inc(tr_r, 1)

            def embed(b, u, j):
                if j == 0:
                    pe.wait_ge(bt_r, b + 1)
                if not isinstance(b, int) or b + j:
                    pe.wait_ge(h0_r, b * TPB + j)
                two_pass(psum[:, 5, 0:EXT + P], bt[u][:, j * P:(j + 1) * P], "h", 0, EXT + P).then_inc(ph_r, 1)

            def spread_max(b):
                pe.wait_ge(gmin_r, b + 1)
                mm(MX[:, 0:1], lhsT=ones[0:1, :], rhs=gmin[:], start=True, stop=True).then_inc(nbc_r, 1)

            def sum_values(b):
                pe.wait_ge(vs_r, b + 1)
                mm(T[:, 0:D], lhsT=ones[:], rhs=vsum[:], start=True, stop=True).then_inc(vsm_r, 1)

            def state(b, u, tiles):
                if tiles[0] == 0:
                    pe.wait_ge(s_free, b + 1)
                    pe.wait_ge(vp_r, b + 1)
                for j in tiles:
                    for i in range(CH):
                        ins = mm(PS[:, i * HW * VC:(i + 1) * HW * VC], lhsT=ek[u][:, j, F0[i]:F0[i] + P],
                                 rhs=vp[u][:, j * H + W0[i]:j * H + W0[i] + HW, :].rearrange("p h c -> p (h c)"),
                                 start=i == 0 and j == 0, stop=i == CH - 1 and j == TPB - 1, skip_group_check=True)
                if tiles[-1] == TPB - 1:
                    ins.then_inc(s_r, 1)

            basin_t(0, 0)
            pe.wait_ge(prep_v, 4)
            random_features((2, 3), (2, 3)).then_inc(prep_pe, 1)
            pe.wait_ge(prep_v, 5)
            pe.wait_ge(prep_hi, 2)
            embed(0, 0, 0)
            for c in range(2):
                n = 3 * D // 2
                for k in range(2):
                    ins = mm(psum[:, c, 0:n], lhsT=gt[:, k, :], rhs=wqkv[:, k, c * n:(c + 1) * n], start=k == 0, stop=k == 1)
            ins.then_inc(prep_pe, 1)
            embed(0, 0, 1)
            by_channel(bank(4), (0, 1))
            for c, n in ((0, KC), (1, KC + 1)):
                for kn in range(2):
                    ins = mm(psum[0:n, 7, c * NE:(c + 1) * NE], lhsT=wpt[:, kn, c * KC:c * KC + n], rhs=rc[:, kn, :],
                             start=kn == 0, stop=kn == 1)
            ins.then_inc(prep_pe, 1)
            embed(0, 0, 2)
            embed(0, 0, 3)
            pe.wait_ge(prep_v, 8)
            random_features((0, 1), (3, 4)).then_inc(prep_pe, 1)
            pe.wait_ge(prep_v, 9)

            def key_scores(b, u, j):
                if not isinstance(b, int) or b * TPB + j >= 2:
                    pe.wait_ge(exp_r, b * TPB + (j - 1))
                lhsT = bt[u][:, j * P:(j + 1) * P]
                q = 2 * (j % 2)
                two_pass(psum[:, q, 0:HALF], lhsT, "kd", 0, HALF)
                two_pass(psum[:, q + 1, 0:HALF], lhsT, "kd", HALF, NF).then_inc(pd_r, 1)

            key_scores(0, 0, 0)

            def step_a(b, h, u):
                if has(b, -1):
                    spread_max(b - 1)
                for j in range(TPB):
                    if j == 0 and has(b, 1):
                        if has(b, -2):
                            pe.wait_ge(ev_r, b - 1)
                        basin_t(b + 1, 1 - u)
                    if j < 3:
                        key_scores(b, u, j + 1)
                    if j < 2 and has(b, -2):
                        state(b - 2, u, (2 + j,))
                    if j in (1, 2) and has(b, 1):
                        embed(b + 1, 1 - u, j)
                    if j == 0 and has(b, -1):
                        pe.wait_ge(nb_r, b)
                    if not isinstance(b, int) or b + j:
                        pe.wait_ge(kv_r, b * TPB + j)
                    two_pass(psum[:, 4, 0:2 * D], bt[u][:, j * P:(j + 1) * P], "qkv", D, 3 * D).then_inc(pkv_r, 1)
                    if j in (0, 2) and has(b, 1):
                        embed(b + 1, 1 - u, j + j // 2)
                    if j == 1 and has(b, -1):
                        if has(b, -2):
                            pe.wait_ge(ev_r, b - 1)
                        sum_values(b - 1)
                if has(b, 1):
                    key_scores(b + 1, 1 - u, 0)
                if has(b, -1):
                    state(b - 1, 1 - u, (0, 1))
                pe.wait_ge(nmin_r, b + 1)
                pe.wait_ge(kv_r, b * TPB + TPB)
                nc.tensor.transpose(MX[0:1, 0:P], nmin[:], ident).then_inc(nt_r, 1)

            steps_of(pe, NB, step_a, ahead=2, peel=2)

            def x_t(b, u):
                pe.wait_ge(xsplit_r, b + 1)
                for j in range(TPB):
                    ins = nc.tensor.transpose(T[:, j * P:(j + 1) * P], split[u][:, j, :], ident)
                ins.then_inc(tc_r, 1)

            def queries(b, u, j):
                lhsT = xt[u][:, j * P:(j + 1) * P]
                for q in range(2):
                    if not isinstance(b, int) or b + j:
                        pe.wait_ge(smax_r, (b * TPB + j) * 2 + (q - 1))
                    two_pass(psum[:, q, 0:HALF], lhsT, "qd", q * HALF, (q + 1) * HALF).then_inc(qd_r, 1)
                if j % 2 == 0:
                    if not isinstance(b, int) or b + j:
                        pe.wait_ge(qsq_r, b * 2 + j // 2)
                ins = two_pass(psum[:, 2, (j % 2) * D:(j % 2 + 1) * D], lhsT, "qkv", 0, D)
                if j % 2:
                    ins.then_inc(qq_r, 1)

            def shift_t(b):
                pe.wait_ge(sd_r, b + 1)
                for j in range(TPB):
                    ins = nc.tensor.transpose(psum[0:2 * H, 3, j * P:(j + 1) * P], sdh[:, j, :], ident)
                ins.then_inc(tc_r, 1)

            def features(b, u, i):
                if not isinstance(b, int) or b * CH + i >= 2:
                    pe.wait_ge(fe_r, b * CH + (i - 1))
                dst = bank(3 + (CH * u + i) % 2)
                mm(dst, lhsT=f_hi["qd"][:, F0[i]:F0[i] + P], rhs=xt[u], start=True, stop=False)
                mm(dst, lhsT=f_lo["qd"][:, F0[i]:F0[i] + P], rhs=xt[u], start=False, stop=False)
                mm(dst, lhsT=ind[:, i * P:(i + 1) * P], rhs=sdt, start=False, stop=True).then_inc(fm_r, 1)

            def attend(b, u, pair):
                if pair == 0:
                    pe.wait_ge(kvb_r, b + 1)
                    pe.wait_ge(eps_r, b * 3 + 2)
                for jj in range(2):
                    j = 2 * pair + jj
                    if j == 1 and has(b, -1):
                        earlier(b - 1)
                    for i in range(CH):
                        c0 = jj * H * VC + W0[i] * VC
                        if j == 0 and i == CH - 1:
                            pe.wait_ge(eps_r, b * 3 + 3)
                        ins = mm(psum[:, (5, 2)[pair], c0:c0 + HW * VC], lhsT=eq[:, i, j * P:(j + 1) * P],
                                 rhs=kv[u][:, i * HW * VC:(i + 1) * HW * VC], start=jj == 0 and i == 0,
                                 stop=jj == 1 and i == CH - 1, skip_group_check=True)
                ins.then_inc(ek_r, 1)

            def attn_t(b, pair):
                pe.wait_ge(norm_r, b * 2 + (pair + 1))
                dst = bank((6, 4)[pair])
                for jj in range(2):
                    for k in range(2):
                        ins = nc.tensor.transpose(dst[0:KC, (jj * 2 + k) * P:(jj * 2 + k + 1) * P],
                                                  attn[pair][:, jj, k * KC:(k + 1) * KC], ident)
                ins.then_inc(tc_r, 1)

            def project(b, pair, n):
                pe.wait_ge(t_ev, n)
                if pair == 0:
                    pe.wait_ge(pref_used, b + 1)
                for jj in range(2):
                    for k in range(2):
                        rows = KC + k
                        ins = mm(psum[:, (7, 5)[pair], jj * EXT:(jj + 1) * EXT],
                                 lhsT=at[pair][0:rows, (jj * 2 + k) * P:(jj * 2 + k + 1) * P],
                                 rhs=wp[0:rows, k, :], start=jj == 0 and k == 0, stop=jj == 1 and k == 1, skip_group_check=True)
                ins.then_inc(pj_r, 1)

            def earlier(b):
                pe.wait_ge(cnt_r, b + 1)
                mm(prefix, lhsT=tri, rhs=cnt[:, TPB, :], start=True, stop=False)
                mm(prefix, lhsT=ones[:], rhs=carry[:], start=False, stop=True).then_inc(pref_r, 1)

            spread_max(NB - 1)
            pe.wait_ge(ev_r, NB - 1)
            x_t(0, 0)
            state(NB - 2, (NB - 2) % 2, (2, 3))
            pe.wait_ge(exp_r, NB * TPB)
            pe.wait_ge(t_ev, 1)
            for j in range(TPB):
                queries(0, 0, j)
            sum_values(NB - 1)
            state(NB - 1, (NB - 1) % 2, range(TPB))
            shift_t(0)
            pe.wait_ge(ev_r, NB)
            x_t(1, 1)
            pe.wait_ge(s_free, NB + 1)
            pe.wait_ge(prep_v, 10)

            def step_b(b, h, u):
                more = has(b, 1)
                n = first_t(b)
                pe.wait_ge(t_ev, n)
                features(b, u, 0)
                features(b, u, 1)
                for j in range(TPB):
                    if more:
                        queries(b + 1, 1 - u, j)
                    if j < 3:
                        features(b, u, j + 2)
                attend(b, u, 0)
                if more:
                    pe.wait_ge(qsq_r, b * 2 + 4)
                attend(b, u, 1)
                attn_t(b, 0)
                if more:
                    shift_t(b + 1)
                attn_t(b, 1)
                project(b, 0, n + 1)
                if has(b, 2):
                    x_t(b + 2, u)
                project(b, 1, n + 3 if more else n + 2)

            steps_of(pe, NB, step_b, ahead=2)
            earlier(NB - 1)
            pe.wait_ge(carry_r, NB)
            mm(prefix, lhsT=ones[:], rhs=carry[:], start=True, stop=True).then_inc(tot_r, 1)

            def rows_t(t):
                pe.wait_ge(xn_r, t + 1)
                if not isinstance(t, int) or t:
                    pe.wait_ge(xe_r, t)
                for k in range(2):
                    ins = nc.tensor.transpose(T[0:KC, k * P:(k + 1) * P], xn[:, k * KC:(k + 1) * KC], ident)
                ins.then_inc(ct_r, 1)

            pe.wait_ge(w_late, 16 * (1 + NE + AFTER_B))
            pe.wait_ge(table_r, 1)
            rows_t(0)

            def step_c(t, h, u):
                e = pe.value_load(tile_expert[0:1, bass.ds(t, 1)], min_val=0, max_val=NE - 1)
                pe.wait_ge(wi_a, t + 1)
                pe.wait_ge(wi_v, t + 1)
                pe.wait_ge(xe_r, t + 1)
                for f in range(DF // P):
                    for k in range(2):
                        ins = mm(psum[:, 3 + f // 4, f % 4 * P:(f % 4 + 1) * P],
                                 lhsT=wi_now[u][:, k, f * P:(f + 1) * P],
                                 rhs=xe[:, k, :], start=k == 0, stop=k == 1)
                    if f in (3, 5):
                        ins.then_inc(hid_r, 1)
                if has(t, 1, NT):
                    rows_t(t + 1)
                if has(t, -1, NT):
                    pe.wait_ge(o_r, t)
                for f in range(DF // P):
                    if f in (0, 4):
                        pe.wait_ge(relu_r, t * 2 + (1 + f // 4))
                        settle(pe)
                    ins = mm(PS[:, 0:D], lhsT=hid[:, f, :],
                             rhs=wo_all[:, bass.ds(e, 1), f, :].rearrange("p e n -> p (e n)"), start=f == 0, stop=f == DF // P - 1)
                ins.then_inc(y_r, 1)

            steps_of(pe, NT, step_c, cycle=ROT)


_INS = ["x", "L0_tok_basin_coords", "L0_tok_proj_w", "L0_tok_norm_w", "L0_attn_W_qkv", "L0_attn_W_proj",
        "L0_attn_b_proj", "L0_attn_proj_mat", "L0_ffn_router_w", "L0_ffn_wi", "L0_ffn_wo"]


def kernel(**inputs):
    import concourse.bacc as bacc
    from concourse.bass_utils import run_bass_kernel_spmd

    nc = bacc.Bacc("TRN2", target_bir_lowering=False, num_devices=1)
    arrays, args = {}, []
    for name in _INS:
        a = np.ascontiguousarray(inputs[name])
        arrays[f"in_{name}"] = a
        args.append(nc.dram_tensor(f"in_{name}", a.shape, mybir.dt.from_np(a.dtype), kind="ExternalInput").ap())
    c = constants()
    arrays["in_consts"] = c
    args.append(nc.dram_tensor("in_consts", c.shape, F32, kind="ExternalInput").ap())
    out = nc.dram_tensor("out", (NB, SEQ, D), F32, kind="ExternalOutput").ap()
    lm_tower(nc, *args, out)
    r = run_bass_kernel_spmd(nc, [arrays], core_ids=[0])
    return r.results[0]["out"]
```
